# Optimizing a Trainium2 kernel written in Bass

```python
import numpy as np
import jax
import jax.numpy as jnp

def _softmax(x, axis=-1):
    return jax.nn.softmax(x, axis=axis)

def _gelu(x):
    return jax.nn.gelu(x, approximate=True)

def _silu(x):
    return jax.nn.silu(x)

def _sigmoid(x):
    return jax.nn.sigmoid(x)

def _layernorm(x, axis=-1, eps=1e-05):
    m = jnp.mean(x, axis=axis, keepdims=True)
    v = jnp.var(x, axis=axis, keepdims=True)
    return (x - m) / jnp.sqrt(v + eps)

def _scatter_add(tgt, idx, src, axis=0):
    return tgt.at[idx].add(src)

def _segment_sum(src, seg, n):
    return jax.ops.segment_sum(src, seg, n)
kernel_name = 'mk_flamingo_gated_d2_seqx_r8_0950f6'

def setup_inputs(seed: int=0):
    np.random.seed(seed)
    _w = jnp.asarray

    def _rec_inputs():
        import jax
        import jax.numpy as jnp
        _rk = jax.random.key(seed)
        x = -0.000125 + 0.9999 * jax.random.normal(jax.random.fold_in(_rk, 1), (64, 128, 128), jnp.float32)
        _lenS = 128 - jax.random.randint(jax.random.fold_in(_rk, 7), (64,), 0, max(1, 128 // 4) + 1, jnp.int32)
        _lenS2 = 77 - jax.random.randint(jax.random.fold_in(_rk, 8), (64,), 0, max(1, 77 // 4) + 1, jnp.int32)
        _ctx_1024P = jax.random.normal(jax.random.fold_in(_rk, 11), (64, 16, 128), jnp.float32)
        _ctx_1024c = jax.random.dirichlet(jax.random.fold_in(_rk, 511), 0.3 * jnp.ones((16,), jnp.float32), (64, 77))
        _ctx_1024t = jnp.einsum('bsk,bkd->bsd', _ctx_1024c, _ctx_1024P)
        _ctx_1024t = _ctx_1024t * jax.lax.rsqrt(jnp.mean(jnp.square(_ctx_1024t)) + 1e-12) * 0.953939
        ctx_1024 = -1.52775e-05 + 0.999936 * (_ctx_1024t + 0.3 * jax.random.normal(jax.random.fold_in(_rk, 611), (64, 77, 128), jnp.float32))
        _validS = jnp.arange(128)[None, :] < _lenS[:, None]
        _validS2 = jnp.arange(77)[None, :] < _lenS2[:, None]
        _causal = jnp.tril(jnp.ones((128, 128), dtype=bool))
        mask_BxS2_if1 = jnp.where(jnp.ones((64, 77), dtype=bool), 1, 0).astype(jnp.int32)
        _g = jax.random.normal(jax.random.fold_in(_rk, 9001), (2, 2), jnp.float32)
        _g = jnp.sign(_g) * jnp.maximum(jnp.abs(_g), 1.0) + (_g == 0) * 1.0
        g_xattn = _g[0]
        g_ffn = _g[1]
        return (x, ctx_1024, mask_BxS2_if1, g_xattn, g_ffn)
    x, ctx_1024, mask_BxS2_if1, g_xattn, g_ffn = _rec_inputs()

    def _L0_xattn_setup():
        import jax, jax.numpy as jnp
        import numpy as np
        NEG = -10000.0
        key = jax.random.key(seed)
        k1, k2, k3 = jax.random.split(key, 3)
        B, L, D, H = (16, 256, 128, 128)
        x1 = jax.random.normal(k1, (B, L, D), dtype=jnp.float32)
        x2 = jax.random.normal(k2, (B, L, D), dtype=jnp.float32)
        x2_mask = jnp.ones((B, L), dtype=jnp.int64)
        W = jax.random.normal(k3, (H, D), dtype=jnp.float32) * (1.0 / np.sqrt(D))
        diagonal = jnp.ones((H,), dtype=jnp.float32)
        return {'x1': x1, 'x2': x2, 'x2_mask': x2_mask, 'W': W, 'diagonal': diagonal}
    _L0_xattn_all = _L0_xattn_setup()
    _L0_xattn_in = {k: v for k, v in _L0_xattn_all.items() if k in ('W', 'diagonal')}
    del _L0_xattn_all

    def _L0_ffn_setup():
        import jax, jax.numpy as jnp
        import numpy as np
        HIDDEN = 128
        N_EXPERTS = 8
        TOP_K = 2
        INTER = 176
        N_SHARED = 2
        SCALE = 1.0
        key = jax.random.key(seed)
        ks = jax.random.split(key, 9)
        s_h = 1.0 / np.sqrt(HIDDEN)
        s_i = 1.0 / np.sqrt(INTER)
        x = jax.random.normal(ks[0], (2, 256, HIDDEN), dtype=jnp.float32)
        gate_w = jax.random.uniform(ks[1], (N_EXPERTS, HIDDEN), jnp.float32, -s_h, s_h)
        wg = jax.random.uniform(ks[2], (N_EXPERTS, HIDDEN, INTER), jnp.float32, -s_h, s_h)
        wu = jax.random.uniform(ks[3], (N_EXPERTS, HIDDEN, INTER), jnp.float32, -s_h, s_h)
        wd = jax.random.uniform(ks[4], (N_EXPERTS, INTER, HIDDEN), jnp.float32, -s_i, s_i)
        si = INTER * N_SHARED
        s_si = 1.0 / np.sqrt(si)
        swg = jax.random.uniform(ks[5], (HIDDEN, si), jnp.float32, -s_h, s_h)
        swu = jax.random.uniform(ks[6], (HIDDEN, si), jnp.float32, -s_h, s_h)
        swd = jax.random.uniform(ks[7], (si, HIDDEN), jnp.float32, -s_si, s_si)
        return {'x': x, 'gate_w': gate_w, 'wg': wg, 'wu': wu, 'wd': wd, 'swg': swg, 'swu': swu, 'swd': swd}
    _L0_ffn_all = _L0_ffn_setup()
    _L0_ffn_in = {k: v for k, v in _L0_ffn_all.items() if k in ('gate_w', 'wg', 'wu', 'wd', 'swg', 'swu', 'swd')}
    del _L0_ffn_all

    def _L1_xattn_setup():
        import jax, jax.numpy as jnp
        import numpy as np
        B, NT, NM, C, H, FF = (8, 128, 256, 128, 8, 512)

        def _ln(x, g, b):
            m = x.mean(-1, keepdims=True)
            v = jnp.mean((x - m) ** 2, axis=-1, keepdims=True)
            return (x - m) / jnp.sqrt(v + 1e-05) * g + b
        key = jax.random.key(seed)
        ks = jax.random.split(key, 8)
        w = lambda k, shape, s=0.02: jax.random.normal(k, shape, dtype=jnp.float32) * s
        return {'tgt': jax.random.normal(ks[0], (B, NT, C), dtype=jnp.float32), 'memory': jax.random.normal(ks[1], (B, NM, C), dtype=jnp.float32), 'qkv_w': w(ks[2], (3 * C, C)), 'qkv_b': jnp.zeros((3 * C,), jnp.float32), 'sa_out_w': w(ks[3], (C, C)), 'sa_out_b': jnp.zeros((C,), jnp.float32), 'in_proj_w': w(ks[4], (3 * C, C)), 'in_proj_b': jnp.zeros((3 * C,), jnp.float32), 'mha_out_w': w(ks[5], (C, C)), 'mha_out_b': jnp.zeros((C,), jnp.float32), 'lin1_w': w(ks[6], (FF, C)), 'lin1_b': jnp.zeros((FF,), jnp.float32), 'lin2_w': w(ks[7], (C, FF)), 'lin2_b': jnp.zeros((C,), jnp.float32), 'ln1_g': jnp.ones((C,), jnp.float32), 'ln1_b': jnp.zeros((C,), jnp.float32), 'ln2_g': jnp.ones((C,), jnp.float32), 'ln2_b': jnp.zeros((C,), jnp.float32), 'ln3_g': jnp.ones((C,), jnp.float32), 'ln3_b': jnp.zeros((C,), jnp.float32)}
    _L1_xattn_all = _L1_xattn_setup()
    _L1_xattn_in = {k: v for k, v in _L1_xattn_all.items() if k in ('qkv_w', 'qkv_b', 'sa_out_w', 'sa_out_b', 'in_proj_w', 'in_proj_b', 'mha_out_w', 'mha_out_b', 'lin1_w', 'lin1_b', 'lin2_w', 'lin2_b', 'ln1_g', 'ln1_b', 'ln2_g', 'ln2_b', 'ln3_g', 'ln3_b')}
    del _L1_xattn_all

    def _L1_ffn_setup():
        import jax, jax.numpy as jnp
        import numpy as np
        B, S, D_MODEL, D_HIDDEN = (4, 256, 128, 512)

        def act_quant(x):
            scale = 127.0 / jnp.clip(jnp.max(jnp.abs(x), axis=-1, keepdims=True), 1e-05)
            return jnp.clip(jnp.round(x * scale), -128, 127) / scale

        def weight_quant(w):
            scale = 1.0 / jnp.clip(jnp.mean(jnp.abs(w)), 1e-05)
            return jnp.clip(jnp.round(w * scale), -1, 1) / scale

        def bit_linear(x, w):
            xq = x + jax.lax.stop_gradient(act_quant(x) - x)
            wq = w + jax.lax.stop_gradient(weight_quant(w) - w)
            return jnp.einsum('bsd,hd->bsh', xq, wq)

        def depthwise_conv1d(x_bcl, w, b):
            y = jax.lax.conv_general_dilated(x_bcl, w, window_strides=(1,), padding=[(1, 1)], dimension_numbers=('NCH', 'OIH', 'NCH'), feature_group_count=x_bcl.shape[1])
            return y + b[None, :, None]
        key = jax.random.key(seed)
        ks = jax.random.split(key, 5)
        lim1 = 1.0 / np.sqrt(D_MODEL)
        lim2 = 1.0 / np.sqrt(D_HIDDEN)
        limc = 1.0 / np.sqrt(3.0)
        return {'x': jax.random.normal(ks[0], (B, S, D_MODEL), dtype=jnp.float32), 'w1': jax.random.uniform(ks[1], (D_HIDDEN, D_MODEL), jnp.float32, -lim1, lim1), 'conv_w': jax.random.uniform(ks[2], (D_HIDDEN, 1, 3), jnp.float32, -limc, limc), 'conv_b': jax.random.uniform(ks[3], (D_HIDDEN,), jnp.float32, -limc, limc), 'w2': jax.random.uniform(ks[4], (D_MODEL, D_HIDDEN), jnp.float32, -lim2, lim2)}
    _L1_ffn_all = _L1_ffn_setup()
    _L1_ffn_in = {k: v for k, v in _L1_ffn_all.items() if k in ('w1', 'conv_w', 'conv_b', 'w2')}
    del _L1_ffn_all
    return {'x': x, 'ctx_1024': ctx_1024, 'mask_BxS2_if1': mask_BxS2_if1, 'g_xattn': g_xattn, 'g_ffn': g_ffn, 'L0_xattn_W': _L0_xattn_in['W'], 'L0_xattn_diagonal': _L0_xattn_in['diagonal'], 'L0_ffn_gate_w': _L0_ffn_in['gate_w'], 'L0_ffn_wg': _L0_ffn_in['wg'], 'L0_ffn_wu': _L0_ffn_in['wu'], 'L0_ffn_wd': _L0_ffn_in['wd'], 'L0_ffn_swg': _L0_ffn_in['swg'], 'L0_ffn_swu': _L0_ffn_in['swu'], 'L0_ffn_swd': _L0_ffn_in['swd'], 'L1_xattn_qkv_w': _L1_xattn_in['qkv_w'], 'L1_xattn_qkv_b': _L1_xattn_in['qkv_b'], 'L1_xattn_sa_out_w': _L1_xattn_in['sa_out_w'], 'L1_xattn_sa_out_b': _L1_xattn_in['sa_out_b'], 'L1_xattn_in_proj_w': _L1_xattn_in['in_proj_w'], 'L1_xattn_in_proj_b': _L1_xattn_in['in_proj_b'], 'L1_xattn_mha_out_w': _L1_xattn_in['mha_out_w'], 'L1_xattn_mha_out_b': _L1_xattn_in['mha_out_b'], 'L1_xattn_lin1_w': _L1_xattn_in['lin1_w'], 'L1_xattn_lin1_b': _L1_xattn_in['lin1_b'], 'L1_xattn_lin2_w': _L1_xattn_in['lin2_w'], 'L1_xattn_lin2_b': _L1_xattn_in['lin2_b'], 'L1_xattn_ln1_g': _L1_xattn_in['ln1_g'], 'L1_xattn_ln1_b': _L1_xattn_in['ln1_b'], 'L1_xattn_ln2_g': _L1_xattn_in['ln2_g'], 'L1_xattn_ln2_b': _L1_xattn_in['ln2_b'], 'L1_xattn_ln3_g': _L1_xattn_in['ln3_g'], 'L1_xattn_ln3_b': _L1_xattn_in['ln3_b'], 'L1_ffn_w1': _L1_ffn_in['w1'], 'L1_ffn_conv_w': _L1_ffn_in['conv_w'], 'L1_ffn_conv_b': _L1_ffn_in['conv_b'], 'L1_ffn_w2': _L1_ffn_in['w2']}

def reference(x, ctx_1024, mask_BxS2_if1, g_xattn, g_ffn, L0_xattn_W, L0_xattn_diagonal, L0_ffn_gate_w, L0_ffn_wg, L0_ffn_wu, L0_ffn_wd, L0_ffn_swg, L0_ffn_swu, L0_ffn_swd, L1_xattn_qkv_w, L1_xattn_qkv_b, L1_xattn_sa_out_w, L1_xattn_sa_out_b, L1_xattn_in_proj_w, L1_xattn_in_proj_b, L1_xattn_mha_out_w, L1_xattn_mha_out_b, L1_xattn_lin1_w, L1_xattn_lin1_b, L1_xattn_lin2_w, L1_xattn_lin2_b, L1_xattn_ln1_g, L1_xattn_ln1_b, L1_xattn_ln2_g, L1_xattn_ln2_b, L1_xattn_ln3_g, L1_xattn_ln3_b, L1_ffn_w1, L1_ffn_conv_w, L1_ffn_conv_b, L1_ffn_w2):
    import jax
    import jax.numpy as jnp

    def _L0_xattn_ref(x1, x2, x2_mask, W, diagonal):
        import jax, jax.numpy as jnp
        import numpy as np
        NEG = -10000.0
        x1_rep = jax.nn.relu(jnp.einsum('bld,hd->blh', x1, W))
        x2_rep = jax.nn.relu(jnp.einsum('bld,hd->blh', x2, W))
        scores = jnp.einsum('bih,bjh->bij', x1_rep * diagonal, x2_rep)
        m = (1.0 - x2_mask.astype(scores.dtype)) * NEG
        alpha = jax.nn.softmax(scores + m[:, None, :], axis=-1)
        return jnp.einsum('bij,bjd->bid', alpha, x2)

    def _L0_ffn_ref(x, gate_w, wg, wu, wd, swg, swu, swd):
        import jax, jax.numpy as jnp
        import numpy as np
        HIDDEN = 128
        N_EXPERTS = 8
        TOP_K = 2
        INTER = 176
        N_SHARED = 2
        SCALE = 1.0
        B, S, H = x.shape
        xf = x.reshape(-1, H)
        T = xf.shape[0]
        logits = xf.astype(jnp.float32) @ gate_w.astype(jnp.float32).T
        scores = jax.nn.softmax(logits, axis=-1)
        topw, topi = jax.lax.top_k(scores, TOP_K)
        denom = topw.sum(axis=-1, keepdims=True) + 1e-20
        topw = topw / denom * SCALE
        wdense = jnp.zeros((T, N_EXPERTS), jnp.float32).at[jnp.arange(T)[:, None], topi].set(topw)
        hg = jnp.einsum('th,ehi->eti', xf, wg)
        hu = jnp.einsum('th,ehi->eti', xf, wu)
        eo = jnp.einsum('eti,eih->eth', jax.nn.silu(hg) * hu, wd)
        y = jnp.einsum('te,eth->th', wdense, eo)
        shared = jax.nn.silu(xf @ swg) * (xf @ swu) @ swd
        return (y + shared).reshape(B, S, H)

    def _L1_xattn_ref(tgt, memory, qkv_w, qkv_b, sa_out_w, sa_out_b, in_proj_w, in_proj_b, mha_out_w, mha_out_b, lin1_w, lin1_b, lin2_w, lin2_b, ln1_g, ln1_b, ln2_g, ln2_b, ln3_g, ln3_b):
        import jax, jax.numpy as jnp
        import numpy as np
        B, NT, NM, C, H, FF = (8, 128, 256, 128, 8, 512)

        def _ln(x, g, b):
            m = x.mean(-1, keepdims=True)
            v = jnp.mean((x - m) ** 2, axis=-1, keepdims=True)
            return (x - m) / jnp.sqrt(v + 1e-05) * g + b
        Bx, N, Cx = tgt.shape
        qkv = tgt @ qkv_w.T + qkv_b
        q, k, v = jnp.split(qkv, 3, axis=-1)
        scores = jnp.einsum('bnc,bmc->bnm', q, k) * jnp.sqrt(jnp.float32(Cx))
        diag = jnp.eye(N, dtype=bool)
        scores = jnp.where(diag[None, :, :], scores, -jnp.inf)
        attn = jax.nn.softmax(scores, axis=-1)
        sa = jnp.einsum('bnm,bmc->bnc', attn, v) @ sa_out_w.T + sa_out_b
        x = _ln(tgt + sa, ln1_g, ln1_b)
        d = Cx // H
        wq, wk, wv = jnp.split(in_proj_w, 3, axis=0)
        bq, bk, bv = jnp.split(in_proj_b, 3, axis=0)
        qh = (x @ wq.T + bq).reshape(Bx, N, H, d).transpose(0, 2, 1, 3)
        kh = (memory @ wk.T + bk).reshape(Bx, -1, H, d).transpose(0, 2, 1, 3)
        vh = (memory @ wv.T + bv).reshape(Bx, -1, H, d).transpose(0, 2, 1, 3)
        a = jax.nn.softmax(jnp.einsum('bhnd,bhmd->bhnm', qh, kh) / jnp.sqrt(jnp.float32(d)), axis=-1)
        ca = jnp.einsum('bhnm,bhmd->bhnd', a, vh).transpose(0, 2, 1, 3).reshape(Bx, N, Cx)
        ca = ca @ mha_out_w.T + mha_out_b
        x = _ln(x + ca, ln2_g, ln2_b)
        ff = jax.nn.relu(x @ lin1_w.T + lin1_b) @ lin2_w.T + lin2_b
        return _ln(x + ff, ln3_g, ln3_b)

    def _L1_ffn_ref(x, w1, conv_w, conv_b, w2):
        import jax, jax.numpy as jnp
        import numpy as np
        B, S, D_MODEL, D_HIDDEN = (4, 256, 128, 512)

        def act_quant(x):
            scale = 127.0 / jnp.clip(jnp.max(jnp.abs(x), axis=-1, keepdims=True), 1e-05)
            return jnp.clip(jnp.round(x * scale), -128, 127) / scale

        def weight_quant(w):
            scale = 1.0 / jnp.clip(jnp.mean(jnp.abs(w)), 1e-05)
            return jnp.clip(jnp.round(w * scale), -1, 1) / scale

        def bit_linear(x, w):
            xq = x + jax.lax.stop_gradient(act_quant(x) - x)
            wq = w + jax.lax.stop_gradient(weight_quant(w) - w)
            return jnp.einsum('bsd,hd->bsh', xq, wq)

        def depthwise_conv1d(x_bcl, w, b):
            y = jax.lax.conv_general_dilated(x_bcl, w, window_strides=(1,), padding=[(1, 1)], dimension_numbers=('NCH', 'OIH', 'NCH'), feature_group_count=x_bcl.shape[1])
            return y + b[None, :, None]
        h = bit_linear(x, w1)
        h = depthwise_conv1d(h.transpose(0, 2, 1), conv_w, conv_b)
        h = h.transpose(0, 2, 1)
        h = jax.nn.silu(h)
        return bit_linear(h, w2)
    x = x + jnp.tanh(g_xattn[0]) * _L0_xattn_ref(_layernorm(x, axis=-1), ctx_1024, mask_BxS2_if1, L0_xattn_W, L0_xattn_diagonal)
    x = x + jnp.tanh(g_ffn[0]) * _L0_ffn_ref(_layernorm(x, axis=-1), L0_ffn_gate_w, L0_ffn_wg, L0_ffn_wu, L0_ffn_wd, L0_ffn_swg, L0_ffn_swu, L0_ffn_swd)
    x = x + jnp.tanh(g_xattn[1]) * _L1_xattn_ref(_layernorm(x, axis=-1), ctx_1024, L1_xattn_qkv_w, L1_xattn_qkv_b, L1_xattn_sa_out_w, L1_xattn_sa_out_b, L1_xattn_in_proj_w, L1_xattn_in_proj_b, L1_xattn_mha_out_w, L1_xattn_mha_out_b, L1_xattn_lin1_w, L1_xattn_lin1_b, L1_xattn_lin2_w, L1_xattn_lin2_b, L1_xattn_ln1_g, L1_xattn_ln1_b, L1_xattn_ln2_g, L1_xattn_ln2_b, L1_xattn_ln3_g, L1_xattn_ln3_b)
    x = x + jnp.tanh(g_ffn[1]) * _L1_ffn_ref(_layernorm(x, axis=-1), L1_ffn_w1, L1_ffn_conv_w, L1_ffn_conv_b, L1_ffn_w2)
    return x

_drawn_inputs = setup_inputs


def setup_inputs(seed=0):
    import zlib

    import numpy as np

    out = dict(_drawn_inputs(seed))
    spreads = {'g_ffn': (-1.0, 0.6),
     'L0_xattn_diagonal': (1.0, 0.2),
     'L1_xattn_qkv_b': (0.0, 0.268),
     'L1_xattn_sa_out_b': (0.0, 0.1),
     'L1_xattn_in_proj_b': (0.0, 0.272),
     'L1_xattn_mha_out_b': (0.0, 0.1),
     'L1_xattn_lin1_b': (0.0, 0.1),
     'L1_xattn_lin2_b': (0.0, 0.1),
     'L1_xattn_ln1_g': (1.0, 0.2),
     'L1_xattn_ln1_b': (0.0, 0.1),
     'L1_xattn_ln2_g': (1.0, 0.2),
     'L1_xattn_ln2_b': (0.0, 0.1),
     'L1_xattn_ln3_g': (1.0, 0.2),
     'L1_xattn_ln3_b': (0.0, 0.1)}
    factors = {}
    for name, (base, spread) in spreads.items():
        noise = np.random.default_rng([zlib.crc32(name.encode()), seed]).standard_normal(out[name].shape)
        drawn = base * np.exp(spread * noise) if base else spread * noise
        out[name] = jnp.asarray(drawn.astype(out[name].dtype))
    for name, factor in factors.items():
        out[name] = (out[name] * factor).astype(out[name].dtype)
    return out
```

```python
import math
from contextlib import ExitStack

import concourse.bass as bass
from concourse import mybir
from concourse.alu_op_type import AluOpType as ALU

ACT = mybir.ActivationFunctionType
AX = mybir.AxisListType
F32 = mybir.dt.float32
F32R = mybir.dt.float32r
BF16 = mybir.dt.bfloat16
I32 = mybir.dt.int32

P = 128
GB = 4
GT = GB * P
LN_EPS = 1e-5
NEG = -10000.0


def later(g, n):
    return not isinstance(g, int) or g >= n


def over_pairs(eng, pairs, prepare, work):
    prepare(0)
    work(0, 1)
    with eng.Fori(1, pairs - 1) as p:
        work(p, p + 1)
    work(pairs - 1, None)


def flamingo_gated(nc, x, ctx_tokens, mask, g_xattn, g_ffn, W, diagonal, gate_w, wg, wu, wd, swg, swu, swd,
                   qkv_w, qkv_b, sa_out_w, sa_out_b, in_proj_w, in_proj_b, mha_out_w, mha_out_b,
                   lin1_w, lin1_b, lin2_w, lin2_b, ln1_g, ln1_b, ln2_g, ln2_b, ln3_g, ln3_b,
                   w1, conv_w, conv_b, w2, sel_const, ramp_const, out):
    B, S, D = x.shape
    M = ctx_tokens.shape[1]
    assert S == P and D == P and B % (2 * GB) == 0
    NG = B // GB
    PAIRS = NG // 2

    top = ExitStack()

    sems_of_phase = []

    def sem(name):
        s = nc.alloc_semaphore(name=name)
        sems_of_phase.append(s)
        return s

    def end_phase():
        nc.clear_and_free_semaphores(list(sems_of_phase))
        nc.all_engine_barrier()
        sems_of_phase.clear()

    def sb(stack, name, shape, dt=F32):
        return stack.enter_context(nc.sbuf_tensor(name, shape, dt))

    def bank(stack, name, dt=F32, width=512):
        return stack.enter_context(nc.psum_tensor(name, [P, width], dt))

    with top:
        X = sb(top, "X", [P, B, D])
        ident = sb(top, "ident", [P, P])
        ident_bf = sb(top, "ident_bf", [P, P], BF16)
        gates = sb(top, "gates", [P, 4])
        graw = sb(top, "graw", [P, 4])
        half_neg = sb(top, "half_neg", [P, GB])
        eps_tile = sb(top, "eps_tile", [P, GB])

        const_filled = sem("const_filled")
        const_ready = sem("const_ready")
        gates_loaded = sem("gates_loaded")
        gates_ready = sem("gates_ready")
        x_loaded = [sem("x_loaded_even"), sem("x_loaded_odd")]
        out_stored = sem("out_stored")
        sems_of_phase.clear()

        def norm_sems(tag):
            return [sem(f"{tag}_{what}") for what in ("stats", "step", "moments", "eps", "rstd", "normed")]

        def norm_tiles(stack, tag):
            return (sb(stack, f"{tag}_stats", [P, 2, GB, 6]), sb(stack, f"{tag}_sums", [P, 2, GB, 2]),
                    sb(stack, f"{tag}_diff", [P, 2, GB]), sb(stack, f"{tag}_diff2", [P, 2, GB]),
                    sb(stack, f"{tag}_mean", [P, 2, GB]), sb(stack, f"{tag}_var", [P, 2, GB]),
                    sb(stack, f"{tag}_vareps", [P, 2, GB]), sb(stack, f"{tag}_rstd", [P, 2, GB]))

        def norm_moments(v, g, slot, src, tiles, sems):
            stt, sums, diff, diff2, mean, var, _, _ = (t[:, slot] for t in tiles)
            stats, step, moments, _, _, _ = sems
            for b in range(GB):
                i = v.bn_stats(stt[:, b, :], src(b))
            i.then_inc(stats, 1)
            v.wait_ge(stats, g + 1)
            v.tensor_tensor(diff, stt[:, :, 1], stt[:, :, 4], ALU.subtract)
            v.tensor_tensor(sums, stt[:, :, 1:3], stt[:, :, 4:6], ALU.add).then_inc(step, 1)
            v.wait_ge(step, 2 * g + 1)
            v.tensor_scalar(mean, sums[:, :, 0], 0.5, None, ALU.mult)
            v.scalar_tensor_tensor(out=diff2, in0=diff, scalar=0.25, in1=diff, op0=ALU.mult, op1=ALU.mult)\
             .then_inc(step, 1)
            v.wait_ge(step, 2 * g + 2)
            v.scalar_tensor_tensor(out=var, in0=sums[:, :, 1], scalar=1.0 / D, in1=diff2,
                                   op0=ALU.mult, op1=ALU.add).then_inc(moments, 1)

        def norm_apply(v, g, slot, src, dst, tiles, sems):
            mean, rstd_t = tiles[4], tiles[7]
            v.wait_ge(sems[4], g + 1)
            for b in range(GB):
                i = v.tensor_scalar(dst(b), src(b), mean[:, slot, b:b + 1], rstd_t[:, slot, b:b + 1],
                                    ALU.subtract, ALU.mult)
            i.then_inc(sems[5], 1)

        def norm_pool(pool, g, slot, tiles, sems):
            var, vareps, rstd_t = tiles[5], tiles[6], tiles[7]
            _, _, moments, eps, rstd, normed = sems
            pool.wait_ge(moments, g + 1)
            if later(g, 2):
                pool.wait_ge(normed, g - 1)
            pool.tensor_tensor(vareps[:, slot, :], var[:, slot, :], eps_tile[:, :], ALU.add).then_inc(eps, 1)
            pool.wait_ge(eps, g + 1)
            pool.tensor_tensor(rstd_t[:, slot, :], vareps[:, slot, :], half_neg[:, :], ALU.pow).then_inc(rstd, 1)

        with ExitStack() as st:
            Wn = sb(st, "Wn", [P, P])
            WT = sb(st, "WT", [P, P])
            diag = sb(st, "diag", [P, 1])
            ctxs = sb(st, "ctxs", [M, 2, GB, D])
            ctxv = sb(st, "ctxv", [M, 2, GB, D])
            mski = sb(st, "mski", [P, 2, GB * M], I32)
            mskf = sb(st, "mskf", [P, 2, GB * M])
            xn = sb(st, "xn", [P, 2, GB, D])
            xT = sb(st, "xT", [P, 2, GT])
            cT = sb(st, "cT", [P, 2, GB * M])
            r1 = sb(st, "r1", [P, 2, GT])
            r2 = sb(st, "r2", [P, 2, GB * M])
            sc = sb(st, "sc", [P, 2, GB, M])
            mx = sb(st, "mx", [P, 2, GB])
            pr = sb(st, "pr", [P, 2, GB, M])
            sm = sb(st, "sm", [P, 2, GB])
            ri = sb(st, "ri", [P, 2, GB])
            rg = sb(st, "rg", [P, 2, GB])
            prT = sb(st, "prT", [M, 2, GT])
            ln = norm_tiles(st, "lnA")

            psX = [bank(st, f"a_psX{s}") for s in range(2)]
            psC = bank(st, "a_psC")
            psR1 = bank(st, "a_psR1")
            psR2 = bank(st, "a_psR2")
            psS = bank(st, "a_psS")
            psP = bank(st, "a_psP")
            psO = bank(st, "a_psO")

            w_loaded = sem("a_w_loaded")
            wT_done = sem("a_wT_done")
            wT_ready = sem("a_wT_ready")
            ctx_loaded = [sem("a_ctx_loaded_even"), sem("a_ctx_loaded_odd")]
            ctxv_loaded = [sem("a_ctxv_loaded_even"), sem("a_ctxv_loaded_odd")]
            mask_loaded = [sem("a_mask_loaded_even"), sem("a_mask_loaded_odd")]
            mask_ready = sem("a_mask_ready")
            lnA = norm_sems("a_ln")
            normed = lnA[-1]
            xT_done = sem("a_xT_done")
            xT_ready = sem("a_xT_ready")
            cT_done = sem("a_cT_done")
            cT_ready = sem("a_cT_ready")
            r1_done = sem("a_r1_done")
            r1_ready = sem("a_r1_ready")
            r2_done = sem("a_r2_done")
            r2_ready = sem("a_r2_ready")
            s_done = sem("a_scores_done")
            s_masked = sem("a_scores_masked")
            max_ready = sem("a_max_ready")
            negmax_ready = sem("a_negmax_ready")
            p_ready = sem("a_probs_ready")
            inv_ready = sem("a_inv_ready")
            rg_ready = sem("a_gated_inv_ready")
            pT_done = sem("a_probsT_done")
            pT_ready = sem("a_probsT_ready")
            o_done = sem("a_out_done")
            x_ready = sem("a_x_ready")

            with nc.Block() as block:
                @block.sync
                def _(sp):
                    sp.dma_start(Wn[:, :], W).then_inc(w_loaded, 16)
                    sp.dma_start(diag[:, :], diagonal.rearrange("(h a) -> h a", a=1)).then_inc(w_loaded, 16)
                    sp.dma_start(graw[:, 0:2], g_xattn.partition_broadcast(P)).then_inc(gates_loaded, 16)
                    sp.dma_start(graw[:, 2:4], g_ffn.partition_broadcast(P)).then_inc(gates_loaded, 16)

                    def load(g, p, slot):
                        if later(g, 2):
                            sp.wait_ge(x_loaded[slot], 16 * p)
                            sp.wait_ge(cT_done, g - 1)
                            sp.wait_ge(mask_ready, g - 1)
                        b0 = g * GB
                        sp.dma_start(X[:, bass.ds(b0, GB), :], x[bass.ds(b0, GB), :, :].rearrange("b s d -> s b d"))\
                          .then_inc(x_loaded[slot], 16)
                        sp.dma_start(ctxs[:, slot, :, :],
                                     ctx_tokens[bass.ds(b0, GB), :, :].rearrange("b m d -> m b d"))\
                          .then_inc(ctx_loaded[slot], 16)
                        sp.dma_start(mski[:, slot, :].rearrange("p (b m) -> p b m", b=GB),
                                     mask[bass.ds(b0, GB), :].partition_broadcast(P)).then_inc(mask_loaded[slot], 16)

                    def prepare(p):
                        for slot in range(2):
                            load(2 * p + slot, p, slot)

                    def work(p, ahead):
                        for slot in range(2):
                            g = 2 * p + slot
                            if later(g, 2):
                                sp.wait_ge(ctxv_loaded[slot], 16 * p)
                                sp.wait_ge(o_done, g - 1)
                            sp.dma_start(ctxv[:, slot, :, :],
                                         ctx_tokens[bass.ds(g * GB, GB), :, :].rearrange("b m d -> m b d"))\
                              .then_inc(ctxv_loaded[slot], 16)
                        if ahead is not None:
                            prepare(ahead)

                    over_pairs(sp, PAIRS, prepare, work)

                @block.gpsimd
                def _(pool):
                    pool.memset(half_neg[:, :], -0.5).then_inc(const_filled, 1)
                    pool.memset(eps_tile[:, :], LN_EPS).then_inc(const_filled, 1)
                    pool.memset(ident[:, :], 0.0).then_inc(const_filled, 1)
                    pool.wait_ge(const_filled, 3)
                    pool.affine_select(out=ident[:, :], in_=ident[:, :], compare_op=ALU.not_equal, fill=1.0,
                                       base=0, pattern=[[-1, P]], channel_multiplier=1).then_inc(const_filled, 1)
                    pool.wait_ge(const_filled, 4)
                    pool.tensor_copy(ident_bf[:, :], ident[:, :]).then_inc(const_ready, 1)

                    def prepare(p):
                        for slot in range(2):
                            g = 2 * p + slot
                            norm_pool(pool, g, slot, ln, lnA)

                    def work(p, ahead):
                        if ahead is not None:
                            prepare(ahead)

                    over_pairs(pool, PAIRS, prepare, work)

                @block.tensor
                def _(pe):
                    pe.wait_ge(const_ready, 1)
                    pe.wait_ge(w_loaded, 32)
                    pe.transpose(psR1[:, 0:P], Wn[:, :], ident[:, :]).then_inc(wT_done, 1)

                    def transposes(g, p, slot):
                        pe.wait_ge(normed, g + 1)
                        if later(g, 2):
                            pe.wait_ge(xT_ready, g - 1)
                        for b in range(GB):
                            i = pe.transpose(psX[slot][:, b * P:(b + 1) * P], xn[:, slot, b, :], ident[:, :])
                        i.then_inc(xT_done, 1)
                        pe.wait_ge(ctx_loaded[slot], 16 * (p + 1))
                        if later(g, 1):
                            pe.wait_ge(cT_ready, g)
                        for b in range(GB):
                            i = pe.transpose(psC[:, b * M:(b + 1) * M], ctxs[:, slot, b, :], ident[0:M, 0:M])
                        i.then_inc(cT_done, 1)

                    def prepare(p):
                        for slot in range(2):
                            transposes(2 * p + slot, p, slot)

                    def work(p, ahead):
                        for slot in range(2):
                            g = 2 * p + slot
                            pe.wait_ge(xT_ready, g + 1)
                            if later(g, 1):
                                pe.wait_ge(r1_ready, g)
                            else:
                                pe.wait_ge(wT_ready, 1)
                            pe.matmul(psR1[:, :], WT[:, :], xT[:, slot, :], start=True, stop=True).then_inc(r1_done, 1)
                            pe.wait_ge(cT_ready, g + 1)
                            if later(g, 1):
                                pe.wait_ge(r2_ready, g)
                            pe.matmul(psR2[:, 0:GB * M], WT[:, :], cT[:, slot, :], start=True, stop=True)\
                              .then_inc(r2_done, 1)
                        for slot in range(2):
                            g = 2 * p + slot
                            pe.wait_ge(r1_ready, g + 1)
                            pe.wait_ge(r2_ready, g + 1)
                            if later(g, 1):
                                pe.wait_ge(s_masked, g)
                            for b in range(GB):
                                i = pe.matmul(psS[:, b * M:(b + 1) * M], r1[:, slot, b * P:(b + 1) * P],
                                              r2[:, slot, b * M:(b + 1) * M], start=True, stop=True)
                            i.then_inc(s_done, 1)
                        if ahead is not None:
                            prepare(ahead)
                        for slot in range(2):
                            g = 2 * p + slot
                            pe.wait_ge(p_ready, GB * (g + 1))
                            if later(g, 1):
                                pe.wait_ge(pT_ready, g)
                            for b in range(GB):
                                i = pe.transpose(psP[0:M, b * P:(b + 1) * P], pr[:, slot, b, :], ident[:, :])
                            i.then_inc(pT_done, 1)
                        for slot in range(2):
                            g = 2 * p + slot
                            pe.wait_ge(pT_ready, g + 1)
                            pe.wait_ge(ctxv_loaded[slot], 16 * (p + 1))
                            if later(g, 1):
                                pe.wait_ge(x_ready, g)
                            for b in range(GB):
                                i = pe.matmul(psO[:, b * P:(b + 1) * P], prT[:, slot, b * P:(b + 1) * P],
                                              ctxv[:, slot, b, :], start=True, stop=True)
                            i.then_inc(o_done, 1)

                    over_pairs(pe, PAIRS, prepare, work)

                @block.scalar
                def _(act):
                    act.wait_ge(gates_loaded, 32)
                    act.activation(gates[:, :], graw[:, :], ACT.Tanh).then_inc(gates_ready, 1)
                    act.wait_ge(wT_done, 1)
                    act.activation(WT[:, :], psR1[:, 0:P], ACT.Copy).then_inc(wT_ready, 1)

                    def prepare(p):
                        for slot in range(2):
                            g = 2 * p + slot
                            act.wait_ge(xT_done, g + 1)
                            if later(g, 2):
                                act.wait_ge(r1_done, g - 1)
                            act.activation(xT[:, slot, :], psX[slot][:, :], ACT.Copy).then_inc(xT_ready, 1)
                            act.wait_ge(cT_done, g + 1)
                            if later(g, 2):
                                act.wait_ge(r2_done, g - 1)
                            act.activation(cT[:, slot, :], psC[:, 0:GB * M], ACT.Copy).then_inc(cT_ready, 1)
                            act.wait_ge(mask_loaded[slot], 16 * (p + 1))
                            if later(g, 2):
                                act.wait_ge(s_masked, g - 1)
                            act.activation(mskf[:, slot, :], mski[:, slot, :], ACT.Copy, scale=-1.0, bias=1.0)\
                               .then_inc(mask_ready, 1)

                    def work(p, ahead):
                        for slot in range(2):
                            g = 2 * p + slot
                            act.wait_ge(r1_done, g + 1)
                            if later(g, 2):
                                act.wait_ge(s_done, g - 1)
                            act.activation(r1[:, slot, :], psR1[:, :], ACT.Relu).then_inc(r1_ready, 1)
                        if ahead is not None:
                            prepare(ahead)
                        for slot in range(2):
                            g = 2 * p + slot
                            act.wait_ge(negmax_ready, g + 1)
                            if later(g, 2):
                                act.wait_ge(pT_done, g - 1)
                                act.wait_ge(inv_ready, g - 1)
                            for b in range(GB):
                                act.activation(pr[:, slot, b, :], sc[:, slot, b, :], ACT.Exp,
                                               bias=mx[:, slot, b:b + 1], accum_out=sm[:, slot, b:b + 1])\
                                   .then_inc(p_ready, 1)
                        for slot in range(2):
                            g = 2 * p + slot
                            act.wait_ge(pT_done, g + 1)
                            if later(g, 2):
                                act.wait_ge(o_done, g - 1)
                            act.activation(prT[:, slot, :], psP[0:M, :], ACT.Copy).then_inc(pT_ready, 1)

                    over_pairs(act, PAIRS, prepare, work)

                @block.vector
                def _(v):
                    def prepare(p):
                        for slot in range(2):
                            g = 2 * p + slot
                            src = lambda b: X[:, bass.ds(g * GB + b, 1), :].rearrange("p a d -> p (a d)")
                            dst = lambda b: xn[:, slot, b, :]
                            v.wait_ge(x_loaded[slot], 16 * (p + 1))
                            norm_moments(v, g, slot, src, ln, lnA)
                        for slot in range(2):
                            g = 2 * p + slot
                            src = lambda b: X[:, bass.ds(g * GB + b, 1), :].rearrange("p a d -> p (a d)")
                            dst = lambda b: xn[:, slot, b, :]
                            if later(g, 2):
                                v.wait_ge(xT_done, g - 1)
                            norm_apply(v, g, slot, src, dst, ln, lnA)

                    def work(p, ahead):
                        for slot in range(2):
                            g = 2 * p + slot
                            v.wait_ge(r2_done, g + 1)
                            if later(g, 2):
                                v.wait_ge(s_done, g - 1)
                            v.tensor_scalar(r2[:, slot, :], psR2[:, 0:GB * M], 0.0, diag[:, 0:1], ALU.max, ALU.mult)\
                             .then_inc(r2_ready, 1)
                        for slot in range(2):
                            g = 2 * p + slot
                            v.wait_ge(s_done, g + 1)
                            v.wait_ge(mask_ready, g + 1)
                            if later(g, 2):
                                v.wait_ge(p_ready, GB * (g - 1))
                            v.scalar_tensor_tensor(out=sc[:, slot, :, :].rearrange("p b m -> p (b m)"),
                                                   in0=mskf[:, slot, :], scalar=NEG, in1=psS[:, 0:GB * M],
                                                   op0=ALU.mult, op1=ALU.add).then_inc(s_masked, 1)
                            v.wait_ge(s_masked, g + 1)
                            v.tensor_reduce(mx[:, slot, :], sc[:, slot, :, :], AX.X, ALU.max, negate=True)\
                             .then_inc(negmax_ready, 1)
                        if ahead is not None:
                            prepare(ahead)
                        for slot in range(2):
                            g = 2 * p + slot
                            v.wait_ge(p_ready, GB * (g + 1))
                            v.reciprocal(ri[:, slot, :], sm[:, slot, :]).then_inc(inv_ready, 1)
                            v.wait_ge(inv_ready, g + 1)
                            if not later(g, 1):
                                v.wait_ge(gates_ready, 1)
                            v.tensor_scalar(rg[:, slot, :], ri[:, slot, :], gates[:, 0:1], None, ALU.mult)\
                             .then_inc(rg_ready, 1)
                        for slot in range(2):
                            g = 2 * p + slot
                            v.wait_ge(o_done, g + 1)
                            v.wait_ge(rg_ready, g + 1)
                            for b in range(GB):
                                xb = X[:, bass.ds(g * GB + b, 1), :].rearrange("p a d -> p (a d)")
                                i = v.scalar_tensor_tensor(out=xb, in0=psO[:, b * P:(b + 1) * P],
                                                           scalar=rg[:, slot, b:b + 1], in1=xb,
                                                           op0=ALU.mult, op1=ALU.add)
                            i.then_inc(x_ready, 1)

                    over_pairs(v, PAIRS, prepare, work)
        end_phase()

        with ExitStack() as st:
            E, _, INTER = wg.shape
            SH = swg.shape[1]
            EH = E * INTER
            HID = EH + SH
            ET = EH // P
            NT = -(-HID // P)
            assert EH == ET * P and NT % 2 == 0
            rows = [min(P, HID - j * P) for j in range(NT)]
            LAG = 3
            PARTS = 3

            wn = sb(st, "wn", [P, 2, HID])
            wh = sb(st, "wh", [P, 2, HID], F32R)
            wl = sb(st, "wl", [P, 2, HID], F32R)
            dn = sb(st, "dn", [P, NT, D])
            dh = sb(st, "dh", [P, NT, D], F32R)
            dl = sb(st, "dl", [P, NT, D], F32R)
            gwn = sb(st, "gwn", [E, D])
            gwh = sb(st, "gwh", [P, P], F32R)
            gwl = sb(st, "gwl", [P, P], F32R)
            gwz = sb(st, "gwz", [P, P])
            seln = sb(st, "seln", [PARTS * E, EH])
            sel = sb(st, "sel", [PARTS * E, EH], BF16)
            ramp = sb(st, "ramp", [P, E])
            ebase = sb(st, "ebase", [P, E])

            xn = sb(st, "b_xn", [P, GB, D])
            xh = sb(st, "b_xh", [P, 2, GT], F32R)
            xl = sb(st, "b_xl", [P, 2, GT], F32R)
            lgT = sb(st, "b_lgT", [P, GT])
            lg = sb(st, "b_lg", [P, GB, E])
            m1 = sb(st, "b_m1", [P, GB])
            dif = sb(st, "b_dif", [P, GB, E])
            f1 = sb(st, "b_f1", [P, GB, E])
            q1 = sb(st, "b_q1", [P, GB])
            k1 = sb(st, "b_k1", [P, GB, E])
            d2 = sb(st, "b_d2", [P, GB, E])
            m2 = sb(st, "b_m2", [P, GB])
            e2 = sb(st, "b_e2", [P, GB, E])
            f2 = sb(st, "b_f2", [P, GB, E])
            q2 = sb(st, "b_q2", [P, GB])
            k2 = sb(st, "b_k2", [P, GB, E])
            kk = sb(st, "b_kk", [P, GB, E])
            ex = sb(st, "b_ex", [P, GB, E])
            em = sb(st, "b_em", [P, GB, E])
            se = sb(st, "b_se", [P, GB])
            sz = sb(st, "b_sz", [P, GB])
            den = sb(st, "b_den", [P, GB])
            rd = sb(st, "b_rd", [P, GB])
            wt = sb(st, "b_wt", [P, GB, E])
            wr = sb(st, "b_wr", [P, GB, E])
            wr2 = sb(st, "b_wr2", [P, GB, E])
            w3 = sb(st, "b_w3", [P, GB, PARTS, E], BF16)
            w3T = sb(st, "b_w3T", [PARTS * E, 2, GT], BF16)
            sg = sb(st, "b_sg", [P, 2, GT])
            mu = sb(st, "b_mu", [P, 2, GT])
            hf = sb(st, "b_hf", [P, 4, GT])
            hh = sb(st, "b_hh", [P, 4, GT], F32R)
            hl = sb(st, "b_hl", [P, 4, GT], F32R)
            ysb = sb(st, "b_ysb", [P, GT])
            ln = norm_tiles(st, "lnB")

            psG = [bank(st, f"b_psG{s}") for s in range(2)]
            psU = [bank(st, f"b_psU{s}") for s in range(2)]
            psW = bank(st, "b_psW")
            psY = bank(st, "b_psY")
            psT = bank(st, "b_psT")
            psL = bank(st, "b_psL")
            psW3 = psL[:, 256:512].bitcast(BF16)

            up_loaded = sem("b_up_loaded")
            down_loaded = sem("b_down_loaded")
            router_loaded = sem("b_router_loaded")
            sel_loaded = sem("b_sel_loaded")
            uph_ready = sem("b_up_upper_ready")
            upl_ready = sem("b_up_lower_ready")
            dnh_ready = sem("b_down_upper_ready")
            dnl_ready = sem("b_down_lower_ready")
            gwT_done = sem("b_gwT_done")
            gwz_ready = sem("b_gwz_ready")
            gwh_ready = sem("b_gwh_ready")
            gwl_ready = sem("b_gwl_ready")
            sel_ready = sem("b_sel_ready")
            ebase_ready = sem("b_ebase_ready")
            lnB = norm_sems("b_ln")
            normed = lnB[-1]
            xT_done = sem("b_xT_done")
            xh_ready = sem("b_xh_ready")
            xl_ready = sem("b_xl_ready")
            lgT_done = sem("b_logitsT_done")
            lgT_ready = sem("b_logitsT_ready")
            lg_done = sem("b_logits_done")
            dif_ready = sem("b_dif_ready")
            ex_ready = sem("b_exp_ready")
            pick = sem("b_pick_step")
            split_step = sem("b_split_step")
            w3_ready = sem("b_w3_ready")
            w3T_done = sem("b_w3T_done")
            w3T_ready = sem("b_w3T_ready")
            g_done = sem("b_gate_done")
            u_done = sem("b_up_done")
            wb_done = sem("b_weight_done")
            sg_ready = sem("b_silu_ready")
            mu_ready = sem("b_mul_ready")
            hf_ready = sem("b_hidden_ready")
            hh_ready = sem("b_hidden_upper_ready")
            hl_ready = sem("b_hidden_lower_ready")
            dn_done = sem("b_down_done")
            y_ready = sem("b_y_ready")
            yb_done = sem("b_y_back_done")
            x_ready = sem("b_x_ready")

            def over_groups(eng, prep, group, tail):
                def prepare(p):
                    prep(0)

                def work(p, ahead):
                    group(2 * p, 0, 2 * p + 1, 1)
                    group(2 * p + 1, 1, None if ahead is None else 2 * ahead, 0)

                over_pairs(eng, PAIRS, prepare, work)
                tail()

            with nc.Block() as block:
                @block.sync
                def _(sp):
                    sp.dma_start(gwn[:, :], gate_w).then_inc(router_loaded, 16)
                    sp.dma_start(ramp[:, :], ramp_const.partition_broadcast(P)).then_inc(router_loaded, 16)
                    sp.dma_start(seln[:, :], sel_const).then_inc(sel_loaded, 16)
                    for k, (we, ws) in enumerate(((wg, swg), (wu, swu))):
                        sp.dma_start(wn[:, k, 0:EH].rearrange("h (e i) -> h e i", e=E),
                                     we.rearrange("e h i -> h e i")).then_inc(up_loaded, 16)
                        sp.dma_start(wn[:, k, EH:HID], ws).then_inc(up_loaded, 16)
                    full = SH // P
                    sp.dma_start(dn[:, 0:ET, :], wd.rearrange("e i d -> (e i) d").rearrange("(j p) d -> p j d", p=P))\
                      .then_inc(down_loaded, 16)
                    sp.dma_start(dn[:, ET:ET + full, :], swd[0:full * P, :].rearrange("(j p) d -> p j d", p=P))\
                      .then_inc(down_loaded, 16)
                    sp.dma_start(dn[0:rows[-1], NT - 1, :], swd[full * P:SH, :]).then_inc(down_loaded, 16)

                @block.tensor
                def _(pe):
                    pe.wait_ge(router_loaded, 32)
                    pe.transpose(psL[:, 0:E], gwn[:, :], ident[0:E, 0:E]).then_inc(gwT_done, 1)

                    def x_transposes(g):
                        pe.wait_ge(normed, g + 1)
                        if later(g, 1):
                            pe.wait_ge(xl_ready, g)
                        if later(g, 3):
                            pe.wait_ge(x_ready, g - 2)
                        for b in range(GB):
                            i = pe.transpose(psT[:, b * P:(b + 1) * P], xn[:, b, :], ident[:, :])
                        i.then_inc(xT_done, 1)

                    def logits(g, slot):
                        if not later(g, 1):
                            pe.wait_ge(gwh_ready, 1)
                            pe.wait_ge(gwl_ready, 1)
                        pe.wait_ge(xh_ready, g + 1)
                        pe.wait_ge(xl_ready, g + 1)
                        if later(g, 1):
                            pe.wait_ge(w3T_ready, g)
                        pe.matmul(psL[:, :], gwh[:, :], xl[:, slot, :], start=True, stop=False)
                        pe.matmul(psL[:, :], gwl[:, :], xh[:, slot, :], start=False, stop=False)
                        pe.matmul(psL[:, :], gwh[:, :], xh[:, slot, :], start=False, stop=True).then_inc(lgT_done, 1)

                    def logits_back(g):
                        pe.wait_ge(lgT_ready, g + 1)
                        for b in range(GB):
                            i = pe.transpose(psL[:, b * P:(b + 1) * P], lgT[:, b * P:(b + 1) * P], ident[:, :])
                        i.then_inc(lg_done, 1)

                    def weight_transposes(g):
                        pe.wait_ge(w3_ready, g + 1)
                        for b in range(GB):
                            i = pe.transpose(psW3[0:PARTS * E, b * P:(b + 1) * P],
                                             w3[:, b, :, :].rearrange("p a e -> p (a e)"), ident_bf[:, :])
                        i.then_inc(w3T_done, 1)

                    def prep(g):
                        x_transposes(g)
                        logits(g, 0)
                        logits_back(g)
                        weight_transposes(g)

                    def down(g, j):
                        n = NT * g + j
                        q = n % 4 if isinstance(n, int) else None
                        q = (NT * (down_slot[0]) + j) % 4
                        m = rows[j]
                        pe.wait_ge(hh_ready, n + 1)
                        pe.wait_ge(hl_ready, n + 1)
                        if j == 0 and later(g, 1):
                            pe.wait_ge(y_ready, g)
                        if j == 0 and not later(g, 1):
                            pe.wait_ge(dnl_ready, 1)
                        pe.matmul(psY[:, :], dh[0:m, j, :], hl[0:m, q, :], start=(j == 0), stop=False)
                        pe.matmul(psY[:, :], dl[0:m, j, :], hh[0:m, q, :], start=False, stop=False)
                        pe.matmul(psY[:, :], dh[0:m, j, :], hh[0:m, q, :], start=False, stop=(j == NT - 1))\
                          .then_inc(dn_done, 1)

                    def y_back(g):
                        pe.wait_ge(y_ready, g + 1)
                        pe.wait_ge(xl_ready, g + 3)
                        for b in range(GB):
                            i = pe.transpose(psT[:, b * P:(b + 1) * P], ysb[:, b * P:(b + 1) * P], ident[:, :])
                        i.then_inc(yb_done, 1)

                    down_slot = [0]

                    def group(g, slot, nxt, nslot):
                        for j in range(NT):
                            n, m = NT * g + j, rows[j]
                            cols = slice(j * P, j * P + m)
                            if j == 0:
                                pe.wait_ge(xh_ready, g + 1)
                                pe.wait_ge(xl_ready, g + 1)
                            if not later(g, 1):
                                pe.wait_ge(uph_ready, j + 1)
                                pe.wait_ge(upl_ready, j + 1)
                            if j >= 2 or later(g, 1):
                                pe.wait_ge(sg_ready, n - 1)
                            for k, ps in enumerate((psG[j % 2], psU[j % 2])):
                                if k == 1 and (j >= 2 or later(g, 1)):
                                    pe.wait_ge(mu_ready, n - 1)
                                pe.matmul(ps[0:m, :], wh[:, k, cols], xl[:, slot, :], start=True, stop=False)
                                pe.matmul(ps[0:m, :], wl[:, k, cols], xh[:, slot, :], start=False, stop=False)
                                pe.matmul(ps[0:m, :], wh[:, k, cols], xh[:, slot, :], start=False, stop=True)\
                                  .then_inc((g_done, u_done)[k], 1)
                            if j < ET:
                                if j == 0:
                                    pe.wait_ge(w3T_ready, g + 1)
                                    if not later(g, 1):
                                        pe.wait_ge(sel_ready, 1)
                                if j >= 1 or later(g, 1):
                                    pe.wait_ge(hf_ready, n if j else NT * g - (NT - ET))
                                pe.matmul(psW[:, :], sel[:, j * P:(j + 1) * P], w3T[:, slot, :],
                                          start=True, stop=True).then_inc(wb_done, 1)
                            if j >= LAG:
                                down_slot[0] = slot
                                down(g, j - LAG)
                            elif later(g, 1):
                                down_slot[0] = 1 - slot
                                down(g - 1, NT - LAG + j)
                            if j == 3 and nxt is not None:
                                x_transposes(nxt)
                            if j == 5 and later(g, 1):
                                if nxt is None:
                                    pe.wait_ge(y_ready, g)
                                    pe.wait_ge(x_ready, g - 1)
                                    for b in range(GB):
                                        i = pe.transpose(psT[:, b * P:(b + 1) * P], ysb[:, b * P:(b + 1) * P],
                                                         ident[:, :])
                                    i.then_inc(yb_done, 1)
                                else:
                                    y_back(g - 1)
                            if nxt is not None:
                                if j == 5:
                                    logits(nxt, nslot)
                                if j == 6:
                                    logits_back(nxt)
                                if j == 12:
                                    weight_transposes(nxt)

                    def tail():
                        down_slot[0] = 1
                        for j in range(NT - LAG, NT):
                            down(NG - 1, j)
                        pe.wait_ge(y_ready, NG)
                        pe.wait_ge(x_ready, NG - 1)
                        for b in range(GB):
                            i = pe.transpose(psT[:, b * P:(b + 1) * P], ysb[:, b * P:(b + 1) * P], ident[:, :])
                        i.then_inc(yb_done, 1)

                    over_groups(pe, prep, group, tail)

                @block.scalar
                def _(act):
                    act.wait_ge(gwz_ready, 2)
                    act.activation(gwh[:, :], gwz[:, :], ACT.Copy).then_inc(gwh_ready, 1)
                    act.wait_ge(up_loaded, 64)
                    for j in range(NT):
                        cols = slice(j * P, j * P + rows[j])
                        act.activation(wh[:, :, cols], wn[:, :, cols], ACT.Copy).then_inc(uph_ready, 1)
                    act.wait_ge(down_loaded, 48)
                    act.activation(dh[:, 0:NT - 1, :], dn[:, 0:NT - 1, :], ACT.Copy)
                    act.activation(dh[0:rows[-1], NT - 1, :], dn[0:rows[-1], NT - 1, :], ACT.Copy).then_inc(dnh_ready, 1)

                    def x_upper(g, slot):
                        act.wait_ge(xT_done, g + 1)
                        if later(g, 2):
                            act.wait_ge(u_done, NT * (g - 1))
                        act.activation(xh[:, slot, :], psT[:, :], ACT.Copy).then_inc(xh_ready, 1)

                    def logits_copy(g):
                        act.wait_ge(lgT_done, g + 1)
                        act.activation(lgT[:, :], psL[:, :], ACT.Copy).then_inc(lgT_ready, 1)

                    def weights_copy(g, slot):
                        act.wait_ge(w3T_done, g + 1)
                        if later(g, 2):
                            act.wait_ge(wb_done, ET * (g - 1))
                        act.activation(w3T[:, slot, :], psW3[0:PARTS * E, :], ACT.Copy).then_inc(w3T_ready, 1)

                    def prep(g):
                        x_upper(g, 0)
                        logits_copy(g)
                        weights_copy(g, 0)

                    def upper(g, j, slot):
                        n, m, q = NT * g + j, rows[j], (NT * slot + j) % 4
                        act.wait_ge(hf_ready, n + 1)
                        if j >= 4 or later(g, 1):
                            act.wait_ge(dn_done, n - 3)
                        act.activation(hh[0:m, q, :], hf[0:m, q, :], ACT.Copy).then_inc(hh_ready, 1)

                    def group(g, slot, nxt, nslot):
                        for j in range(NT):
                            n, m = NT * g + j, rows[j]
                            act.wait_ge(g_done, n + 1)
                            if j >= 2 or later(g, 1):
                                act.wait_ge(mu_ready, n - 1)
                            act.activation(sg[0:m, j % 2, :], psG[j % 2][0:m, :], ACT.Silu).then_inc(sg_ready, 1)
                            if j >= 1:
                                upper(g, j - 1, slot)
                            elif later(g, 1):
                                upper(g - 1, NT - 1, 1 - slot)
                            if j == 3 and later(g, 1):
                                act.wait_ge(dn_done, NT * g)
                                if later(g, 2):
                                    act.wait_ge(yb_done, g - 1)
                                act.activation(ysb[:, :], psY[:, :], ACT.Copy, scale=gates[:, 2:3])\
                                   .then_inc(y_ready, 1)
                            if nxt is not None:
                                if j == 4:
                                    x_upper(nxt, nslot)
                                if j == 6:
                                    logits_copy(nxt)
                                if j == 13:
                                    weights_copy(nxt, nslot)

                    def tail():
                        upper(NG - 1, NT - 1, 1)
                        act.wait_ge(dn_done, NT * NG)
                        act.wait_ge(yb_done, NG - 1)
                        act.activation(ysb[:, :], psY[:, :], ACT.Copy, scale=gates[:, 2:3]).then_inc(y_ready, 1)

                    over_groups(act, prep, group, tail)

                @block.gpsimd
                def _(pool):
                    pool.memset(ebase[:, :], math.e).then_inc(ebase_ready, 1)
                    pool.wait_ge(sel_loaded, 16)
                    pool.tensor_copy(sel[:, :], seln[:, :]).then_inc(sel_ready, 1)

                    def exps(g, b):
                        if b == 0:
                            pool.wait_ge(dif_ready, g + 1)
                            if later(g, 1):
                                pool.wait_ge(w3_ready, g)
                        pool.tensor_tensor(ex[:, b, :], ebase[:, :], dif[:, b, :], ALU.pow).then_inc(ex_ready, 1)

                    def prep(g):
                        pool.wait_ge(ebase_ready, 1)
                        norm_pool(pool, g, 0, ln, lnB)
                        for b in range(GB):
                            exps(g, b)

                    def group(g, slot, nxt, nslot):
                        for j in range(NT):
                            n, m, q = NT * g + j, rows[j], (NT * slot + j) % 4
                            pool.wait_ge(hh_ready, n + 1)
                            if j >= 4 or later(g, 1):
                                pool.wait_ge(dn_done, n - 3)
                            pool.tensor_tensor(hl[0:m, q, :], hf[0:m, q, :], hh[0:m, q, :].bitcast(F32),
                                               ALU.subtract).then_inc(hl_ready, 1)
                            if nxt is not None:
                                if j == 1:
                                    norm_pool(pool, nxt, nslot, ln, lnB)
                                if 7 <= j < 7 + GB:
                                    exps(nxt, j - 7)

                    over_groups(pool, prep, group, lambda: None)

                @block.vector
                def _(v):
                    v.memset(gwz[:, :], 0.0).then_inc(gwz_ready, 1)
                    v.wait_ge(gwz_ready, 1)
                    v.wait_ge(gwT_done, 1)
                    v.tensor_copy(gwz[:, 0:E], psL[:, 0:E]).then_inc(gwz_ready, 1)
                    v.wait_ge(gwh_ready, 1)
                    v.tensor_tensor(gwl[:, :], gwz[:, :], gwh[:, :].bitcast(F32), ALU.subtract).then_inc(gwl_ready, 1)

                    def x_of(g, b):
                        return X[:, bass.ds(g * GB + b, 1), :].rearrange("p a d -> p (a d)")

                    def moments(g, slot):
                        norm_moments(v, g, slot, lambda b: x_of(g, b), ln, lnB)

                    def apply(g, slot):
                        if later(g, 1):
                            v.wait_ge(xT_done, g)
                        norm_apply(v, g, slot, lambda b: x_of(g, b), lambda b: xn[:, b, :], ln, lnB)

                    def x_lower(g, slot):
                        v.wait_ge(xh_ready, g + 1)
                        if later(g, 2):
                            v.wait_ge(u_done, NT * (g - 1))
                        v.tensor_tensor(xl[:, slot, :], psT[:, :], xh[:, slot, :].bitcast(F32), ALU.subtract)\
                         .then_inc(xl_ready, 1)

                    def wide(t):
                        return t[:, :].unsqueeze(2).broadcast_to([P, GB, E])

                    ramp4 = ramp[:, :].unsqueeze(1).broadcast_to([P, GB, E])
                    STEPS = 18

                    def pick_two(g):
                        v.wait_ge(lg_done, g + 1)
                        v.tensor_copy(lg[:, :, :], psL[:, :].rearrange("p (b e) -> p b e", b=GB)[:, :, 0:E])\
                         .then_inc(pick, 1)
                        v.wait_ge(pick, STEPS * g + 1)
                        v.tensor_reduce(m1[:, :], lg[:, :, :], AX.X, ALU.max).then_inc(pick, 1)
                        v.wait_ge(pick, STEPS * g + 2)
                        if later(g, 1):
                            v.wait_ge(ex_ready, GB * g)
                        v.tensor_tensor(dif[:, :, :], lg[:, :, :], wide(m1), ALU.subtract).then_inc(dif_ready, 1)
                        v.wait_ge(dif_ready, g + 1)
                        v.scalar_tensor_tensor(out=f1[:, :, :], in0=dif[:, :, :], scalar=0.0, in1=ramp4,
                                               op0=ALU.is_equal, op1=ALU.mult).then_inc(pick, 1)
                        v.wait_ge(pick, STEPS * g + 3)
                        v.tensor_reduce(q1[:, :], f1[:, :, :], AX.X, ALU.max).then_inc(pick, 1)
                        v.wait_ge(pick, STEPS * g + 4)
                        v.tensor_tensor(k1[:, :, :], f1[:, :, :], wide(q1), ALU.is_equal).then_inc(pick, 1)
                        v.wait_ge(pick, STEPS * g + 5)
                        v.scalar_tensor_tensor(out=d2[:, :, :], in0=k1[:, :, :], scalar=-3e38, in1=dif[:, :, :],
                                               op0=ALU.mult, op1=ALU.add).then_inc(pick, 1)
                        v.wait_ge(pick, STEPS * g + 6)
                        v.tensor_reduce(m2[:, :], d2[:, :, :], AX.X, ALU.max).then_inc(pick, 1)
                        v.wait_ge(pick, STEPS * g + 7)
                        v.tensor_tensor(e2[:, :, :], d2[:, :, :], wide(m2), ALU.is_equal).then_inc(pick, 1)
                        v.wait_ge(pick, STEPS * g + 8)
                        v.tensor_tensor(f2[:, :, :], e2[:, :, :], ramp4, ALU.mult).then_inc(pick, 1)
                        v.wait_ge(pick, STEPS * g + 9)
                        v.tensor_reduce(q2[:, :], f2[:, :, :], AX.X, ALU.max).then_inc(pick, 1)
                        v.wait_ge(pick, STEPS * g + 10)
                        v.tensor_tensor(k2[:, :, :], f2[:, :, :], wide(q2), ALU.is_equal).then_inc(pick, 1)
                        v.wait_ge(pick, STEPS * g + 11)
                        v.tensor_tensor(kk[:, :, :], k1[:, :, :], k2[:, :, :], ALU.add).then_inc(pick, 1)

                    def routing(g):
                        v.wait_ge(ex_ready, GB * (g + 1))
                        v.wait_ge(pick, STEPS * g + 12)
                        v.tensor_tensor(em[:, :, :], ex[:, :, :], kk[:, :, :], ALU.mult)
                        v.tensor_reduce(sz[:, :], ex[:, :, :], AX.X, ALU.add).then_inc(pick, 1)
                        v.wait_ge(pick, STEPS * g + 13)
                        v.tensor_reduce(se[:, :], em[:, :, :], AX.X, ALU.add).then_inc(pick, 1)
                        v.wait_ge(pick, STEPS * g + 14)
                        v.scalar_tensor_tensor(out=den[:, :], in0=sz[:, :], scalar=1e-20, in1=se[:, :],
                                               op0=ALU.mult, op1=ALU.add).then_inc(pick, 1)
                        v.wait_ge(pick, STEPS * g + 15)
                        v.reciprocal(rd[:, :], den[:, :]).then_inc(pick, 1)
                        v.wait_ge(pick, STEPS * g + 16)
                        v.tensor_tensor(wt[:, :, :], em[:, :, :], wide(rd), ALU.mult).then_inc(pick, 1)
                        v.wait_ge(pick, STEPS * g + 17)
                        if later(g, 1):
                            v.wait_ge(w3T_done, g)
                        v.tensor_copy(w3[:, :, 0, :], wt[:, :, :]).then_inc(pick, 1)
                        v.wait_ge(pick, STEPS * g + 18)

                    def routing_parts(g):
                        v.tensor_tensor(wr[:, :, :], wt[:, :, :], w3[:, :, 0, :], ALU.subtract).then_inc(split_step, 1)
                        v.wait_ge(split_step, 2 * g + 1)
                        v.tensor_copy(w3[:, :, 1, :], wr[:, :, :]).then_inc(split_step, 1)
                        v.wait_ge(split_step, 2 * g + 2)
                        v.tensor_tensor(w3[:, :, 2, :], wr[:, :, :], w3[:, :, 1, :], ALU.subtract).then_inc(w3_ready, 1)

                    def prep(g):
                        moments(g, 0)
                        apply(g, 0)
                        x_lower(g, 0)
                        pick_two(g)
                        routing(g)
                        routing_parts(g)
                        v.wait_ge(uph_ready, 1)
                        for j in range(NT):
                            cols = slice(j * P, j * P + rows[j])
                            v.wait_ge(uph_ready, j + 1)
                            v.tensor_tensor(wl[:, :, cols], wn[:, :, cols], wh[:, :, cols].bitcast(F32),
                                            ALU.subtract).then_inc(upl_ready, 1)
                        v.wait_ge(dnh_ready, 1)
                        v.tensor_tensor(dl[:, 0:NT - 1, :], dn[:, 0:NT - 1, :], dh[:, 0:NT - 1, :].bitcast(F32), ALU.subtract)
                        v.tensor_tensor(dl[0:rows[-1], NT - 1, :], dn[0:rows[-1], NT - 1, :],
                                        dh[0:rows[-1], NT - 1, :].bitcast(F32), ALU.subtract).then_inc(dnl_ready, 1)

                    def add_y(g):
                        v.wait_ge(yb_done, g + 1)
                        xg = X[:, bass.ds(g * GB, GB), :].rearrange("p b d -> p (b d)")
                        v.tensor_tensor(xg, psT[:, :], xg, ALU.add).then_inc(x_ready, 1)

                    def group(g, slot, nxt, nslot):
                        for j in range(NT):
                            n, m, q = NT * g + j, rows[j], (NT * slot + j) % 4
                            dst = (mu[0:m, j % 2, :] if j < ET else hf[0:m, q, :])
                            v.wait_ge(u_done, n + 1)
                            v.wait_ge(sg_ready, n + 1)
                            if j >= ET:
                                v.wait_ge(hl_ready, n - 3)
                            i = v.tensor_tensor(dst, psU[j % 2][0:m, :], sg[0:m, j % 2, :], ALU.mult)
                            i.then_inc(mu_ready, 1)
                            if j < ET:
                                v.wait_ge(mu_ready, n + 1)
                                v.wait_ge(wb_done, ET * g + j + 1)
                                if j >= 4 or later(g, 1):
                                    v.wait_ge(hl_ready, n - 3)
                                v.tensor_tensor(hf[:, q, :], psW[:, :], mu[:, j % 2, :], ALU.mult).then_inc(hf_ready, 1)
                            else:
                                v.wait_ge(mu_ready, n + 1)
                                v.sem_inc(hf_ready, 1)
                            if nxt is not None:
                                if j == 0:
                                    moments(nxt, nslot)
                                if j == 2:
                                    apply(nxt, nslot)
                                if j == 4:
                                    x_lower(nxt, nslot)
                                if j == 7:
                                    pick_two(nxt)
                                if j == 11:
                                    routing(nxt)
                                    routing_parts(nxt)
                            if j == 6 and later(g, 1):
                                add_y(g - 1)

                    def tail():
                        add_y(NG - 1)

                    over_groups(v, prep, group, tail)

        end_phase()

        with ExitStack() as st:
            H = 8
            HD = D // H
            HM = H * M
            HB = HM // 2
            FT = lin1_w.shape[0] // P
            VW = H * (P + HD)
            Q_SCALE = HD ** -0.5

            nat = sb(st, "c_nat", [P, 6, D])
            l1n = sb(st, "c_l1n", [P, FT, D])
            l2n = sb(st, "c_l2n", [P, FT * P])
            tr = sb(st, "c_tr", [P, 6, D])
            l1T = sb(st, "c_l1T", [P, FT, P])
            l1g = sb(st, "c_l1g", [P, FT, P])
            l2T = sb(st, "c_l2T", [P, FT, P])
            qg = sb(st, "c_qg", [P, D])
            m1t = sb(st, "c_m1t", [P, D])
            cols = sb(st, "c_cols", [P, 7])
            l2b = sb(st, "c_ln2b", [P, 1])
            l1b = sb(st, "c_l1b", [P, FT])
            rows_bc = sb(st, "c_rows", [P, 9, D])
            bvb = sb(st, "c_bvb", [P, 2, P])
            y1b = sb(st, "c_y1b", [P, D])
            r1b = sb(st, "c_r1b", [P, D])
            r1b0 = sb(st, "c_r1b0", [P, D])
            r2b = sb(st, "c_r2b", [P, D])
            g3 = sb(st, "c_g3", [P, D])
            b3 = sb(st, "c_b3", [P, D])
            bq2 = sb(st, "c_bq2", [P, 1])
            l1b2 = sb(st, "c_l1b2", [P, FT])
            SAO, MHO, L1B, G1, B1, G2, B2, L2B = range(8)

            ctxs = sb(st, "c_ctxs", [M, 2, GB, D])
            xn = sb(st, "c_xn", [P, GB, D])
            xT = sb(st, "c_xT", [P, GT])
            y1 = sb(st, "c_y1", [P, GB, D])
            n1 = sb(st, "c_n1", [P, GB, D])
            n1T = sb(st, "c_n1T", [P, GT])
            r1t = sb(st, "c_r1t", [P, GB, D])
            r1 = sb(st, "c_r1", [P, 2, GB, D])
            cT = sb(st, "c_cT", [P, GB * M])
            qT = sb(st, "c_qT", [P, 2, GT])
            kT = sb(st, "c_kT", [P, GB * M])
            kbd = sb(st, "c_kbd", [P, 2, GB, HM])
            vp = sb(st, "c_vp", [M, 2, GB, VW])
            sc = sb(st, "c_sc", [P, 2, H, M])
            mx = sb(st, "c_mx", [P, 2, H])
            pr = sb(st, "c_pr", [P, 2, H, M])
            sm = sb(st, "c_sm", [P, 2, H])
            iv = sb(st, "c_iv", [P, 2, H])
            pn = sb(st, "c_pn", [P, 2, H, M])
            pT = sb(st, "c_pT", [M, 2, H, P])
            ca = sb(st, "c_ca", [P, 2, GT])
            y2 = sb(st, "c_y2", [P, GB, D])
            n2 = sb(st, "c_n2", [P, GB, D])
            n2T = sb(st, "c_n2T", [P, GT])
            r2t = sb(st, "c_r2t", [P, GB, D])
            r2 = sb(st, "c_r2", [P, GB, D])
            hT = sb(st, "c_hT", [P, FT, GT])
            y3 = sb(st, "c_y3", [P, GB, D])
            n3 = sb(st, "c_n3", [P, GB, D])
            o3 = sb(st, "c_o3", [P, GB, D])
            o3b = sb(st, "c_o3b", [P, GB, D])
            lns = [norm_tiles(st, f"c_ln{i}") for i in range(4)]

            psS = st.enter_context(nc.psum_tensor("c_psS", [P, 2, 512], F32))
            psP = st.enter_context(nc.psum_tensor("c_psP", [P, 2, 512], F32))
            psO = bank(st, "c_psO")
            bA = bank(st, "c_bA")
            bB = bank(st, "c_bB")
            bC = bank(st, "c_bC")

            w_loaded = sem("c_w_loaded")
            zeroed = sem("c_zeroed")
            wT_done = sem("c_wT_done")
            wT_ready = sem("c_wT_ready")
            fold_done = sem("c_fold_done")
            fold_ready = sem("c_fold_ready")
            bvb_ready = sem("c_bvb_ready")
            rowsum_step = sem("c_rowsum_step")
            consts_ready = sem("c_consts_ready")
            ctx_loaded = [sem("c_ctx_loaded_even"), sem("c_ctx_loaded_odd")]
            kbd_loaded = [sem("c_kbd_loaded_even"), sem("c_kbd_loaded_odd")]
            sems = [norm_sems(f"c_ln{i}") for i in range(4)]
            n0_ready, n1_ready, n2_ready, n3_ready = (s[-1] for s in sems)
            t0_done, t0_ready = sem("c_t0_done"), sem("c_t0_ready")
            y1_done, y1_ready = sem("c_y1_done"), sem("c_y1_ready")
            c_done, c_ready = sem("c_ctxT_done"), sem("c_ctxT_ready")
            k_done, k_ready = sem("c_k_done"), sem("c_k_ready")
            v_done, v_ready = sem("c_v_done"), sem("c_v_ready")
            t1_done, t1_ready = sem("c_t1_done"), sem("c_t1_ready")
            q_done, q_ready = sem("c_q_done"), sem("c_q_ready")
            s_done, s_ready = sem("c_scores_done"), sem("c_scores_ready")
            mx_ready = sem("c_max_ready")
            exp_ready = sem("c_exp_ready")
            sum_ready = sem("c_sum_ready")
            inv_ready = sem("c_inv_ready")
            pn_ready = sem("c_probs_ready")
            tp_done, tp_ready = sem("c_probsT_done"), sem("c_probsT_ready")
            pv_done, ca_ready = sem("c_pv_done"), sem("c_ca_ready")
            out_done, y2_ready = sem("c_out_done"), sem("c_y2_ready")
            t2_done, t2_ready = sem("c_t2_done"), sem("c_t2_ready")
            l1_done = sem("c_lin1_done")
            l1a_ready, l1v_ready = sem("c_lin1_scalar_ready"), sem("c_lin1_vector_ready")
            l2_done, y3_ready = sem("c_lin2_done"), sem("c_y3_ready")
            r1t_ready, r1_ready = sem("c_r1_product"), sem("c_r1_ready")
            r2t_ready, r2_ready = sem("c_r2_product"), sem("c_r2_ready")
            o3_ready, o3b_ready = sem("c_o3_product"), sem("c_o3_ready")
            x_ready = sem("c_x_ready")

            def over_groups(eng, prep, group, post):
                def prepare(p):
                    prep(0)

                def work(p, ahead):
                    first = isinstance(p, int) and p == 0
                    group(2 * p, 0, 2 * p + 1, None if first else 2 * p - 1)
                    group(2 * p + 1, 1, None if ahead is None else 2 * ahead, 2 * p)

                over_pairs(eng, PAIRS, prepare, work)
                post(NG - 1)

            def bcast(t):
                return t[:, :].unsqueeze(1).broadcast_to([P, GB, D])

            N_W = 2 + 4 + 2
            N_COL = 8 + FT
            N_ROW = 9
            ALL_LOADED = 16 * (N_W + N_COL + N_ROW)

            with nc.Block() as block:
                @block.sync
                def _(sp):
                    def col(dst, src):
                        sp.dma_start(dst, src.rearrange("(c a) -> c a", a=1)).then_inc(w_loaded, 16)

                    def row(i, src):
                        sp.dma_start(rows_bc[:, i, :], src.partition_broadcast(P)).then_inc(w_loaded, 16)

                    sp.dma_start(nat[:, 0, :], qkv_w[2 * D:3 * D, :]).then_inc(w_loaded, 16)
                    sp.dma_start(nat[:, 1, :], sa_out_w).then_inc(w_loaded, 16)
                    for i in range(3):
                        sp.dma_start(nat[:, 2 + i, :], in_proj_w[i * D:(i + 1) * D, :]).then_inc(w_loaded, 16)
                    sp.dma_start(nat[:, 5, :], mha_out_w).then_inc(w_loaded, 16)
                    sp.dma_start(l1n[:, :, :], lin1_w.rearrange("(f p) c -> p f c", p=P)).then_inc(w_loaded, 16)
                    sp.dma_start(l2n[:, :], lin2_w).then_inc(w_loaded, 16)
                    col(cols[:, 0:1], qkv_b[2 * D:3 * D])
                    for i in range(3):
                        col(cols[:, 1 + i:2 + i], in_proj_b[i * D:(i + 1) * D])
                    col(cols[:, 4:5], ln1_g)
                    col(cols[:, 5:6], ln1_b)
                    col(cols[:, 6:7], ln2_g)
                    col(l2b[:, :], ln2_b)
                    for f in range(FT):
                        col(l1b[:, f:f + 1], lin1_b[f * P:(f + 1) * P])
                    for i, src in enumerate((sa_out_b, mha_out_b, ln3_b, ln1_g, ln1_b, ln2_g, ln2_b, lin2_b, ln3_g)):
                        row(i, src)

                    def load(g, p, slot):
                        if later(g, 2):
                            sp.wait_ge(c_done, g - 1)
                        sp.dma_start(ctxs[:, slot, :, :],
                                     ctx_tokens[bass.ds(g * GB, GB), :, :].rearrange("b m d -> m b d"))\
                          .then_inc(ctx_loaded[slot], 16)

                    def spread(g, p, slot):
                        sp.wait_ge(k_ready, g + 1)
                        if not later(g, 2):
                            sp.wait_ge(zeroed, 2)
                        for h in range(H):
                            sp.dma_start(kbd[h * HD:(h + 1) * HD, slot, :, h * M:(h + 1) * M],
                                         kT[h * HD:(h + 1) * HD, :].rearrange("p (b m) -> p b m", b=GB))\
                              .then_inc(kbd_loaded[slot], 16)

                    def prepare(p):
                        load(0, 0, 0)
                        load(1, 0, 1)
                        spread(0, 0, 0)

                    def work(p, ahead):
                        spread(2 * p + 1, p, 1)
                        if ahead is not None:
                            load(2 * ahead, ahead, 0)
                            load(2 * ahead + 1, ahead, 1)
                            spread(2 * ahead, ahead, 0)

                    over_pairs(sp, PAIRS, prepare, work)

                @block.tensor
                def _(pe):
                    pe.wait_ge(w_loaded, ALL_LOADED)
                    for i in range(6):
                        bk = (bA, bB)[i % 2]
                        if i >= 2:
                            pe.wait_ge(wT_ready, i - 1)
                        pe.transpose(bk[:, 0:P], nat[:, i, :], ident[:, :]).then_inc(wT_done, 1)
                    pe.wait_ge(wT_ready, 5)
                    for f in range(FT):
                        i = pe.transpose(bA[:, f * P:(f + 1) * P], l1n[:, f, :], ident[:, :])
                    i.then_inc(wT_done, 1)
                    pe.wait_ge(wT_ready, 6)
                    for f in range(FT):
                        i = pe.transpose(bB[:, f * P:(f + 1) * P], l2n[:, f * P:(f + 1) * P], ident[:, :])
                    i.then_inc(wT_done, 1)
                    pe.wait_ge(bvb_ready, 1)
                    pe.wait_ge(wT_ready, 7)
                    pe.matmul(bC[:, 0:P], nat[:, 0, :], tr[:, 1, :], start=True, stop=True)
                    pe.matmul(bC[:, P:2 * P], bvb[:, 0, :], tr[:, 1, :], start=True, stop=True)
                    pe.matmul(bC[:, 2 * P:3 * P], bvb[:, 1, :], tr[:, 5, :], start=True, stop=True)
                    i = pe.matmul(bC[:, 3 * P:3 * P + 1], tr[:, 2, :], cols[:, 5:6], start=True, stop=True)
                    for f in range(FT):
                        i = pe.matmul(bC[:, 3 * P + 1 + f:3 * P + 2 + f], l1T[:, f, :], l2b[:, :],
                                      start=True, stop=True)
                    i.then_inc(fold_done, 1)

                    def four(dst, src, idn):
                        for b in range(GB):
                            i = pe.transpose(dst(b), src(b), idn)
                        return i

                    def at(bk, b, w=P):
                        return bk[:, b * w:(b + 1) * w]

                    def t0(g):
                        pe.wait_ge(n0_ready, g + 1)
                        if later(g, 1):
                            pe.wait_ge(q_ready, g)
                        four(lambda b: at(bB, b), lambda b: xn[:, b, :], ident[:, :]).then_inc(t0_done, 1)

                    def y1_and_ctx(g, p, slot):
                        pe.wait_ge(t0_ready, g + 1)
                        if not later(g, 1):
                            pe.wait_ge(consts_ready, 1)
                        for b in range(GB):
                            i = pe.matmul(at(bB, b), xT[:, b * P:(b + 1) * P], m1t[:, :], start=True, stop=True)
                        i.then_inc(y1_done, 1)
                        pe.wait_ge(ctx_loaded[slot], 16 * (p + 1))
                        if later(g, 1):
                            pe.wait_ge(v_ready, g)
                        four(lambda b: at(bC, b, M), lambda b: ctxs[:, slot, b, :], ident[0:M, 0:M])\
                            .then_inc(c_done, 1)

                    def kv(g):
                        pe.wait_ge(c_ready, g + 1)
                        pe.wait_ge(y1_ready, g + 1)
                        pe.matmul(bB[:, 0:GB * M], tr[:, 3, :], cT[:, :], start=True, stop=True).then_inc(k_done, 1)
                        if later(g, 2):
                            pe.wait_ge(l1v_ready, 2 * (g - 1))
                        for b in range(GB):
                            i = pe.matmul(bC[0:M, b * P:(b + 1) * P], cT[:, b * M:(b + 1) * M], tr[:, 4, :],
                                          start=True, stop=True)
                        i.then_inc(v_done, 1)

                    def t1(g):
                        pe.wait_ge(n1_ready, g + 1)
                        pe.wait_ge(k_ready, g + 1)
                        four(lambda b: at(bB, b), lambda b: n1[:, b, :], ident[:, :]).then_inc(t1_done, 1)

                    def q(g):
                        pe.wait_ge(t1_ready, g + 1)
                        pe.matmul(bB[:, :], qg[:, :], n1T[:, :], start=True, stop=True).then_inc(q_done, 1)

                    def scores(g, b, p, slot):
                        if b == 0:
                            pe.wait_ge(q_ready, g + 1)
                            pe.wait_ge(kbd_loaded[slot], 16 * H * (p + 1))
                        if b or later(g, 1):
                            pe.wait_ge(s_ready, GB * g + b)
                        for k in range(2):
                            i = pe.matmul(psS[:, k, 0:HB], qT[:, slot, b * P:(b + 1) * P],
                                          kbd[:, slot, b, k * HB:(k + 1) * HB], start=True, stop=True)
                        i.then_inc(s_done, 1)

                    def probsT(g, b):
                        pe.wait_ge(pn_ready, GB * g + b + 1)
                        for k in range(2):
                            if b or later(g, 1):
                                pe.wait_ge(tp_ready, 2 * (GB * g + b - 1) + k + 1)
                            for h in range(4 * k, 4 * k + 4):
                                i = pe.transpose(psP[0:M, k, (h % 4) * P:(h % 4 + 1) * P], pn[:, b % 2, h, :],
                                                 ident[:, :])
                            i.then_inc(tp_done, 1)

                    def pv(g, b, slot):
                        pe.wait_ge(tp_ready, 2 * (GB * g + b + 1))
                        if b == 0:
                            pe.wait_ge(v_ready, g + 1)
                            if later(g, 1):
                                pe.wait_ge(ca_ready, g)
                        for h in range(H):
                            i = pe.matmul(at(psO, b), vp[:, slot, b, h * P:(h + 1) * P], pT[:, b % 2, h, :],
                                          start=(h == 0), stop=(h == H - 1))
                        i.then_inc(pv_done, 1)

                    def out_proj(g, slot):
                        pe.wait_ge(ca_ready, g + 1)
                        if later(g, 1):
                            pe.wait_ge(y3_ready, g)
                        for b in range(GB):
                            i = pe.matmul(at(bA, b), ca[:, slot, b * P:(b + 1) * P], tr[:, 5, :],
                                          start=True, stop=True)
                        i.then_inc(out_done, 1)

                    def t2(g):
                        pe.wait_ge(n2_ready, g + 1)
                        four(lambda b: at(bA, b), lambda b: n2[:, b, :], ident[:, :]).then_inc(t2_done, 1)

                    def lin1(g, in_c):
                        pe.wait_ge(t2_ready, g + 1)
                        for f in range(FT):
                            if f == 1:
                                pe.wait_ge(c_ready, in_c)
                            if f == 2:
                                pe.wait_ge(l1a_ready, 2 * g + 1)
                            if f == 3:
                                pe.wait_ge(l1v_ready, 2 * g + 1)
                            pe.matmul((bA, bC)[f % 2][:, :], l1g[:, f, :], n2T[:, :], start=True, stop=True)\
                              .then_inc(l1_done, 1)

                    def lin2(g):
                        pe.wait_ge(l1a_ready, 2 * g + 2)
                        pe.wait_ge(l1v_ready, 2 * g + 2)
                        for b in range(GB):
                            for f in range(FT):
                                i = pe.matmul(at(bA, b), hT[:, f, b * P:(b + 1) * P], l2T[:, f, :],
                                              start=(f == 0), stop=(f == FT - 1))
                        i.then_inc(l2_done, 1)

                    def prep(g):
                        t0(g)
                        y1_and_ctx(g, 0, 0)
                        kv(g)
                        t1(g)
                        q(g)

                    def group(g, slot, nxt, prv):
                        p = (g - slot) // 2 if isinstance(g, int) else pair[0]
                        np_ = p if slot == 0 else p + 1
                        scores(g, 0, p, slot)
                        if prv is not None:
                            out_proj(prv, 1 - slot)
                        if nxt is not None:
                            t0(nxt)
                        scores(g, 1, p, slot)
                        probsT(g, 0)
                        if nxt is not None:
                            y1_and_ctx(nxt, np_, 1 - slot)
                        scores(g, 2, p, slot)
                        probsT(g, 1)
                        pv(g, 0, slot)
                        if prv is not None:
                            t2(prv)
                        scores(g, 3, p, slot)
                        probsT(g, 2)
                        pv(g, 1, slot)
                        if prv is not None:
                            lin1(prv, g + 1 if nxt is None else g + 2)
                        if nxt is not None:
                            kv(nxt)
                        probsT(g, 3)
                        pv(g, 2, slot)
                        if nxt is not None:
                            t1(nxt)
                        if prv is not None:
                            lin2(prv)
                        pv(g, 3, slot)
                        if nxt is not None:
                            q(nxt)

                    def post(g):
                        out_proj(g, 1)
                        t2(g)
                        lin1(g, NG)
                        lin2(g)

                    def prepare(p):
                        prep(0)

                    pair = [None]

                    def work(p, ahead):
                        pair[0] = p
                        first = isinstance(p, int) and p == 0
                        group(2 * p, 0, 2 * p + 1, None if first else 2 * p - 1)
                        group(2 * p + 1, 1, None if ahead is None else 2 * ahead, 2 * p)

                    over_pairs(pe, PAIRS, prepare, work)
                    post(NG - 1)

                @block.scalar
                def _(act):
                    for i in range(6):
                        act.wait_ge(wT_done, i + 1)
                        act.activation(tr[:, i, :], (bA, bB)[i % 2][:, 0:P], ACT.Copy).then_inc(wT_ready, 1)
                    act.wait_ge(wT_done, 7)
                    act.activation(l1T[:, :, :].rearrange("p f c -> p (f c)"), bA[:, :], ACT.Copy).then_inc(wT_ready, 1)
                    act.wait_ge(wT_done, 8)
                    act.activation(l2T[:, :, :].rearrange("p f c -> p (f c)"), bB[:, :], ACT.Copy).then_inc(wT_ready, 1)

                    def c_t0(g):
                        act.wait_ge(t0_done, g + 1)
                        if later(g, 1):
                            act.wait_ge(y1_done, g)
                        act.activation(xT[:, :], bB[:, :], ACT.Copy).then_inc(t0_ready, 1)

                    def c_ctx(g):
                        act.wait_ge(c_done, g + 1)
                        if later(g, 1):
                            act.wait_ge(v_done, g)
                        act.activation(cT[:, :], bC[:, 0:GB * M], ACT.Copy).then_inc(c_ready, 1)

                    def c_k(g, p, slot):
                        act.wait_ge(k_done, g + 1)
                        if later(g, 1):
                            act.wait_ge(kbd_loaded[1 - slot], 16 * H * (p + 1 if slot else p))
                        if later(g, 2):
                            act.wait_ge(s_done, GB * (g - 1))
                        act.activation(kT[:, :], bB[:, 0:GB * M], ACT.Identity, bias=cols[:, 2:3]).then_inc(k_ready, 1)

                    def c_v(g, slot):
                        act.wait_ge(v_done, g + 1)
                        if later(g, 2):
                            act.wait_ge(pv_done, GB * (g - 1))
                        else:
                            act.wait_ge(zeroed, 2)
                        dst = vp[:, slot, :, :].rearrange("p b (h w) -> p b h w", w=P + HD)[:, :, :, 0:HD]
                        act.activation(dst, bC[0:M, :].rearrange("p (b h i) -> p b h i", b=GB, h=H), ACT.Copy)\
                           .then_inc(v_ready, 1)

                    def c_t1(g):
                        act.wait_ge(t1_done, g + 1)
                        if later(g, 1):
                            act.wait_ge(q_done, g)
                        act.activation(n1T[:, :], bB[:, :], ACT.Copy).then_inc(t1_ready, 1)

                    def exps(g, b):
                        act.wait_ge(s_ready, GB * g + b + 1)
                        if b >= 2 or later(g, 1):
                            act.wait_ge(pn_ready, GB * g + b - 1)
                        act.activation(pr[:, b % 2, :, :], sc[:, b % 2, :, :], ACT.Exp).then_inc(exp_ready, 1)

                    def c_probsT(g, b):
                        for k in range(2):
                            act.wait_ge(tp_done, 2 * (GB * g + b) + k + 1)
                            if k == 0 and (b >= 2 or later(g, 1)):
                                act.wait_ge(pv_done, GB * g + b - 1)
                            act.activation(pT[:, b % 2, 4 * k:4 * k + 4, :].rearrange("p h t -> p (h t)"),
                                           psP[0:M, k, :], ACT.Copy).then_inc(tp_ready, 1)

                    def c_ca(g, slot):
                        act.wait_ge(pv_done, GB * (g + 1))
                        if later(g, 2):
                            act.wait_ge(out_done, g - 1)
                        act.activation(ca[:, slot, :], psO[:, :], ACT.Copy).then_inc(ca_ready, 1)

                    def c_t2(g):
                        act.wait_ge(t2_done, g + 1)
                        if later(g, 1):
                            act.wait_ge(l1_done, FT * g)
                        act.activation(n2T[:, :], bA[:, :], ACT.Copy).then_inc(t2_ready, 1)

                    def c_lin1(g, f):
                        act.wait_ge(l1_done, FT * g + f + 1)
                        if f == 0:
                            act.wait_ge(consts_ready, 1)
                            if later(g, 1):
                                act.wait_ge(l2_done, g)
                        act.activation(hT[:, f, :], bA[:, :], ACT.Relu, bias=l1b2[:, f:f + 1]).then_inc(l1a_ready, 1)

                    def prep(g):
                        c_t0(g)
                        c_ctx(g)
                        c_k(g, 0, 0)
                        c_v(g, 0)
                        c_t1(g)

                    def group(g, slot, nxt, prv, p):
                        np_ = p if slot == 0 else p + 1
                        exps(g, 0)
                        if nxt is not None:
                            c_t0(nxt)
                        exps(g, 1)
                        c_probsT(g, 0)
                        if nxt is not None:
                            c_ctx(nxt)
                        exps(g, 2)
                        c_probsT(g, 1)
                        if prv is not None:
                            c_t2(prv)
                        exps(g, 3)
                        c_probsT(g, 2)
                        if prv is not None:
                            c_lin1(prv, 0)
                            c_lin1(prv, 2)
                        if nxt is not None:
                            c_k(nxt, np_, 1 - slot)
                            c_v(nxt, 1 - slot)
                        c_probsT(g, 3)
                        if nxt is not None:
                            c_t1(nxt)
                        c_ca(g, slot)

                    def prepare(p):
                        prep(0)

                    def work(p, ahead):
                        first = isinstance(p, int) and p == 0
                        group(2 * p, 0, 2 * p + 1, None if first else 2 * p - 1, p)
                        group(2 * p + 1, 1, None if ahead is None else 2 * ahead, 2 * p, p)

                    over_pairs(act, PAIRS, prepare, work)
                    c_t2(NG - 1)
                    c_lin1(NG - 1, 0)
                    c_lin1(NG - 1, 2)

                @block.gpsimd
                def _(pool):
                    for slot in range(2):
                        pool.memset(kbd[:, slot, :, :], 0.0)
                        pool.memset(vp[:, slot, :, :], 0.0).then_inc(zeroed, 1)
                    pool.wait_ge(consts_ready, 1)

                    def probs(g, b):
                        pool.wait_ge(exp_ready, GB * g + b + 1)
                        pool.wait_ge(inv_ready, GB * g + b + 1)
                        if b >= 2 or later(g, 1):
                            pool.wait_ge(tp_done, 2 * (GB * g + b - 1))
                        pool.tensor_tensor(pn[:, b % 2, :, :], pr[:, b % 2, :, :],
                                           iv[:, b % 2, :].unsqueeze(2).broadcast_to([P, H, M]), ALU.mult)\
                            .then_inc(pn_ready, 1)

                    def residual1(g, slot):
                        pool.wait_ge(n1_ready, g + 1)
                        if later(g, 2):
                            pool.wait_ge(y2_ready, g - 1)
                        pool.tensor_tensor(r1t[:, :, :], n1[:, :, :], bcast(rows_bc[:, G1, :]), ALU.mult)\
                            .then_inc(r1t_ready, 1)
                        pool.wait_ge(r1t_ready, g + 1)
                        pool.tensor_tensor(r1[:, slot, :, :], r1t[:, :, :], bcast(r1b), ALU.add).then_inc(r1_ready, 1)

                    def residual2(g):
                        pool.wait_ge(n2_ready, g + 1)
                        if later(g, 1):
                            pool.wait_ge(y3_ready, g)
                        pool.tensor_tensor(r2t[:, :, :], n2[:, :, :], bcast(rows_bc[:, G2, :]), ALU.mult)\
                            .then_inc(r2t_ready, 1)
                        pool.wait_ge(r2t_ready, g + 1)
                        pool.tensor_tensor(r2[:, :, :], r2t[:, :, :], bcast(r2b), ALU.add).then_inc(r2_ready, 1)

                    def last(g):
                        pool.wait_ge(n3_ready, g + 1)
                        if later(g, 1):
                            pool.wait_ge(x_ready, g)
                        pool.tensor_tensor(o3[:, :, :], n3[:, :, :], bcast(g3), ALU.mult).then_inc(o3_ready, 1)
                        pool.wait_ge(o3_ready, g + 1)
                        pool.tensor_tensor(o3b[:, :, :], o3[:, :, :], bcast(b3), ALU.add).then_inc(o3b_ready, 1)

                    def prep(g):
                        norm_pool(pool, g, 0, lns[0], sems[0])
                        norm_pool(pool, g, 0, lns[1], sems[1])
                        residual1(g, 0)

                    def group(g, slot, nxt, prv):
                        if nxt is not None:
                            norm_pool(pool, nxt, 1 - slot, lns[0], sems[0])
                        probs(g, 0)
                        if prv is not None:
                            norm_pool(pool, prv, 1 - slot, lns[2], sems[2])
                        probs(g, 1)
                        if nxt is not None:
                            norm_pool(pool, nxt, 1 - slot, lns[1], sems[1])
                        probs(g, 2)
                        probs(g, 3)
                        if prv is not None:
                            residual2(prv)
                        if nxt is not None:
                            residual1(nxt, 1 - slot)
                        if prv is not None:
                            norm_pool(pool, prv, 1 - slot, lns[3], sems[3])
                            last(prv)

                    def post(g):
                        norm_pool(pool, g, 1, lns[2], sems[2])
                        residual2(g)
                        norm_pool(pool, g, 1, lns[3], sems[3])
                        last(g)

                    over_groups(pool, prep, group, post)

                @block.vector
                def _(v):
                    v.wait_ge(w_loaded, ALL_LOADED)
                    for i, c in enumerate((0, 3)):
                        v.tensor_scalar(bvb[:, i, :], ident[:, :], 0.0, cols[:, c:c + 1], ALU.mult, ALU.add)\
                         .then_inc(rowsum_step, 1)
                    v.wait_ge(rowsum_step, 2)
                    v.sem_inc(bvb_ready, 1)
                    v.tensor_tensor(r1b0[:, :], rows_bc[:, B1, :], rows_bc[:, MHO, :], ALU.add).then_inc(rowsum_step, 1)
                    v.tensor_tensor(r2b[:, :], rows_bc[:, B2, :], rows_bc[:, L2B, :], ALU.add).then_inc(rowsum_step, 1)
                    v.tensor_scalar(g3[:, :], rows_bc[:, 8, :], gates[:, 1:2], None, ALU.mult)
                    v.tensor_scalar(b3[:, :], rows_bc[:, 2, :], gates[:, 1:2], None, ALU.mult)
                    v.wait_ge(wT_ready, 8)
                    v.tensor_scalar(qg[:, :], tr[:, 2, :], cols[:, 4:5], None, ALU.mult)
                    v.tensor_scalar(l1g[:, :, :], l1T[:, :, :], cols[:, 6:7], None, ALU.mult)
                    v.wait_ge(rowsum_step, 4)
                    v.wait_ge(fold_done, 1)
                    v.tensor_tensor(m1t[:, :], bC[:, 0:P], ident[:, :], ALU.add)
                    v.tensor_tensor(y1b[:, :], bC[:, P:2 * P], rows_bc[:, 0, :], ALU.add)
                    v.tensor_tensor(r1b[:, :], bC[:, 2 * P:3 * P], r1b0[:, :], ALU.add)
                    v.tensor_tensor(bq2[:, :], bC[:, 3 * P:3 * P + 1], cols[:, 1:2], ALU.add)
                    v.tensor_tensor(l1b2[:, :], bC[:, 3 * P + 1:3 * P + 1 + FT], l1b[:, :], ALU.add)\
                     .then_inc(consts_ready, 1)
                    v.wait_ge(consts_ready, 1)

                    def x_of(g, b):
                        return X[:, bass.ds(g * GB + b, 1), :].rearrange("p a d -> p (a d)")

                    def moments(i, g, slot, src):
                        norm_moments(v, g, slot, src, lns[i], sems[i])

                    def apply(i, g, slot, src, dst):
                        norm_apply(v, g, slot, src, dst, lns[i], sems[i])

                    def moments0(g, slot):
                        moments(0, g, slot, lambda b: x_of(g, b))

                    def apply0(g, slot):
                        if later(g, 1):
                            v.wait_ge(t0_done, g)
                        apply(0, g, slot, lambda b: x_of(g, b), lambda b: xn[:, b, :])

                    def first_sum(g):
                        v.wait_ge(y1_done, g + 1)
                        v.tensor_tensor(y1[:, :, :], bB[:, :].rearrange("p (b d) -> p b d", b=GB), bcast(y1b), ALU.add)\
                         .then_inc(y1_ready, 1)

                    def moments1(g, slot):
                        v.wait_ge(y1_ready, g + 1)
                        moments(1, g, slot, lambda b: y1[:, b, :])

                    def apply1(g, slot):
                        if later(g, 1):
                            v.wait_ge(t1_done, g)
                            v.wait_ge(r1t_ready, g)
                        apply(1, g, slot, lambda b: y1[:, b, :], lambda b: n1[:, b, :])

                    def q_copy(g, slot):
                        v.wait_ge(q_done, g + 1)
                        if later(g, 2):
                            v.wait_ge(s_done, GB * (g - 1))
                        v.tensor_scalar(qT[:, slot, :], bB[:, :], bq2[:, :], Q_SCALE, ALU.add, ALU.mult)\
                         .then_inc(q_ready, 1)

                    def softmax_a(g, b):
                        s4 = psS[:, :, 0:HB].rearrange("p k (h m) -> p k h m", m=M)
                        v.wait_ge(s_done, GB * g + b + 1)
                        v.tensor_reduce(mx[:, b % 2, :].rearrange("p (k h) -> p k h", k=2), s4, AX.X, ALU.max)\
                         .then_inc(mx_ready, 1)
                        v.wait_ge(mx_ready, GB * g + b + 1)
                        if b >= 2 or later(g, 1):
                            v.wait_ge(exp_ready, GB * g + b - 1)
                        v.tensor_tensor(sc[:, b % 2, :, :].rearrange("p (k h) m -> p k h m", k=2), s4,
                                        mx[:, b % 2, :].rearrange("p (k h) -> p k h", k=2).unsqueeze(3)
                                        .broadcast_to([P, 2, H // 2, M]), ALU.subtract).then_inc(s_ready, 1)

                    def softmax_b(g, b):
                        v.wait_ge(exp_ready, GB * g + b + 1)
                        v.tensor_reduce(sm[:, b % 2, :], pr[:, b % 2, :, :], AX.X, ALU.add).then_inc(sum_ready, 1)
                        v.wait_ge(sum_ready, GB * g + b + 1)
                        if b >= 2 or later(g, 1):
                            v.wait_ge(pn_ready, GB * g + b - 1)
                        v.reciprocal(iv[:, b % 2, :], sm[:, b % 2, :]).then_inc(inv_ready, 1)

                    def second_sum(g, slot):
                        v.wait_ge(out_done, g + 1)
                        v.wait_ge(r1_ready, g + 1)
                        v.tensor_tensor(y2[:, :, :], bA[:, :].rearrange("p (b d) -> p b d", b=GB), r1[:, slot, :, :],
                                        ALU.add).then_inc(y2_ready, 1)

                    def moments2(g, slot):
                        v.wait_ge(y2_ready, g + 1)
                        moments(2, g, slot, lambda b: y2[:, b, :])

                    def apply2(g, slot):
                        if later(g, 1):
                            v.wait_ge(t2_done, g)
                            v.wait_ge(r2t_ready, g)
                        apply(2, g, slot, lambda b: y2[:, b, :], lambda b: n2[:, b, :])

                    def relu_copy(g, f):
                        v.wait_ge(l1_done, FT * g + f + 1)
                        if f == 1 and later(g, 1):
                            v.wait_ge(l2_done, g)
                        v.tensor_scalar(hT[:, f, :], bC[:, :], l1b2[:, f:f + 1], 0.0, ALU.add, ALU.max)\
                         .then_inc(l1v_ready, 1)

                    def third_sum(g):
                        v.wait_ge(l2_done, g + 1)
                        v.wait_ge(r2_ready, g + 1)
                        v.tensor_tensor(y3[:, :, :], bA[:, :].rearrange("p (b d) -> p b d", b=GB), r2[:, :, :],
                                        ALU.add).then_inc(y3_ready, 1)

                    def moments3(g, slot):
                        v.wait_ge(y3_ready, g + 1)
                        moments(3, g, slot, lambda b: y3[:, b, :])

                    def apply3(g, slot):
                        if later(g, 1):
                            v.wait_ge(o3_ready, g)
                        apply(3, g, slot, lambda b: y3[:, b, :], lambda b: n3[:, b, :])

                    def add_x(g):
                        v.wait_ge(o3b_ready, g + 1)
                        xg = X[:, bass.ds(g * GB, GB), :].rearrange("p b d -> p (b d)")
                        v.tensor_tensor(xg, xg, o3b[:, :, :].rearrange("p b d -> p (b d)"), ALU.add).then_inc(x_ready, 1)

                    def prep(g):
                        moments0(g, 0)
                        apply0(g, 0)
                        first_sum(g)
                        moments1(g, 0)
                        apply1(g, 0)
                        q_copy(g, 0)

                    def group(g, slot, nxt, prv):
                        other = 1 - slot
                        if nxt is not None:
                            moments0(nxt, other)
                        softmax_a(g, 0)
                        if nxt is not None:
                            apply0(nxt, other)
                        if prv is not None:
                            if later(prv, 1):
                                add_x(prv - 1)
                            second_sum(prv, other)
                            moments2(prv, other)
                        softmax_a(g, 1)
                        softmax_b(g, 0)
                        if prv is not None:
                            apply2(prv, other)
                        if nxt is not None:
                            first_sum(nxt)
                            moments1(nxt, other)
                        softmax_b(g, 1)
                        softmax_a(g, 2)
                        softmax_b(g, 2)
                        softmax_a(g, 3)
                        if nxt is not None:
                            apply1(nxt, other)
                        softmax_b(g, 3)
                        if prv is not None:
                            relu_copy(prv, 1)
                            relu_copy(prv, 3)
                            third_sum(prv)
                            moments3(prv, other)
                        if nxt is not None:
                            q_copy(nxt, other)
                        if prv is not None:
                            apply3(prv, other)

                    def post(g):
                        add_x(g - 1)
                        second_sum(g, 1)
                        moments2(g, 1)
                        apply2(g, 1)
                        relu_copy(g, 1)
                        relu_copy(g, 3)
                        third_sum(g)
                        moments3(g, 1)
                        apply3(g, 1)
                        add_x(g)

                    over_groups(v, prep, group, post)

        end_phase()

        with ExitStack() as st:
            HC = w1.shape[0] // P
            HW = HC * P
            TAPS = conv_w.shape[2]
            BIG = 1.5 * 2.0 ** 23
            QMAX = 127.0
            W_COUNT = float(HW * D)
            TQ_LAG = 3

            w1n = sb(st, "d_w1n", [P, HC, D])
            w2n = sb(st, "d_w2n", [P, HC, P])
            cwn = sb(st, "d_cwn", [P, HC, TAPS])
            cbn = sb(st, "d_cbn", [P, HW])
            asum = sb(st, "d_asum", [P, 2])
            ones = sb(st, "d_ones", [P, P])
            ones_bf = sb(st, "d_ones_bf", [P, P], BF16)
            mean = sb(st, "d_mean", [P, 2])
            rmean = sb(st, "d_rmean", [P, 2])
            ta = sb(st, "d_ta", [P, 2, HW])
            tb = sb(st, "d_tb", [P, 2, HW])
            tt = sb(st, "d_tt", [P, 2, HW])
            w1k = sb(st, "d_w1k", [P, TAPS, HC, D])
            wkh = sb(st, "d_wkh", [P, TAPS, HW], F32R)
            wkl = sb(st, "d_wkl", [P, TAPS, HW], F32R)
            w2T = sb(st, "d_w2T", [P, HC, P], BF16)
            cb1 = sb(st, "d_cb1", [P, HW], BF16)
            cr1 = sb(st, "d_cr1", [P, HW])
            cb2 = sb(st, "d_cb2", [P, HW], BF16)
            cr2 = sb(st, "d_cr2", [P, HW])
            cm1 = sb(st, "d_cm1", [P, HW])
            cm2 = sb(st, "d_cm2", [P, HW])
            cb = sb(st, "d_cb", [P, HW], BF16)
            sw2 = sb(st, "d_sw2", [P, 1])
            big = sb(st, "d_big", [P, HW])

            xn = sb(st, "d_xn", [P, GB, D])
            am = sb(st, "d_am", [P, GB])
            amc = sb(st, "d_amc", [P, GB])
            ar = sb(st, "d_ar", [P, GB])
            asc = sb(st, "d_asc", [P, GB])
            ais = sb(st, "d_ais", [P, GB])
            za = sb(st, "d_za", [P, GB, D])
            zb = sb(st, "d_zb", [P, GB, D])
            xq = sb(st, "d_xq", [P, GB, D])
            xh = sb(st, "d_xh", [P, 2, GB, P + 2], F32R)
            xl = sb(st, "d_xl", [P, 2, GB, P + 2], F32R)
            sl = sb(st, "d_sl", [P, GB, HW])
            hm = sb(st, "d_hm", [P, GB])
            hmc = sb(st, "d_hmc", [P, GB])
            hr = sb(st, "d_hr", [P, GB])
            hsc = sb(st, "d_hsc", [P, GB])
            hf = sb(st, "d_hf", [P, 2, GB])
            hz = sb(st, "d_hz", [P, GB, HW])
            hc = sb(st, "d_hc", [P, GB, HW])
            hq = sb(st, "d_hq", [P, GB, HW], BF16)
            hqT = sb(st, "d_hqT", [P, GB, HC, P], BF16)
            ln = norm_tiles(st, "lnD")

            psT = bank(st, "d_psT")
            psH = [bank(st, f"d_psH{b}") for b in range(GB)]
            psQ = [bank(st, f"d_psQ{b}", BF16, 1024) for b in range(2)]
            psO = bank(st, "d_psO")

            w_loaded = sem("d_w_loaded")
            prepv = sem("d_vector_prepared")
            step = sem("d_prepare_step")
            ones_ready = sem("d_ones_ready")
            sums_done = sem("d_sums_done")
            wk_done = sem("d_wk_done")
            wkh_ready = sem("d_wk_upper_ready")
            wkl_ready = sem("d_wk_lower_ready")
            w2T_ready = sem("d_w2T_ready")
            padded = sem("d_padded")
            lnD = norm_sems("d_ln")
            normed = lnD[-1]
            quant = sem("d_quant_step")
            xq_ready = sem("d_xq_ready")
            xT_done = sem("d_xT_done")
            xh_ready = sem("d_xh_ready")
            xl_ready = sem("d_xl_ready")
            h_done = sem("d_hidden_done")
            sl_ready = sem("d_silu_ready")
            hstep = sem("d_hidden_scale_step")
            hz_ready = sem("d_hidden_scaled")
            hc_ready = sem("d_hidden_clipped")
            hq_ready = sem("d_hidden_rounded")
            tq_done = sem("d_hiddenT_done")
            tq_ready = sem("d_hiddenT_ready")
            o_done = sem("d_out_done")
            x_ready = sem("d_x_ready")

            def over_groups(eng, prep, group, tail):
                def prepare(p):
                    prep(0)

                def work(p, ahead):
                    group(2 * p, 0, 2 * p + 1)
                    group(2 * p + 1, 1, None if ahead is None else 2 * ahead)

                over_pairs(eng, PAIRS, prepare, work)
                tail()

            with nc.Block() as block:
                @block.sync
                def _(sp):
                    sp.dma_start(w1n[:, :, :], w1.rearrange("(c p) d -> p c d", p=P)).then_inc(w_loaded, 16)
                    sp.dma_start(w2n[:, :, :].rearrange("p c k -> p (c k)"), w2).then_inc(w_loaded, 16)
                    sp.dma_start(cwn[:, :, :], conv_w.rearrange("(c p) a k -> p c (a k)", p=P)).then_inc(w_loaded, 16)
                    sp.dma_start(cbn[:, :], conv_b.partition_broadcast(P)).then_inc(w_loaded, 16)

                    def store(g):
                        sp.wait_ge(x_ready, g + 1)
                        sp.dma_start(out[bass.ds(g * GB, GB), :, :].rearrange("b s d -> s b d"),
                                     X[:, bass.ds(g * GB, GB), :]).then_inc(out_stored, 16)

                    with sp.Fori(0, NG) as g:
                        store(g)
                    sp.wait_ge(out_stored, 16 * NG)

                @block.tensor
                def _(pe):
                    pe.wait_ge(ones_ready, 1)
                    pe.wait_ge(prepv, 1)
                    pe.matmul(psO[:, 0:2], ones[:, :], asum[:, :], start=True, stop=True).then_inc(sums_done, 1)
                    pe.wait_ge(prepv, 2)
                    for k in range(TAPS):
                        for c in range(HC):
                            i = pe.transpose(psH[k][:, c * P:(c + 1) * P], w1k[:, k, c, :], ident[:, :])
                        i.then_inc(wk_done, 1)
                    for c in range(HC):
                        i = pe.transpose(psH[TAPS][:, c * P:(c + 1) * P], tt[:, 1, c * P:(c + 1) * P], ident[:, :])
                    i.then_inc(wk_done, 1)

                    def x_transposes(g):
                        pe.wait_ge(xq_ready, g + 1)
                        if later(g, 1):
                            pe.wait_ge(xl_ready, g)
                        for b in range(GB):
                            i = pe.transpose(psT[:, b * P:(b + 1) * P], xq[:, b, :], ident[:, :])
                        i.then_inc(xT_done, 1)

                    def hidden(g, b, slot):
                        if b == 0:
                            if not later(g, 1):
                                pe.wait_ge(wkl_ready, TAPS)
                                pe.wait_ge(w2T_ready, 1)
                                pe.wait_ge(prepv, 3)
                            pe.wait_ge(xh_ready, g + 1)
                            pe.wait_ge(xl_ready, g + 1)
                        if later(g, 1):
                            pe.wait_ge(sl_ready, GB * (g - 1) + b + 1)
                        pe.matmul(psH[b][:, :], ones_bf[:, :], cb[:, :], start=True, stop=False)
                        for k in range(TAPS):
                            h, lo = xh[:, slot, b, k:k + P], xl[:, slot, b, k:k + P]
                            pe.matmul(psH[b][:, :], lo, wkh[:, k, :], start=False, stop=False)
                            pe.matmul(psH[b][:, :], h, wkl[:, k, :], start=False, stop=False)
                            i = pe.matmul(psH[b][:, :], h, wkh[:, k, :], start=False, stop=(k == TAPS - 1))
                        i.then_inc(h_done, 1)

                    def hidden_transposes(g, b):
                        n = GB * g + b
                        pe.wait_ge(hq_ready, n + 1)
                        if b >= 2 or later(g, 1):
                            pe.wait_ge(tq_ready, n - 1)
                        for c in range(HC):
                            i = pe.transpose(psQ[b % 2][:, c * P:(c + 1) * P], hq[:, b, c * P:(c + 1) * P],
                                             ident_bf[:, :])
                        i.then_inc(tq_done, 1)

                    def second(g, b):
                        pe.wait_ge(tq_ready, GB * g + b + 1)
                        if b == 0 and later(g, 1):
                            pe.wait_ge(x_ready, g)
                        for c in range(HC):
                            i = pe.matmul(psO[:, b * P:(b + 1) * P], hqT[:, b, c, :], w2T[:, c, :],
                                          start=(c == 0), stop=(c == HC - 1))
                        i.then_inc(o_done, 1)

                    def group(g, slot, nxt):
                        for b in range(GB):
                            hidden(g, b, slot)
                            if b == TQ_LAG:
                                hidden_transposes(g, 0)
                            elif later(g, 1):
                                hidden_transposes(g - 1, b + 1)
                            if later(g, 1):
                                second(g - 1, b)
                            if b == 1 and nxt is not None:
                                x_transposes(nxt)

                    def tail():
                        for b in range(GB):
                            if b < GB - 1:
                                hidden_transposes(NG - 1, b + 1)
                            second(NG - 1, b)

                    over_groups(pe, x_transposes, group, tail)

                @block.scalar
                def _(act):
                    for k in range(TAPS):
                        act.wait_ge(wk_done, k + 1)
                        act.activation(wkh[:, k, :], psH[k][:, :], ACT.Copy).then_inc(wkh_ready, 1)
                    act.wait_ge(wk_done, TAPS + 1)
                    act.activation(w2T[:, :, :].rearrange("p c k -> p (c k)"), psH[TAPS][:, :], ACT.Copy)\
                       .then_inc(w2T_ready, 1)

                    def x_upper(g, slot):
                        act.wait_ge(xT_done, g + 1)
                        if later(g, 2):
                            act.wait_ge(h_done, GB * (g - 1))
                        else:
                            act.wait_ge(padded, 1)
                        act.activation(xh[:, slot, :, 1:P + 1], psT[:, :].rearrange("p (b t) -> p b t", b=GB),
                                       ACT.Copy).then_inc(xh_ready, 1)

                    def silu(g, b):
                        act.wait_ge(h_done, GB * g + b + 1)
                        if later(g, 1):
                            act.wait_ge(hz_ready, GB * (g - 1) + b + 1)
                        act.activation(sl[:, b, :], psH[b][:, :], ACT.Silu).then_inc(sl_ready, 1)

                    def scale(g, b):
                        act.wait_ge(hstep, 4 * (GB * g + b) + 4)
                        if later(g, 1):
                            act.wait_ge(hc_ready, GB * (g - 1) + b + 1)
                        act.activation(hz[:, b, :], sl[:, b, :], ACT.Identity, bias=big[:, 0:1],
                                       scale=hsc[:, b:b + 1]).then_inc(hz_ready, 1)

                    def copy_hidden(g, b):
                        act.wait_ge(tq_done, GB * g + b + 1)
                        if later(g, 1):
                            act.wait_ge(o_done, GB * (g - 1) + b + 1)
                        act.activation(hqT[:, b, :, :].rearrange("p c k -> p (c k)"), psQ[b % 2][:, 0:HW],
                                       ACT.Copy).then_inc(tq_ready, 1)

                    def group(g, slot, nxt):
                        for b in range(GB):
                            silu(g, b)
                            if b >= 1:
                                scale(g, b - 1)
                            elif later(g, 1):
                                scale(g - 1, GB - 1)
                            if later(g, 1):
                                copy_hidden(g - 1, b)
                            if b == 2 and nxt is not None:
                                x_upper(nxt, 1 - slot)

                    def tail():
                        scale(NG - 1, GB - 1)
                        for b in range(GB):
                            copy_hidden(NG - 1, b)

                    over_groups(act, lambda g: x_upper(g, 0), group, tail)

                @block.gpsimd
                def _(pool):
                    pool.memset(ones[:, :], 1.0)
                    pool.memset(ones_bf[:, :], 1.0)
                    pool.memset(big[:, :], BIG).then_inc(ones_ready, 1)
                    pool.memset(xh[:, :, :, :].bitcast(F32), 0.0)
                    pool.memset(xl[:, :, :, :].bitcast(F32), 0.0).then_inc(padded, 1)

                    def rounded(g, b):
                        pool.wait_ge(hc_ready, GB * g + b + 1)
                        if later(g, 1):
                            pool.wait_ge(tq_done, GB * (g - 1) + b + 1)
                        pool.tensor_tensor(hq[:, b, :], hc[:, b, :], big[:, :], ALU.subtract).then_inc(hq_ready, 1)

                    def group(g, slot, nxt):
                        for b in range(GB):
                            if b >= 1:
                                rounded(g, b - 1)
                            elif later(g, 1):
                                rounded(g - 1, GB - 1)
                            if b == 0 and nxt is not None:
                                norm_pool(pool, nxt, 1 - slot, ln, lnD)

                    over_groups(pool, lambda g: norm_pool(pool, g, 0, ln, lnD), group,
                                lambda: rounded(NG - 1, GB - 1))

                @block.vector
                def _(v):
                    v.wait_ge(w_loaded, 64)
                    for i, w in enumerate((w1n, w2n)):
                        ins = v.tensor_reduce(asum[:, i:i + 1], w[:, :, :].rearrange("p c d -> p (c d)"), AX.X,
                                              ALU.add, apply_absolute_value=True)
                    ins.then_inc(prepv, 1)
                    v.wait_ge(sums_done, 1)
                    v.tensor_scalar(mean[:, :], psO[:, 0:2], 1.0 / W_COUNT, 1e-5, ALU.mult, ALU.max).then_inc(step, 1)
                    v.wait_ge(step, 1)
                    v.reciprocal(rmean[:, :], mean[:, :])
                    v.tensor_scalar(sw2[:, :], mean[:, 1:2], gates[:, 3:4], None, ALU.mult).then_inc(step, 1)
                    v.wait_ge(step, 2)
                    for i, w in enumerate((w1n, w2n)):
                        ins = v.tensor_scalar(ta[:, i, :], w[:, :, :].rearrange("p c d -> p (c d)"),
                                              rmean[:, i:i + 1], BIG, ALU.mult, ALU.add)
                    ins.then_inc(step, 1)
                    v.wait_ge(step, 3)
                    v.tensor_scalar(tb[:, :, :], ta[:, :, :], BIG, 1.0, ALU.subtract, ALU.min).then_inc(step, 1)
                    v.wait_ge(step, 4)
                    v.tensor_scalar(tt[:, :, :], tb[:, :, :], -1.0, None, ALU.max).then_inc(step, 1)
                    v.wait_ge(step, 5)
                    for k in range(TAPS):
                        for c in range(HC):
                            ins = v.tensor_scalar(w1k[:, k, c, :], tt[:, 0, c * D:(c + 1) * D], cwn[:, c, k:k + 1],
                                                  mean[:, 0:1], ALU.mult, ALU.mult)
                    ins.then_inc(prepv, 1)
                    v.tensor_copy(cb1[:, :], cbn[:, :]).then_inc(step, 1)
                    v.wait_ge(step, 6)
                    v.tensor_tensor(cr1[:, :], cbn[:, :], cb1[:, :], ALU.subtract)
                    v.tensor_scalar(cm1[:, :], cb1[:, :], ident[:, 0:1], None, ALU.mult).then_inc(step, 1)
                    v.wait_ge(step, 7)
                    v.tensor_copy(cb2[:, :], cr1[:, :]).then_inc(step, 1)
                    v.wait_ge(step, 8)
                    v.tensor_tensor(cr2[:, :], cr1[:, :], cb2[:, :], ALU.subtract)
                    v.scalar_tensor_tensor(out=cm2[:, :], in0=cb2[:, :], scalar=ident[:, 1:2], in1=cm1[:, :],
                                           op0=ALU.mult, op1=ALU.add).then_inc(step, 1)
                    v.wait_ge(step, 9)
                    v.scalar_tensor_tensor(out=cb[:, :], in0=cr2[:, :], scalar=ident[:, 2:3], in1=cm2[:, :],
                                           op0=ALU.mult, op1=ALU.add).then_inc(prepv, 1)
                    for k in range(TAPS):
                        v.wait_ge(wkh_ready, k + 1)
                        v.tensor_tensor(wkl[:, k, :], psH[k][:, :], wkh[:, k, :].bitcast(F32), ALU.subtract)\
                         .then_inc(wkl_ready, 1)

                    def x_of(g, b):
                        return X[:, bass.ds(g * GB + b, 1), :].rearrange("p a d -> p (a d)")

                    def moments(g, slot):
                        norm_moments(v, g, slot, lambda b: x_of(g, b), ln, lnD)

                    STEPS = 6

                    def quantise(g, slot):
                        norm_apply(v, g, slot, lambda b: x_of(g, b), lambda b: xn[:, b, :], ln, lnD)
                        v.wait_ge(normed, g + 1)
                        v.tensor_reduce(am[:, :], xn[:, :, :], AX.X, ALU.max, apply_absolute_value=True)\
                         .then_inc(quant, 1)
                        v.wait_ge(quant, STEPS * g + 1)
                        v.tensor_scalar(amc[:, :], am[:, :], 1e-5, None, ALU.max).then_inc(quant, 1)
                        v.wait_ge(quant, STEPS * g + 2)
                        v.reciprocal(ar[:, :], amc[:, :])
                        v.tensor_scalar(ais[:, :], amc[:, :], 1.0 / QMAX, None, ALU.mult).then_inc(quant, 1)
                        v.wait_ge(quant, STEPS * g + 3)
                        v.tensor_scalar(asc[:, :], ar[:, :], QMAX, None, ALU.mult).then_inc(quant, 1)
                        v.wait_ge(quant, STEPS * g + 4)
                        for b in range(GB):
                            i = v.tensor_scalar(za[:, b, :], xn[:, b, :], asc[:, b:b + 1], BIG, ALU.mult, ALU.add)
                        i.then_inc(quant, 1)
                        v.wait_ge(quant, STEPS * g + 5)
                        v.tensor_scalar(zb[:, :, :], za[:, :, :], BIG - QMAX - 1, BIG + QMAX, ALU.max, ALU.min)\
                         .then_inc(quant, 1)
                        v.wait_ge(quant, STEPS * g + 6)
                        if later(g, 1):
                            v.wait_ge(xT_done, g)
                        for b in range(GB):
                            i = v.tensor_scalar(xq[:, b, :], zb[:, b, :], BIG, ais[:, b:b + 1],
                                                ALU.subtract, ALU.mult)
                        i.then_inc(xq_ready, 1)

                    def x_lower(g, slot):
                        v.wait_ge(xh_ready, g + 1)
                        v.tensor_tensor(xl[:, slot, :, 1:P + 1], psT[:, :].rearrange("p (b t) -> p b t", b=GB),
                                        xh[:, slot, :, 1:P + 1].bitcast(F32), ALU.subtract).then_inc(xl_ready, 1)

                    def hidden_scale(g, b, slot):
                        n = GB * g + b
                        v.wait_ge(sl_ready, n + 1)
                        v.tensor_reduce(hm[:, b:b + 1], sl[:, b, :], AX.X, ALU.max, apply_absolute_value=True)\
                         .then_inc(hstep, 1)
                        v.wait_ge(hstep, 4 * n + 1)
                        v.tensor_scalar(hmc[:, b:b + 1], hm[:, b:b + 1], 1e-5, None, ALU.max).then_inc(hstep, 1)
                        v.wait_ge(hstep, 4 * n + 2)
                        v.reciprocal(hr[:, b:b + 1], hmc[:, b:b + 1])
                        v.tensor_scalar(hf[:, slot, b:b + 1], hmc[:, b:b + 1], 1.0 / QMAX, sw2[:, :],
                                        ALU.mult, ALU.mult).then_inc(hstep, 1)
                        v.wait_ge(hstep, 4 * n + 3)
                        v.tensor_scalar(hsc[:, b:b + 1], hr[:, b:b + 1], QMAX, None, ALU.mult).then_inc(hstep, 1)

                    def hidden_clip(g, b):
                        n = GB * g + b
                        v.wait_ge(hz_ready, n + 1)
                        if later(g, 1):
                            v.wait_ge(hq_ready, GB * (g - 1) + b + 1)
                        v.tensor_scalar(hc[:, b, :], hz[:, b, :], BIG - QMAX - 1, BIG + QMAX, ALU.max, ALU.min)\
                         .then_inc(hc_ready, 1)

                    def final(g, slot):
                        v.wait_ge(o_done, GB * (g + 1))
                        for b in range(GB):
                            i = v.scalar_tensor_tensor(out=x_of(g, b), in0=psO[:, b * P:(b + 1) * P],
                                                       scalar=hf[:, slot, b:b + 1], in1=x_of(g, b),
                                                       op0=ALU.mult, op1=ALU.add)
                        i.then_inc(x_ready, 1)

                    def prep(g):
                        moments(g, 0)
                        quantise(g, 0)
                        x_lower(g, 0)

                    def group(g, slot, nxt):
                        for b in range(GB):
                            hidden_scale(g, b, slot)
                            if b >= 1:
                                hidden_clip(g, b - 1)
                            elif later(g, 1):
                                hidden_clip(g - 1, GB - 1)
                            if nxt is not None:
                                if b == 0:
                                    moments(nxt, 1 - slot)
                                    quantise(nxt, 1 - slot)
                                if b == 2:
                                    x_lower(nxt, 1 - slot)
                        if later(g, 1):
                            final(g - 1, 1 - slot)

                    def tail():
                        hidden_clip(NG - 1, GB - 1)
                        final(NG - 1, 1)

                    over_groups(v, prep, group, tail)


_INS = ['x', 'ctx_1024', 'mask_BxS2_if1', 'g_xattn', 'g_ffn', 'L0_xattn_W', 'L0_xattn_diagonal',
        'L0_ffn_gate_w', 'L0_ffn_wg', 'L0_ffn_wu', 'L0_ffn_wd', 'L0_ffn_swg', 'L0_ffn_swu', 'L0_ffn_swd',
        'L1_xattn_qkv_w', 'L1_xattn_qkv_b', 'L1_xattn_sa_out_w', 'L1_xattn_sa_out_b',
        'L1_xattn_in_proj_w', 'L1_xattn_in_proj_b', 'L1_xattn_mha_out_w', 'L1_xattn_mha_out_b',
        'L1_xattn_lin1_w', 'L1_xattn_lin1_b', 'L1_xattn_lin2_w', 'L1_xattn_lin2_b',
        'L1_xattn_ln1_g', 'L1_xattn_ln1_b', 'L1_xattn_ln2_g', 'L1_xattn_ln2_b', 'L1_xattn_ln3_g', 'L1_xattn_ln3_b',
        'L1_ffn_w1', 'L1_ffn_conv_w', 'L1_ffn_conv_b', 'L1_ffn_w2']


def kernel(**inputs):
    import numpy as np
    import concourse.bacc as bacc
    from concourse.bass_utils import run_bass_kernel_spmd

    nc = bacc.Bacc("TRN2", target_bir_lowering=False, num_devices=1)
    arrays, args = {}, []
    for name in _INS:
        a = np.ascontiguousarray(inputs[name])
        arrays[f"in_{name}"] = a
        args.append(nc.dram_tensor(f"in_{name}", a.shape, mybir.dt.from_np(a.dtype), kind="ExternalInput").ap())
    n_exp, _, inter = inputs['L0_ffn_wg'].shape
    consts = {
        "sel": np.tile(np.repeat(np.eye(n_exp, dtype=np.float32), inter, axis=1), (3, 1)),
        "ramp": np.arange(n_exp, 0, -1, dtype=np.float32),
    }
    for name, a in consts.items():
        arrays[f"const_{name}"] = a
        args.append(nc.dram_tensor(f"const_{name}", a.shape, F32, kind="ExternalInput").ap())
    out = nc.dram_tensor("out_x", inputs['x'].shape, F32, kind="ExternalOutput").ap()
    flamingo_gated(nc, *args, out)
    r = run_bass_kernel_spmd(nc, [arrays], core_ids=[0])
    return r.results[0]["out_x"]
```

```python
import math
from contextlib import ExitStack

import concourse.bass as bass
from concourse import mybir
from concourse.alu_op_type import AluOpType as ALU

ACT = mybir.ActivationFunctionType
AX = mybir.AxisListType
F32 = mybir.dt.float32
F32R = mybir.dt.float32r
BF16 = mybir.dt.bfloat16
I32 = mybir.dt.int32

P = 128
GB = 4
GT = GB * P
LN_EPS = 1e-5
NEG = -10000.0


def later(g, n):
    return not isinstance(g, int) or g >= n


def over_pairs(eng, pairs, prepare, work, peeled=1):
    prepare(0)
    for p in range(peeled):
        work(p, p + 1)
    with eng.Fori(peeled, pairs - 1) as p:
        work(p, p + 1)
    work(pairs - 1, None)


def flamingo_gated(nc, x, ctx_tokens, mask, g_xattn, g_ffn, W, diagonal, gate_w, wg, wu, wd, swg, swu, swd,
                   qkv_w, qkv_b, sa_out_w, sa_out_b, in_proj_w, in_proj_b, mha_out_w, mha_out_b,
                   lin1_w, lin1_b, lin2_w, lin2_b, ln1_g, ln1_b, ln2_g, ln2_b, ln3_g, ln3_b,
                   w1, conv_w, conv_b, w2, sel_const, ramp_const, out):
    B, S, D = x.shape
    M = ctx_tokens.shape[1]
    assert S == P and D == P and B % (2 * GB) == 0
    NG = B // GB
    PAIRS = NG // 2

    top = ExitStack()

    sems_of_phase = []

    def sem(name):
        s = nc.alloc_semaphore(name=name)
        sems_of_phase.append(s)
        return s

    def end_phase():
        nc.clear_and_free_semaphores(list(sems_of_phase))
        nc.all_engine_barrier()
        sems_of_phase.clear()

    def sb(stack, name, shape, dt=F32):
        return stack.enter_context(nc.sbuf_tensor(name, shape, dt))

    def bank(stack, name, dt=F32, width=512):
        return stack.enter_context(nc.psum_tensor(name, [P, width], dt))

    with top:
        X = sb(top, "X", [P, B, D])
        ident = sb(top, "ident", [P, P])
        ident_bf = sb(top, "ident_bf", [P, P], BF16)
        gates = sb(top, "gates", [P, 4])
        graw = sb(top, "graw", [P, 4])
        half_neg = sb(top, "half_neg", [P, GB])
        eps_tile = sb(top, "eps_tile", [P, GB])

        const_filled = sem("const_filled")
        const_ready = sem("const_ready")
        gates_loaded = sem("gates_loaded")
        gates_ready = sem("gates_ready")
        x_loaded = [sem("x_loaded_even"), sem("x_loaded_odd")]
        out_stored = sem("out_stored")
        sems_of_phase.clear()

        def norm_sems(tag):
            return [sem(f"{tag}_{what}") for what in ("stats", "step", "moments", "eps", "rstd", "normed")]

        def norm_tiles(stack, tag):
            return (sb(stack, f"{tag}_stats", [P, 2, GB, 6]), sb(stack, f"{tag}_sums", [P, 2, GB, 2]),
                    sb(stack, f"{tag}_diff", [P, 2, GB]), sb(stack, f"{tag}_diff2", [P, 2, GB]),
                    sb(stack, f"{tag}_mean", [P, 2, GB]), sb(stack, f"{tag}_var", [P, 2, GB]),
                    sb(stack, f"{tag}_vareps", [P, 2, GB]), sb(stack, f"{tag}_rstd", [P, 2, GB]))

        def norm_moments(v, g, slot, src, tiles, sems):
            stt, sums, diff, diff2, mean, var, _, _ = (t[:, slot] for t in tiles)
            stats, step, moments, _, _, _ = sems
            for b in range(GB):
                i = v.bn_stats(stt[:, b, :], src(b))
            i.then_inc(stats, 1)
            v.wait_ge(stats, g + 1)
            v.tensor_tensor(diff, stt[:, :, 1], stt[:, :, 4], ALU.subtract)
            v.tensor_tensor(sums, stt[:, :, 1:3], stt[:, :, 4:6], ALU.add).then_inc(step, 1)
            v.wait_ge(step, 2 * g + 1)
            v.tensor_scalar(mean, sums[:, :, 0], 0.5, None, ALU.mult)
            v.scalar_tensor_tensor(out=diff2, in0=diff, scalar=0.25, in1=diff, op0=ALU.mult, op1=ALU.mult)\
             .then_inc(step, 1)
            v.wait_ge(step, 2 * g + 2)
            v.scalar_tensor_tensor(out=var, in0=sums[:, :, 1], scalar=1.0 / D, in1=diff2,
                                   op0=ALU.mult, op1=ALU.add).then_inc(moments, 1)

        def norm_apply(v, g, slot, src, dst, tiles, sems):
            mean, rstd_t = tiles[4], tiles[7]
            v.wait_ge(sems[4], g + 1)
            for b in range(GB):
                i = v.tensor_scalar(dst(b), src(b), mean[:, slot, b:b + 1], rstd_t[:, slot, b:b + 1],
                                    ALU.subtract, ALU.mult)
            i.then_inc(sems[5], 1)

        def norm_pool(pool, g, slot, tiles, sems):
            var, vareps, rstd_t = tiles[5], tiles[6], tiles[7]
            _, _, moments, eps, rstd, normed = sems
            pool.wait_ge(moments, g + 1)
            if later(g, 2):
                pool.wait_ge(normed, g - 1)
            pool.tensor_tensor(vareps[:, slot, :], var[:, slot, :], eps_tile[:, :], ALU.add).then_inc(eps, 1)
            pool.wait_ge(eps, g + 1)
            pool.tensor_tensor(rstd_t[:, slot, :], vareps[:, slot, :], half_neg[:, :], ALU.pow).then_inc(rstd, 1)

        with ExitStack() as st:
            Wn = sb(st, "Wn", [P, P])
            WT = sb(st, "WT", [P, P])
            diag = sb(st, "diag", [P, 1])
            ctxs = sb(st, "ctxs", [M, 2, GB, D])
            ctxv = sb(st, "ctxv", [M, 2, GB, D])
            mski = sb(st, "mski", [P, 2, GB * M], I32)
            mskf = sb(st, "mskf", [P, 2, GB * M])
            xn = sb(st, "xn", [P, 2, GB, D])
            xT = sb(st, "xT", [P, 2, GT])
            cT = sb(st, "cT", [P, 2, GB * M])
            r1 = sb(st, "r1", [P, 2, GT])
            r2 = sb(st, "r2", [P, 2, GB * M])
            sc = sb(st, "sc", [P, 2, GB, M])
            mx = sb(st, "mx", [P, 2, GB])
            pr = sb(st, "pr", [P, 2, GB, M])
            sm = sb(st, "sm", [P, 2, GB])
            ri = sb(st, "ri", [P, 2, GB])
            rg = sb(st, "rg", [P, 2, GB])
            prT = sb(st, "prT", [M, 2, GT])
            ln = norm_tiles(st, "lnA")

            psX = [bank(st, f"a_psX{s}") for s in range(2)]
            psC = bank(st, "a_psC")
            psR1 = bank(st, "a_psR1")
            psR2 = bank(st, "a_psR2")
            psS = bank(st, "a_psS")
            psP = bank(st, "a_psP")
            psO = bank(st, "a_psO")

            w_loaded = sem("a_w_loaded")
            wT_done = sem("a_wT_done")
            wT_ready = sem("a_wT_ready")
            ctx_loaded = [sem("a_ctx_loaded_even"), sem("a_ctx_loaded_odd")]
            ctxv_loaded = [sem("a_ctxv_loaded_even"), sem("a_ctxv_loaded_odd")]
            mask_loaded = [sem("a_mask_loaded_even"), sem("a_mask_loaded_odd")]
            mask_ready = sem("a_mask_ready")
            lnA = norm_sems("a_ln")
            normed = lnA[-1]
            xT_done = sem("a_xT_done")
            xT_ready = sem("a_xT_ready")
            cT_done = sem("a_cT_done")
            cT_ready = sem("a_cT_ready")
            r1_done = sem("a_r1_done")
            r1_ready = sem("a_r1_ready")
            r2_done = sem("a_r2_done")
            r2_ready = sem("a_r2_ready")
            s_done = sem("a_scores_done")
            s_masked = sem("a_scores_masked")
            max_ready = sem("a_max_ready")
            negmax_ready = sem("a_negmax_ready")
            p_ready = sem("a_probs_ready")
            inv_ready = sem("a_inv_ready")
            rg_ready = sem("a_gated_inv_ready")
            pT_done = sem("a_probsT_done")
            pT_ready = sem("a_probsT_ready")
            o_done = sem("a_out_done")
            x_ready = sem("a_x_ready")

            with nc.Block() as block:
                @block.sync
                def _(sp):
                    sp.dma_start(Wn[:, :], W).then_inc(w_loaded, 16)
                    sp.dma_start(diag[:, :], diagonal.rearrange("(h a) -> h a", a=1)).then_inc(w_loaded, 16)
                    sp.dma_start(graw[:, 0:2], g_xattn.partition_broadcast(P)).then_inc(gates_loaded, 16)
                    sp.dma_start(graw[:, 2:4], g_ffn.partition_broadcast(P)).then_inc(gates_loaded, 16)

                    def load(g, p, slot):
                        if later(g, 2):
                            sp.wait_ge(x_loaded[slot], 16 * p)
                            sp.wait_ge(cT_done, g - 1)
                            sp.wait_ge(mask_ready, g - 1)
                        b0 = g * GB
                        sp.dma_start(X[:, bass.ds(b0, GB), :], x[bass.ds(b0, GB), :, :].rearrange("b s d -> s b d"))\
                          .then_inc(x_loaded[slot], 16)
                        sp.dma_start(ctxs[:, slot, :, :],
                                     ctx_tokens[bass.ds(b0, GB), :, :].rearrange("b m d -> m b d"))\
                          .then_inc(ctx_loaded[slot], 16)
                        sp.dma_start(mski[:, slot, :].rearrange("p (b m) -> p b m", b=GB),
                                     mask[bass.ds(b0, GB), :].partition_broadcast(P)).then_inc(mask_loaded[slot], 16)

                    def prepare(p):
                        for slot in range(2):
                            load(2 * p + slot, p, slot)

                    def work(p, ahead):
                        for slot in range(2):
                            g = 2 * p + slot
                            if later(g, 2):
                                sp.wait_ge(ctxv_loaded[slot], 16 * p)
                                sp.wait_ge(o_done, g - 1)
                            sp.dma_start(ctxv[:, slot, :, :],
                                         ctx_tokens[bass.ds(g * GB, GB), :, :].rearrange("b m d -> m b d"))\
                              .then_inc(ctxv_loaded[slot], 16)
                        if ahead is not None:
                            prepare(ahead)

                    over_pairs(sp, PAIRS, prepare, work)

                @block.gpsimd
                def _(pool):
                    pool.memset(half_neg[:, :], -0.5).then_inc(const_filled, 1)
                    pool.memset(eps_tile[:, :], LN_EPS).then_inc(const_filled, 1)
                    pool.memset(ident[:, :], 0.0).then_inc(const_filled, 1)
                    pool.wait_ge(const_filled, 3)
                    pool.affine_select(out=ident[:, :], in_=ident[:, :], compare_op=ALU.not_equal, fill=1.0,
                                       base=0, pattern=[[-1, P]], channel_multiplier=1).then_inc(const_filled, 1)
                    pool.wait_ge(const_filled, 4)
                    pool.tensor_copy(ident_bf[:, :], ident[:, :]).then_inc(const_ready, 1)

                    def prepare(p):
                        for slot in range(2):
                            g = 2 * p + slot
                            norm_pool(pool, g, slot, ln, lnA)

                    def work(p, ahead):
                        if ahead is not None:
                            prepare(ahead)

                    over_pairs(pool, PAIRS, prepare, work)

                @block.tensor
                def _(pe):
                    pe.wait_ge(const_ready, 1)
                    pe.wait_ge(w_loaded, 32)
                    pe.transpose(psR1[:, 0:P], Wn[:, :], ident[:, :]).then_inc(wT_done, 1)

                    def transposes(g, p, slot):
                        pe.wait_ge(normed, g + 1)
                        if later(g, 2):
                            pe.wait_ge(xT_ready, g - 1)
                        for b in range(GB):
                            i = pe.transpose(psX[slot][:, b * P:(b + 1) * P], xn[:, slot, b, :], ident[:, :])
                        i.then_inc(xT_done, 1)
                        pe.wait_ge(ctx_loaded[slot], 16 * (p + 1))
                        if later(g, 1):
                            pe.wait_ge(cT_ready, g)
                        for b in range(GB):
                            i = pe.transpose(psC[:, b * M:(b + 1) * M], ctxs[:, slot, b, :], ident[0:M, 0:M])
                        i.then_inc(cT_done, 1)

                    def prepare(p):
                        for slot in range(2):
                            transposes(2 * p + slot, p, slot)

                    def work(p, ahead):
                        for slot in range(2):
                            g = 2 * p + slot
                            pe.wait_ge(xT_ready, g + 1)
                            if later(g, 1):
                                pe.wait_ge(r1_ready, g)
                            else:
                                pe.wait_ge(wT_ready, 1)
                            pe.matmul(psR1[:, :], WT[:, :], xT[:, slot, :], start=True, stop=True).then_inc(r1_done, 1)
                            pe.wait_ge(cT_ready, g + 1)
                            if later(g, 1):
                                pe.wait_ge(r2_ready, g)
                            pe.matmul(psR2[:, 0:GB * M], WT[:, :], cT[:, slot, :], start=True, stop=True)\
                              .then_inc(r2_done, 1)
                        for slot in range(2):
                            g = 2 * p + slot
                            pe.wait_ge(r1_ready, g + 1)
                            pe.wait_ge(r2_ready, g + 1)
                            if later(g, 1):
                                pe.wait_ge(s_masked, g)
                            for b in range(GB):
                                i = pe.matmul(psS[:, b * M:(b + 1) * M], r1[:, slot, b * P:(b + 1) * P],
                                              r2[:, slot, b * M:(b + 1) * M], start=True, stop=True)
                            i.then_inc(s_done, 1)
                        if ahead is not None:
                            prepare(ahead)
                        for slot in range(2):
                            g = 2 * p + slot
                            pe.wait_ge(p_ready, GB * (g + 1))
                            if later(g, 1):
                                pe.wait_ge(pT_ready, g)
                            for b in range(GB):
                                i = pe.transpose(psP[0:M, b * P:(b + 1) * P], pr[:, slot, b, :], ident[:, :])
                            i.then_inc(pT_done, 1)
                        for slot in range(2):
                            g = 2 * p + slot
                            pe.wait_ge(pT_ready, g + 1)
                            pe.wait_ge(ctxv_loaded[slot], 16 * (p + 1))
                            if later(g, 1):
                                pe.wait_ge(x_ready, g)
                            for b in range(GB):
                                i = pe.matmul(psO[:, b * P:(b + 1) * P], prT[:, slot, b * P:(b + 1) * P],
                                              ctxv[:, slot, b, :], start=True, stop=True)
                            i.then_inc(o_done, 1)

                    over_pairs(pe, PAIRS, prepare, work)

                @block.scalar
                def _(act):
                    act.wait_ge(gates_loaded, 32)
                    act.activation(gates[:, :], graw[:, :], ACT.Tanh).then_inc(gates_ready, 1)
                    act.wait_ge(wT_done, 1)
                    act.activation(WT[:, :], psR1[:, 0:P], ACT.Copy).then_inc(wT_ready, 1)

                    def prepare(p):
                        for slot in range(2):
                            g = 2 * p + slot
                            act.wait_ge(xT_done, g + 1)
                            if later(g, 2):
                                act.wait_ge(r1_done, g - 1)
                            act.activation(xT[:, slot, :], psX[slot][:, :], ACT.Copy).then_inc(xT_ready, 1)
                            act.wait_ge(cT_done, g + 1)
                            if later(g, 2):
                                act.wait_ge(r2_done, g - 1)
                            act.activation(cT[:, slot, :], psC[:, 0:GB * M], ACT.Copy).then_inc(cT_ready, 1)
                            act.wait_ge(mask_loaded[slot], 16 * (p + 1))
                            if later(g, 2):
                                act.wait_ge(s_masked, g - 1)
                            act.activation(mskf[:, slot, :], mski[:, slot, :], ACT.Copy, scale=-1.0, bias=1.0)\
                               .then_inc(mask_ready, 1)

                    def work(p, ahead):
                        for slot in range(2):
                            g = 2 * p + slot
                            act.wait_ge(r1_done, g + 1)
                            if later(g, 2):
                                act.wait_ge(s_done, g - 1)
                            act.activation(r1[:, slot, :], psR1[:, :], ACT.Relu).then_inc(r1_ready, 1)
                        if ahead is not None:
                            prepare(ahead)
                        for slot in range(2):
                            g = 2 * p + slot
                            act.wait_ge(negmax_ready, g + 1)
                            if later(g, 2):
                                act.wait_ge(pT_done, g - 1)
                                act.wait_ge(inv_ready, g - 1)
                            for b in range(GB):
                                act.activation(pr[:, slot, b, :], sc[:, slot, b, :], ACT.Exp,
                                               bias=mx[:, slot, b:b + 1], accum_out=sm[:, slot, b:b + 1])\
                                   .then_inc(p_ready, 1)
                        for slot in range(2):
                            g = 2 * p + slot
                            act.wait_ge(pT_done, g + 1)
                            if later(g, 2):
                                act.wait_ge(o_done, g - 1)
                            act.activation(prT[:, slot, :], psP[0:M, :], ACT.Copy).then_inc(pT_ready, 1)

                    over_pairs(act, PAIRS, prepare, work)

                @block.vector
                def _(v):
                    def prepare(p):
                        for slot in range(2):
                            g = 2 * p + slot
                            src = lambda b: X[:, bass.ds(g * GB + b, 1), :].rearrange("p a d -> p (a d)")
                            dst = lambda b: xn[:, slot, b, :]
                            v.wait_ge(x_loaded[slot], 16 * (p + 1))
                            norm_moments(v, g, slot, src, ln, lnA)
                        for slot in range(2):
                            g = 2 * p + slot
                            src = lambda b: X[:, bass.ds(g * GB + b, 1), :].rearrange("p a d -> p (a d)")
                            dst = lambda b: xn[:, slot, b, :]
                            if later(g, 2):
                                v.wait_ge(xT_done, g - 1)
                            norm_apply(v, g, slot, src, dst, ln, lnA)

                    def work(p, ahead):
                        for slot in range(2):
                            g = 2 * p + slot
                            v.wait_ge(r2_done, g + 1)
                            if later(g, 2):
                                v.wait_ge(s_done, g - 1)
                            v.tensor_scalar(r2[:, slot, :], psR2[:, 0:GB * M], 0.0, diag[:, 0:1], ALU.max, ALU.mult)\
                             .then_inc(r2_ready, 1)
                        for slot in range(2):
                            g = 2 * p + slot
                            v.wait_ge(s_done, g + 1)
                            v.wait_ge(mask_ready, g + 1)
                            if later(g, 2):
                                v.wait_ge(p_ready, GB * (g - 1))
                            v.scalar_tensor_tensor(out=sc[:, slot, :, :].rearrange("p b m -> p (b m)"),
                                                   in0=mskf[:, slot, :], scalar=NEG, in1=psS[:, 0:GB * M],
                                                   op0=ALU.mult, op1=ALU.add).then_inc(s_masked, 1)
                            v.wait_ge(s_masked, g + 1)
                            v.tensor_reduce(mx[:, slot, :], sc[:, slot, :, :], AX.X, ALU.max, negate=True)\
                             .then_inc(negmax_ready, 1)
                        if ahead is not None:
                            prepare(ahead)
                        for slot in range(2):
                            g = 2 * p + slot
                            v.wait_ge(p_ready, GB * (g + 1))
                            v.reciprocal(ri[:, slot, :], sm[:, slot, :]).then_inc(inv_ready, 1)
                            v.wait_ge(inv_ready, g + 1)
                            if not later(g, 1):
                                v.wait_ge(gates_ready, 1)
                            v.tensor_scalar(rg[:, slot, :], ri[:, slot, :], gates[:, 0:1], None, ALU.mult)\
                             .then_inc(rg_ready, 1)
                        for slot in range(2):
                            g = 2 * p + slot
                            v.wait_ge(o_done, g + 1)
                            v.wait_ge(rg_ready, g + 1)
                            for b in range(GB):
                                xb = X[:, bass.ds(g * GB + b, 1), :].rearrange("p a d -> p (a d)")
                                i = v.scalar_tensor_tensor(out=xb, in0=psO[:, b * P:(b + 1) * P],
                                                           scalar=rg[:, slot, b:b + 1], in1=xb,
                                                           op0=ALU.mult, op1=ALU.add)
                            i.then_inc(x_ready, 1)

                    over_pairs(v, PAIRS, prepare, work)
        end_phase()

        with ExitStack() as st:
            E, _, INTER = wg.shape
            SH = swg.shape[1]
            EH = E * INTER
            ET = EH // P
            ST = -(-SH // P)
            NT = ST + ET
            assert EH == ET * P and NT % 2 == 0
            rows = [min(P, SH - j * P) for j in range(ST)] + [P] * ET
            HS = NT // 2
            VECTOR_LOW = (8, 9, 10)
            POOL_LOW = [j for j in range(NT) if j not in VECTOR_LOW]
            LAG = 4
            DOWN_PARTS = [(slice(0, ST - 1), P), (slice(ST - 1, ST), rows[ST - 1]), (slice(ST, NT), P)]
            PARTS = 3

            wn = sb(st, "wn", [P, 2, NT * P])
            wh = sb(st, "wh", [P, 2, NT * P], F32R)
            wl = sb(st, "wl", [P, 2, NT * P], F32R)
            dn = sb(st, "dn", [P, NT, D])
            dh = sb(st, "dh", [P, NT, D], F32R)
            dl = sb(st, "dl", [P, NT, D], F32R)
            gwn = sb(st, "gwn", [E, D])
            gwh = sb(st, "gwh", [P, P], F32R)
            gwl = sb(st, "gwl", [P, P], F32R)
            gwz = sb(st, "gwz", [P, P])
            seln = sb(st, "seln", [PARTS * E, EH])
            sel = sb(st, "sel", [PARTS * E, EH], BF16)
            ramp = sb(st, "ramp", [P, E])
            ebase = sb(st, "ebase", [P, E])

            xn = sb(st, "b_xn", [P, GB, D])
            xh = sb(st, "b_xh", [P, 2, GT], F32R)
            xl = sb(st, "b_xl", [P, 2, GT], F32R)
            lgT = sb(st, "b_lgT", [P, GT])
            lg = sb(st, "b_lg", [P, GB, E])
            m1 = sb(st, "b_m1", [P, GB])
            dif = sb(st, "b_dif", [P, GB, E])
            f1 = sb(st, "b_f1", [P, GB, E])
            q1 = sb(st, "b_q1", [P, GB])
            k1 = sb(st, "b_k1", [P, GB, E])
            d2 = sb(st, "b_d2", [P, GB, E])
            m2 = sb(st, "b_m2", [P, GB])
            e2 = sb(st, "b_e2", [P, GB, E])
            f2 = sb(st, "b_f2", [P, GB, E])
            q2 = sb(st, "b_q2", [P, GB])
            k2 = sb(st, "b_k2", [P, GB, E])
            kk = sb(st, "b_kk", [P, GB, E])
            ex = sb(st, "b_ex", [P, GB, E])
            em = sb(st, "b_em", [P, GB, E])
            se = sb(st, "b_se", [P, GB])
            sz = sb(st, "b_sz", [P, GB])
            den = sb(st, "b_den", [P, GB])
            rd = sb(st, "b_rd", [P, GB])
            wt = sb(st, "b_wt", [P, GB, E])
            wr = sb(st, "b_wr", [P, GB, E])
            w3 = sb(st, "b_w3", [P, GB, PARTS, E], BF16)
            w3T = sb(st, "b_w3T", [PARTS * E, 2, GT], BF16)
            sg = sb(st, "b_sg", [P, 2, GT])
            mu = sb(st, "b_mu", [P, HS, GT])
            hf = sb(st, "b_hf", [P, HS, GT])
            hh = sb(st, "b_hh", [P, HS, GT], F32R)
            hl = sb(st, "b_hl", [P, HS, GT], F32R)
            ysb = sb(st, "b_ysb", [P, GT])
            ln = norm_tiles(st, "lnB")

            psG = [bank(st, f"b_psG{s}") for s in range(2)]
            psU = [bank(st, f"b_psU{s}") for s in range(2)]
            psW = bank(st, "b_psW")
            psY = bank(st, "b_psY")
            psT = bank(st, "b_psT")
            psL = bank(st, "b_psL")
            psW3 = psL[:, 256:512].bitcast(BF16)

            up_loaded = sem("b_up_loaded")
            down_loaded = sem("b_down_loaded")
            router_loaded = sem("b_router_loaded")
            sel_loaded = sem("b_sel_loaded")
            uph_ready = sem("b_up_upper_ready")
            upl_ready = sem("b_up_lower_ready")
            dnh_ready = sem("b_down_upper_ready")
            dnl_ready = sem("b_down_lower_ready")
            gwT_done = sem("b_gwT_done")
            gwz_ready = sem("b_gwz_ready")
            gwh_ready = sem("b_gwh_ready")
            gwl_ready = sem("b_gwl_ready")
            sel_ready = sem("b_sel_ready")
            ebase_ready = sem("b_ebase_ready")
            lnB = norm_sems("b_ln")
            normed = lnB[-1]
            xT_done = sem("b_xT_done")
            xh_ready = sem("b_xh_ready")
            xl_ready = sem("b_xl_ready")
            lgT_done = sem("b_logitsT_done")
            lgT_ready = sem("b_logitsT_ready")
            lg_done = sem("b_logits_done")
            dif_ready = sem("b_dif_ready")
            ex_ready = sem("b_exp_ready")
            pick = sem("b_pick_step")
            split_step = sem("b_split_step")
            w3_ready = sem("b_w3_ready")
            w3T_done = sem("b_w3T_done")
            w3T_ready = sem("b_w3T_ready")
            g_done = sem("b_gate_done")
            u_done = sem("b_up_done")
            wb_done = sem("b_weight_done")
            sg_ready = sem("b_silu_ready")
            mu_ready = sem("b_mul_ready")
            hf_ready = sem("b_hidden_ready")
            hh_ready = sem("b_hidden_upper_ready")
            hlp_ready = sem("b_hidden_lower_pool_ready")
            hlv_ready = sem("b_hidden_lower_vector_ready")
            dn_done = sem("b_down_done")
            y_ready = sem("b_y_ready")
            yb_done = sem("b_y_back_done")
            x_ready = sem("b_x_ready")

            def wait_split(eng, g, j):
                if j in VECTOR_LOW:
                    eng.wait_ge(hlv_ready, len(VECTOR_LOW) * g + VECTOR_LOW.index(j) + 1)
                else:
                    eng.wait_ge(hlp_ready, len(POOL_LOW) * g + POOL_LOW.index(j) + 1)

            def wait_slot_split(eng, g, j):
                if j >= HS:
                    wait_split(eng, g, j - HS)
                elif later(g, 1):
                    wait_split(eng, g - 1, j + HS)

            def lower(eng, g, j, ready):
                n, m, q = NT * g + j, rows[j], j % HS
                eng.wait_ge(hh_ready, n + 1)
                if j >= HS or later(g, 1):
                    eng.wait_ge(dn_done, n - HS + 1)
                eng.tensor_tensor(hl[0:m, q, :], hf[0:m, q, :], hh[0:m, q, :].bitcast(F32),
                                  ALU.subtract).then_inc(ready, 1)

            def over_groups(eng, prep, group, tail):
                def prepare(p):
                    prep(0)

                def work(p, ahead):
                    group(2 * p, 0, 2 * p + 1, 1)
                    group(2 * p + 1, 1, None if ahead is None else 2 * ahead, 0)

                over_pairs(eng, PAIRS, prepare, work)
                tail()

            with nc.Block() as block:
                @block.sync
                def _(sp):
                    sp.dma_start(gwn[:, :], gate_w).then_inc(router_loaded, 16)
                    sp.dma_start(ramp[:, :], ramp_const.partition_broadcast(P)).then_inc(router_loaded, 16)
                    sp.dma_start(seln[:, :], sel_const).then_inc(sel_loaded, 16)
                    for k, (we, ws) in enumerate(((wg, swg), (wu, swu))):
                        sp.dma_start(wn[:, k, ST * P:NT * P].rearrange("h (e i) -> h e i", e=E),
                                     we.rearrange("e h i -> h e i")).then_inc(up_loaded, 16)
                        sp.dma_start(wn[:, k, 0:SH], ws).then_inc(up_loaded, 16)
                    full = SH // P
                    sp.dma_start(dn[:, 0:full, :], swd[0:full * P, :].rearrange("(j p) d -> p j d", p=P))\
                      .then_inc(down_loaded, 16)
                    sp.dma_start(dn[0:SH - full * P, full, :], swd[full * P:SH, :]).then_inc(down_loaded, 16)
                    sp.dma_start(dn[:, ST:NT, :], wd.rearrange("e i d -> (e i) d").rearrange("(j p) d -> p j d", p=P))\
                      .then_inc(down_loaded, 16)

                @block.tensor
                def _(pe):
                    pe.wait_ge(router_loaded, 32)
                    pe.transpose(psL[:, 0:E], gwn[:, :], ident[0:E, 0:E]).then_inc(gwT_done, 1)

                    def x_transposes(g):
                        pe.wait_ge(normed, g + 1)
                        if later(g, 1):
                            pe.wait_ge(xl_ready, g)
                        if later(g, 3):
                            pe.wait_ge(x_ready, g - 2)
                        for b in range(GB):
                            i = pe.transpose(psT[:, b * P:(b + 1) * P], xn[:, b, :], ident[:, :])
                        i.then_inc(xT_done, 1)

                    def logits(g, slot):
                        if not later(g, 1):
                            pe.wait_ge(gwh_ready, 1)
                            pe.wait_ge(gwl_ready, 1)
                        pe.wait_ge(xh_ready, g + 1)
                        pe.wait_ge(xl_ready, g + 1)
                        if later(g, 1):
                            pe.wait_ge(w3T_ready, g)
                        pe.matmul(psL[:, :], gwh[:, :], xl[:, slot, :], start=True, stop=False)
                        pe.matmul(psL[:, :], gwl[:, :], xh[:, slot, :], start=False, stop=False)
                        pe.matmul(psL[:, :], gwh[:, :], xh[:, slot, :], start=False, stop=True).then_inc(lgT_done, 1)

                    def logits_back(g):
                        pe.wait_ge(lgT_ready, g + 1)
                        for b in range(GB):
                            i = pe.transpose(psL[:, b * P:(b + 1) * P], lgT[:, b * P:(b + 1) * P], ident[:, :])
                        i.then_inc(lg_done, 1)

                    def weight_transposes(g):
                        pe.wait_ge(w3_ready, g + 1)
                        for b in range(GB):
                            i = pe.transpose(psW3[0:PARTS * E, b * P:(b + 1) * P],
                                             w3[:, b, :, :].rearrange("p a e -> p (a e)"), ident_bf[:, :])
                        i.then_inc(w3T_done, 1)

                    def prep(g):
                        x_transposes(g)
                        logits(g, 0)
                        logits_back(g)
                        weight_transposes(g)

                    def spread(g, j, slot):
                        e = j - ST
                        if e == 0:
                            pe.wait_ge(w3T_ready, g + 1)
                            if not later(g, 1):
                                pe.wait_ge(sel_ready, 1)
                        if e > 0 or later(g, 1):
                            pe.wait_ge(hf_ready, ET * g + e)
                        pe.matmul(psW[:, :], sel[:, e * P:(e + 1) * P], w3T[:, slot, :],
                                  start=True, stop=True).then_inc(wb_done, 1)

                    def down(g, j):
                        n, m, q = NT * g + j, rows[j], j % HS
                        pe.wait_ge(hh_ready, n + 1)
                        wait_split(pe, g, j)
                        if j == 0:
                            if later(g, 1):
                                pe.wait_ge(y_ready, g)
                            else:
                                pe.wait_ge(dnl_ready, 1)
                        pe.matmul(psY[:, :], dh[0:m, j, :], hl[0:m, q, :], start=(j == 0), stop=False)
                        pe.matmul(psY[:, :], dl[0:m, j, :], hh[0:m, q, :], start=False, stop=False)
                        pe.matmul(psY[:, :], dh[0:m, j, :], hh[0:m, q, :], start=False, stop=(j == NT - 1))\
                          .then_inc(dn_done, 1)

                    def y_back(g, bank_free, count):
                        pe.wait_ge(y_ready, g + 1)
                        pe.wait_ge(bank_free, count)
                        for b in range(GB):
                            i = pe.transpose(psT[:, b * P:(b + 1) * P], ysb[:, b * P:(b + 1) * P], ident[:, :])
                        i.then_inc(yb_done, 1)

                    def group(g, slot, nxt, nslot):
                        for j in range(NT):
                            n, m = NT * g + j, rows[j]
                            cols = slice(j * P, j * P + m)
                            if j == 0:
                                pe.wait_ge(xh_ready, g + 1)
                                pe.wait_ge(xl_ready, g + 1)
                            if not later(g, 1):
                                pe.wait_ge(uph_ready, j + 1)
                                pe.wait_ge(upl_ready, j + 1)
                            if j >= 2 or later(g, 1):
                                pe.wait_ge(sg_ready, n - 1)
                            for k, ps in enumerate((psG[j % 2], psU[j % 2])):
                                if k == 1 and (j >= 2 or later(g, 1)):
                                    pe.wait_ge(mu_ready, n - 1)
                                pe.matmul(ps[0:m, :], wh[:, k, cols], xl[:, slot, :], start=True, stop=False)
                                pe.matmul(ps[0:m, :], wl[:, k, cols], xh[:, slot, :], start=False, stop=False)
                                pe.matmul(ps[0:m, :], wh[:, k, cols], xh[:, slot, :], start=False, stop=True)\
                                  .then_inc((g_done, u_done)[k], 1)
                            if j > ST:
                                spread(g, j - 1, slot)
                            elif j == 0 and later(g, 1):
                                spread(g - 1, NT - 1, 1 - slot)
                            if j >= LAG:
                                down(g, j - LAG)
                            elif later(g, 1):
                                down(g - 1, NT - LAG + j)
                            if j == 3 and later(g, 1):
                                weight_transposes(g)
                            if j == 5 and nxt is not None:
                                x_transposes(nxt)
                            if j == 7 and later(g, 1):
                                if nxt is None:
                                    y_back(g - 1, x_ready, g - 1)
                                else:
                                    y_back(g - 1, xl_ready, g + 2)
                            if nxt is not None:
                                if j == 7:
                                    logits(nxt, nslot)
                                if j == 8:
                                    logits_back(nxt)

                    def tail():
                        spread(NG - 1, NT - 1, 1)
                        for j in range(NT - LAG, NT):
                            down(NG - 1, j)
                        y_back(NG - 1, x_ready, NG - 1)

                    over_groups(pe, prep, group, tail)

                @block.scalar
                def _(act):
                    act.wait_ge(gwz_ready, 2)
                    act.activation(gwh[:, :], gwz[:, :], ACT.Copy).then_inc(gwh_ready, 1)
                    act.wait_ge(up_loaded, 64)
                    for j in range(NT):
                        cols = slice(j * P, j * P + rows[j])
                        act.activation(wh[:, :, cols], wn[:, :, cols], ACT.Copy).then_inc(uph_ready, 1)
                    act.wait_ge(down_loaded, 48)
                    for tiles, m in DOWN_PARTS:
                        i = act.activation(dh[0:m, tiles, :], dn[0:m, tiles, :], ACT.Copy)
                    i.then_inc(dnh_ready, 1)

                    def x_upper(g, slot):
                        act.wait_ge(xT_done, g + 1)
                        if later(g, 2):
                            act.wait_ge(u_done, NT * (g - 1))
                        act.activation(xh[:, slot, :], psT[:, :], ACT.Copy).then_inc(xh_ready, 1)

                    def logits_copy(g):
                        act.wait_ge(lgT_done, g + 1)
                        act.activation(lgT[:, :], psL[:, :], ACT.Copy).then_inc(lgT_ready, 1)

                    def weights_copy(g, slot):
                        act.wait_ge(w3T_done, g + 1)
                        if later(g, 2):
                            act.wait_ge(wb_done, ET * (g - 1))
                        act.activation(w3T[:, slot, :], psW3[0:PARTS * E, :], ACT.Copy).then_inc(w3T_ready, 1)

                    def prep(g):
                        x_upper(g, 0)
                        logits_copy(g)
                        weights_copy(g, 0)

                    def upper(g, j):
                        n, m, q = NT * g + j, rows[j], j % HS
                        if j < ST:
                            act.wait_ge(mu_ready, n + 1)
                        else:
                            act.wait_ge(hf_ready, ET * g + j - ST + 1)
                        if j >= HS or later(g, 1):
                            act.wait_ge(dn_done, n - HS + 1)
                        act.activation(hh[0:m, q, :], hf[0:m, q, :], ACT.Copy).then_inc(hh_ready, 1)

                    def y_copy(g):
                        act.wait_ge(dn_done, NT * (g + 1))
                        if later(g, 1):
                            act.wait_ge(yb_done, g)
                        act.activation(ysb[:, :], psY[:, :], ACT.Copy, scale=gates[:, 2:3]).then_inc(y_ready, 1)

                    def group(g, slot, nxt, nslot):
                        for j in range(NT):
                            n, m = NT * g + j, rows[j]
                            act.wait_ge(g_done, n + 1)
                            if j >= 2 or later(g, 1):
                                act.wait_ge(mu_ready, n - 1)
                            act.activation(sg[0:m, j % 2, :], psG[j % 2][0:m, :], ACT.Silu).then_inc(sg_ready, 1)
                            if j >= 2:
                                upper(g, j - 2)
                            elif later(g, 1):
                                upper(g - 1, NT - 2 + j)
                            if j == 3 and later(g, 1):
                                weights_copy(g, slot)
                            if j == 3 and later(g, 1):
                                y_copy(g - 1)
                            if nxt is not None:
                                if j == 5:
                                    x_upper(nxt, nslot)
                                if j == 7:
                                    logits_copy(nxt)

                    def tail():
                        upper(NG - 1, NT - 2)
                        upper(NG - 1, NT - 1)
                        y_copy(NG - 1)

                    over_groups(act, prep, group, tail)

                @block.gpsimd
                def _(pool):
                    pool.memset(ebase[:, :], math.e).then_inc(ebase_ready, 1)
                    pool.wait_ge(sel_loaded, 16)
                    pool.tensor_copy(sel[:, :], seln[:, :]).then_inc(sel_ready, 1)

                    EXP_STEPS = (7, 8, 9, 10)

                    def exps(g, b):
                        if b == 0:
                            pool.wait_ge(dif_ready, g + 1)
                            if later(g, 1):
                                pool.wait_ge(w3_ready, g)
                        pool.tensor_tensor(ex[:, b, :], ebase[:, :], dif[:, b, :], ALU.pow).then_inc(ex_ready, 1)

                    def prep(g):
                        pool.wait_ge(ebase_ready, 1)
                        norm_pool(pool, g, 0, ln, lnB)
                        for b in range(GB):
                            exps(g, b)

                    def group(g, slot, nxt, nslot):
                        for j in range(NT):
                            if j in POOL_LOW:
                                lower(pool, g, j, hlp_ready)
                            if nxt is not None:
                                if j == 0:
                                    norm_pool(pool, nxt, nslot, ln, lnB)
                                for b in range(GB):
                                    if j == EXP_STEPS[b]:
                                        exps(nxt, b)

                    over_groups(pool, prep, group, lambda: None)

                @block.vector
                def _(v):
                    v.memset(gwz[:, :], 0.0).then_inc(gwz_ready, 1)
                    v.wait_ge(gwz_ready, 1)
                    v.wait_ge(gwT_done, 1)
                    v.tensor_copy(gwz[:, 0:E], psL[:, 0:E]).then_inc(gwz_ready, 1)
                    v.wait_ge(gwh_ready, 1)
                    v.tensor_tensor(gwl[:, :], gwz[:, :], gwh[:, :].bitcast(F32), ALU.subtract).then_inc(gwl_ready, 1)

                    def x_of(g, b):
                        return X[:, bass.ds(g * GB + b, 1), :].rearrange("p a d -> p (a d)")

                    def moments(g, slot):
                        norm_moments(v, g, slot, lambda b: x_of(g, b), ln, lnB)

                    def apply(g, slot):
                        if later(g, 1):
                            v.wait_ge(xT_done, g)
                        norm_apply(v, g, slot, lambda b: x_of(g, b), lambda b: xn[:, b, :], ln, lnB)

                    def x_lower(g, slot):
                        v.wait_ge(xh_ready, g + 1)
                        if later(g, 2):
                            v.wait_ge(u_done, NT * (g - 1))
                        v.tensor_tensor(xl[:, slot, :], psT[:, :], xh[:, slot, :].bitcast(F32), ALU.subtract)\
                         .then_inc(xl_ready, 1)

                    def wide(t):
                        return t[:, :].unsqueeze(2).broadcast_to([P, GB, E])

                    ramp4 = ramp[:, :].unsqueeze(1).broadcast_to([P, GB, E])
                    STEPS = 18

                    def differences(g):
                        v.wait_ge(lg_done, g + 1)
                        v.tensor_copy(lg[:, :, :], psL[:, :].rearrange("p (b e) -> p b e", b=GB)[:, :, 0:E])\
                         .then_inc(pick, 1)
                        v.wait_ge(pick, STEPS * g + 1)
                        v.tensor_reduce(m1[:, :], lg[:, :, :], AX.X, ALU.max).then_inc(pick, 1)
                        v.wait_ge(pick, STEPS * g + 2)
                        if later(g, 1):
                            v.wait_ge(ex_ready, GB * g)
                        v.tensor_tensor(dif[:, :, :], lg[:, :, :], wide(m1), ALU.subtract).then_inc(dif_ready, 1)

                    def pick_two(g):
                        v.wait_ge(dif_ready, g + 1)
                        v.scalar_tensor_tensor(out=f1[:, :, :], in0=dif[:, :, :], scalar=0.0, in1=ramp4,
                                               op0=ALU.is_equal, op1=ALU.mult).then_inc(pick, 1)
                        v.wait_ge(pick, STEPS * g + 3)
                        v.tensor_reduce(q1[:, :], f1[:, :, :], AX.X, ALU.max).then_inc(pick, 1)
                        v.wait_ge(pick, STEPS * g + 4)
                        v.tensor_tensor(k1[:, :, :], f1[:, :, :], wide(q1), ALU.is_equal).then_inc(pick, 1)
                        v.wait_ge(pick, STEPS * g + 5)
                        v.scalar_tensor_tensor(out=d2[:, :, :], in0=k1[:, :, :], scalar=-3e38, in1=dif[:, :, :],
                                               op0=ALU.mult, op1=ALU.add).then_inc(pick, 1)
                        v.wait_ge(pick, STEPS * g + 6)
                        v.tensor_reduce(m2[:, :], d2[:, :, :], AX.X, ALU.max).then_inc(pick, 1)
                        v.wait_ge(pick, STEPS * g + 7)
                        v.tensor_tensor(e2[:, :, :], d2[:, :, :], wide(m2), ALU.is_equal).then_inc(pick, 1)
                        v.wait_ge(pick, STEPS * g + 8)
                        v.tensor_tensor(f2[:, :, :], e2[:, :, :], ramp4, ALU.mult).then_inc(pick, 1)
                        v.wait_ge(pick, STEPS * g + 9)
                        v.tensor_reduce(q2[:, :], f2[:, :, :], AX.X, ALU.max).then_inc(pick, 1)
                        v.wait_ge(pick, STEPS * g + 10)
                        v.tensor_tensor(k2[:, :, :], f2[:, :, :], wide(q2), ALU.is_equal).then_inc(pick, 1)
                        v.wait_ge(pick, STEPS * g + 11)
                        v.tensor_tensor(kk[:, :, :], k1[:, :, :], k2[:, :, :], ALU.add).then_inc(pick, 1)

                    def routing(g):
                        v.wait_ge(ex_ready, GB * (g + 1))
                        v.wait_ge(pick, STEPS * g + 12)
                        v.tensor_tensor(em[:, :, :], ex[:, :, :], kk[:, :, :], ALU.mult)
                        v.tensor_reduce(sz[:, :], ex[:, :, :], AX.X, ALU.add).then_inc(pick, 1)
                        v.wait_ge(pick, STEPS * g + 13)
                        v.tensor_reduce(se[:, :], em[:, :, :], AX.X, ALU.add).then_inc(pick, 1)
                        v.wait_ge(pick, STEPS * g + 14)
                        v.scalar_tensor_tensor(out=den[:, :], in0=sz[:, :], scalar=1e-20, in1=se[:, :],
                                               op0=ALU.mult, op1=ALU.add).then_inc(pick, 1)
                        v.wait_ge(pick, STEPS * g + 15)
                        v.reciprocal(rd[:, :], den[:, :]).then_inc(pick, 1)
                        v.wait_ge(pick, STEPS * g + 16)
                        v.tensor_tensor(wt[:, :, :], em[:, :, :], wide(rd), ALU.mult).then_inc(pick, 1)
                        v.wait_ge(pick, STEPS * g + 17)
                        if later(g, 1):
                            v.wait_ge(w3T_done, g)
                        v.tensor_copy(w3[:, :, 0, :], wt[:, :, :]).then_inc(pick, 1)
                        v.wait_ge(pick, STEPS * g + 18)

                    def routing_parts(g):
                        v.tensor_tensor(wr[:, :, :], wt[:, :, :], w3[:, :, 0, :], ALU.subtract).then_inc(split_step, 1)
                        v.wait_ge(split_step, 2 * g + 1)
                        v.tensor_copy(w3[:, :, 1, :], wr[:, :, :]).then_inc(split_step, 1)
                        v.wait_ge(split_step, 2 * g + 2)
                        v.tensor_tensor(w3[:, :, 2, :], wr[:, :, :], w3[:, :, 1, :], ALU.subtract).then_inc(w3_ready, 1)

                    def prep(g):
                        moments(g, 0)
                        apply(g, 0)
                        x_lower(g, 0)
                        differences(g)
                        pick_two(g)
                        routing(g)
                        routing_parts(g)
                        v.wait_ge(uph_ready, 1)
                        for j in range(NT):
                            cols = slice(j * P, j * P + rows[j])
                            v.wait_ge(uph_ready, j + 1)
                            v.tensor_tensor(wl[:, :, cols], wn[:, :, cols], wh[:, :, cols].bitcast(F32),
                                            ALU.subtract).then_inc(upl_ready, 1)
                        v.wait_ge(dnh_ready, 1)
                        for tiles, m in DOWN_PARTS:
                            i = v.tensor_tensor(dl[0:m, tiles, :], dn[0:m, tiles, :], dh[0:m, tiles, :].bitcast(F32),
                                                ALU.subtract)
                        i.then_inc(dnl_ready, 1)

                    def add_y(g):
                        v.wait_ge(yb_done, g + 1)
                        xg = X[:, bass.ds(g * GB, GB), :].rearrange("p b d -> p (b d)")
                        v.tensor_tensor(xg, psT[:, :], xg, ALU.add).then_inc(x_ready, 1)

                    def weighted(g, j):
                        n, e, q = NT * g + j, ET * g + j - ST, j % HS
                        v.wait_ge(mu_ready, n + 1)
                        v.wait_ge(wb_done, e + 1)
                        wait_slot_split(v, g, j)
                        v.tensor_tensor(hf[:, q, :], psW[:, :], mu[:, q, :], ALU.mult).then_inc(hf_ready, 1)

                    def group(g, slot, nxt, nslot):
                        for j in range(NT):
                            n, m, q = NT * g + j, rows[j], j % HS
                            v.wait_ge(u_done, n + 1)
                            v.wait_ge(sg_ready, n + 1)
                            if j < ST:
                                wait_slot_split(v, g, j)
                            elif j >= ST + HS:
                                v.wait_ge(hf_ready, ET * g + j - ST - HS + 1)
                            elif j >= ST and later(g, 1):
                                v.wait_ge(hf_ready, ET * g + j - HS + 1)
                            v.tensor_tensor((hf if j < ST else mu)[0:m, q, :],
                                            psU[j % 2][0:m, :], sg[0:m, j % 2, :], ALU.mult).then_inc(mu_ready, 1)
                            if j > ST:
                                weighted(g, j - 1)
                            elif j == 0 and later(g, 1):
                                weighted(g - 1, NT - 1)
                            if later(g, 1):
                                if j == 1:
                                    routing(g)
                                    routing_parts(g)
                                if j == 8:
                                    add_y(g - 1)
                            if nxt is not None:
                                if j == 1:
                                    moments(nxt, nslot)
                                if j == 4:
                                    apply(nxt, nslot)
                                if j == 5:
                                    x_lower(nxt, nslot)
                                if j == 9:
                                    differences(nxt)
                                if j == 10:
                                    pick_two(nxt)
                            if j - 3 in VECTOR_LOW:
                                lower(v, g, j - 3, hlv_ready)

                    def tail():
                        weighted(NG - 1, NT - 1)
                        add_y(NG - 1)

                    over_groups(v, prep, group, tail)

        end_phase()

        with ExitStack() as st:
            H = 8
            HD = D // H
            HM = H * M
            HB = HM // 2
            FT = lin1_w.shape[0] // P
            VW = H * (P + HD)
            Q_SCALE = HD ** -0.5

            nat = sb(st, "c_nat", [P, 6, D])
            l1n = sb(st, "c_l1n", [P, FT, D])
            l2n = sb(st, "c_l2n", [P, FT * P])
            tr = sb(st, "c_tr", [P, 6, D])
            l1T = sb(st, "c_l1T", [P, FT, P])
            l1g = sb(st, "c_l1g", [P, FT, P])
            l2T = sb(st, "c_l2T", [P, FT, P])
            qg = sb(st, "c_qg", [P, D])
            m1t = sb(st, "c_m1t", [P, D])
            cols = sb(st, "c_cols", [P, 7])
            l2b = sb(st, "c_ln2b", [P, 1])
            l1b = sb(st, "c_l1b", [P, FT])
            rows_bc = sb(st, "c_rows", [P, 9, D])
            bvb = sb(st, "c_bvb", [P, 2, P])
            y1b = sb(st, "c_y1b", [P, D])
            r1b = sb(st, "c_r1b", [P, D])
            r1b0 = sb(st, "c_r1b0", [P, D])
            r2b = sb(st, "c_r2b", [P, D])
            g3 = sb(st, "c_g3", [P, D])
            b3 = sb(st, "c_b3", [P, D])
            bq2 = sb(st, "c_bq2", [P, 1])
            bq3 = sb(st, "c_bq3", [P, 1])
            l1b2 = sb(st, "c_l1b2", [P, FT])
            SAO, MHO, L1B, G1, B1, G2, B2, L2B = range(8)

            ctxs = sb(st, "c_ctxs", [M, 2, GB, D])
            xn = sb(st, "c_xn", [P, GB, D])
            xT = sb(st, "c_xT", [P, GT])
            y1 = sb(st, "c_y1", [P, GB, D])
            n1 = sb(st, "c_n1", [P, GB, D])
            n1T = sb(st, "c_n1T", [P, GT])
            r1t = sb(st, "c_r1t", [P, GB, D])
            r1 = sb(st, "c_r1", [P, 2, GB, D])
            cT = sb(st, "c_cT", [P, GB * M])
            qT = sb(st, "c_qT", [P, 2, GT])
            kT = sb(st, "c_kT", [P, GB * M])
            kbd = sb(st, "c_kbd", [P, 2, GB, HM])
            vp = sb(st, "c_vp", [M, 2, GB, VW])
            sc = sb(st, "c_sc", [P, 2, H, M])
            mx = sb(st, "c_mx", [P, 2, H])
            pr = sb(st, "c_pr", [P, 2, H, M])
            sm = sb(st, "c_sm", [P, 2, H])
            iv = sb(st, "c_iv", [P, 2, H])
            pn = sb(st, "c_pn", [P, 2, H, M])
            pT = sb(st, "c_pT", [M, 2, H, P])
            ca = sb(st, "c_ca", [P, 2, GT])
            y2 = sb(st, "c_y2", [P, GB, D])
            n2 = sb(st, "c_n2", [P, GB, D])
            n2T = sb(st, "c_n2T", [P, GT])
            r2t = sb(st, "c_r2t", [P, GB, D])
            r2 = sb(st, "c_r2", [P, GB, D])
            hT = sb(st, "c_hT", [P, FT, GT])
            y3 = sb(st, "c_y3", [P, GB, D])
            n3 = sb(st, "c_n3", [P, GB, D])
            o3 = sb(st, "c_o3", [P, GB, D])
            o3b = sb(st, "c_o3b", [P, GB, D])
            lns = [norm_tiles(st, f"c_ln{i}") for i in range(4)]

            psS = st.enter_context(nc.psum_tensor("c_psS", [P, 2, 512], F32))
            psP = st.enter_context(nc.psum_tensor("c_psP", [P, 2, 512], F32))
            psO = bank(st, "c_psO")
            bA = bank(st, "c_bA")
            bB = bank(st, "c_bB")
            bC = bank(st, "c_bC")

            w_loaded = sem("c_w_loaded")
            zeroed = sem("c_zeroed")
            wT_done = sem("c_wT_done")
            wT_ready = sem("c_wT_ready")
            fold_done = sem("c_fold_done")
            fold_ready = sem("c_fold_ready")
            bvb_ready = sem("c_bvb_ready")
            rowsum_step = sem("c_rowsum_step")
            consts_ready = sem("c_consts_ready")
            ctx_loaded = [sem("c_ctx_loaded_even"), sem("c_ctx_loaded_odd")]
            kbd_loaded = [sem("c_kbd_loaded_even"), sem("c_kbd_loaded_odd")]
            sems = [norm_sems(f"c_ln{i}") for i in range(4)]
            n0_ready, n1_ready, n2_ready, n3_ready = (s[-1] for s in sems)
            t0_done, t0_ready = sem("c_t0_done"), sem("c_t0_ready")
            y1_done, y1_ready = sem("c_y1_done"), sem("c_y1_ready")
            c_done, c_ready = sem("c_ctxT_done"), sem("c_ctxT_ready")
            k_done, k_ready = sem("c_k_done"), sem("c_k_ready")
            v_done, v_ready = sem("c_v_done"), sem("c_v_ready")
            t1_done, t1_ready = sem("c_t1_done"), sem("c_t1_ready")
            q_done, q_ready = sem("c_q_done"), sem("c_q_ready")
            s_done, s_ready = sem("c_scores_done"), sem("c_scores_ready")
            mx_ready = sem("c_max_ready")
            exp_ready = sem("c_exp_ready")
            sum_ready = sem("c_sum_ready")
            inv_ready = sem("c_inv_ready")
            pn_ready = sem("c_probs_ready")
            tp_done, tp_ready = sem("c_probsT_done"), sem("c_probsT_ready")
            pv_done, ca_ready = sem("c_pv_done"), sem("c_ca_ready")
            out_done, y2_ready = sem("c_out_done"), sem("c_y2_ready")
            t2_done, t2_ready = sem("c_t2_done"), sem("c_t2_ready")
            l1_done = sem("c_lin1_done")
            l1_ready = sem("c_lin1_ready")
            l2_done, y3_ready = sem("c_lin2_done"), sem("c_y3_ready")
            r1t_ready, r1_ready = sem("c_r1_product"), sem("c_r1_ready")
            r2t_ready, r2_ready = sem("c_r2_product"), sem("c_r2_ready")
            o3_ready, o3b_ready = sem("c_o3_product"), sem("c_o3_ready")
            x_ready = sem("c_x_ready")

            def over_groups(eng, prep, group, post):
                def prepare(p):
                    prep(0)

                def work(p, ahead):
                    g = 2 * p
                    started = not isinstance(p, int) or p > 0
                    group(g, 0, g + 1, g - 1 if started else None, g - 2 if started else None, p)
                    group(g + 1, 1, None if ahead is None else 2 * ahead, g, g - 1 if started else None, p)

                over_pairs(eng, PAIRS, prepare, work, peeled=2)
                post()

            def bcast(t):
                return t[:, :].unsqueeze(1).broadcast_to([P, GB, D])

            N_W = 2 + 4 + 2
            N_COL = 8 + FT
            N_ROW = 9
            ALL_LOADED = 16 * (N_W + N_COL + N_ROW)

            with nc.Block() as block:
                @block.sync
                def _(sp):
                    def col(dst, src):
                        sp.dma_start(dst, src.rearrange("(c a) -> c a", a=1)).then_inc(w_loaded, 16)

                    def row(i, src):
                        sp.dma_start(rows_bc[:, i, :], src.partition_broadcast(P)).then_inc(w_loaded, 16)

                    sp.dma_start(nat[:, 0, :], qkv_w[2 * D:3 * D, :]).then_inc(w_loaded, 16)
                    sp.dma_start(nat[:, 1, :], sa_out_w).then_inc(w_loaded, 16)
                    for i in range(3):
                        sp.dma_start(nat[:, 2 + i, :], in_proj_w[i * D:(i + 1) * D, :]).then_inc(w_loaded, 16)
                    sp.dma_start(nat[:, 5, :], mha_out_w).then_inc(w_loaded, 16)
                    sp.dma_start(l1n[:, :, :], lin1_w.rearrange("(f p) c -> p f c", p=P)).then_inc(w_loaded, 16)
                    sp.dma_start(l2n[:, :], lin2_w).then_inc(w_loaded, 16)
                    col(cols[:, 0:1], qkv_b[2 * D:3 * D])
                    for i in range(3):
                        col(cols[:, 1 + i:2 + i], in_proj_b[i * D:(i + 1) * D])
                    col(cols[:, 4:5], ln1_g)
                    col(cols[:, 5:6], ln1_b)
                    col(cols[:, 6:7], ln2_g)
                    col(l2b[:, :], ln2_b)
                    for f in range(FT):
                        col(l1b[:, f:f + 1], lin1_b[f * P:(f + 1) * P])
                    for i, src in enumerate((sa_out_b, mha_out_b, ln3_b, ln1_g, ln1_b, ln2_g, ln2_b, lin2_b, ln3_g)):
                        row(i, src)

                    def load(g, p, slot):
                        if later(g, 2):
                            sp.wait_ge(c_done, g - 1)
                        sp.dma_start(ctxs[:, slot, :, :],
                                     ctx_tokens[bass.ds(g * GB, GB), :, :].rearrange("b m d -> m b d"))\
                          .then_inc(ctx_loaded[slot], 16)

                    def spread(g, p, slot):
                        sp.wait_ge(k_ready, g + 1)
                        if not later(g, 2):
                            sp.wait_ge(zeroed, 2)
                        for h in range(H):
                            sp.dma_start(kbd[h * HD:(h + 1) * HD, slot, :, h * M:(h + 1) * M],
                                         kT[h * HD:(h + 1) * HD, :].rearrange("p (b m) -> p b m", b=GB))\
                              .then_inc(kbd_loaded[slot], 16)

                    def prepare(p):
                        load(0, 0, 0)
                        load(1, 0, 1)
                        spread(0, 0, 0)

                    def work(p, ahead):
                        spread(2 * p + 1, p, 1)
                        if ahead is not None:
                            load(2 * ahead, ahead, 0)
                            load(2 * ahead + 1, ahead, 1)
                            spread(2 * ahead, ahead, 0)

                    over_pairs(sp, PAIRS, prepare, work)

                @block.tensor
                def _(pe):
                    pe.wait_ge(w_loaded, ALL_LOADED)
                    for i in range(6):
                        bk = (bA, bB)[i % 2]
                        if i >= 2:
                            pe.wait_ge(wT_ready, i - 1)
                        pe.transpose(bk[:, 0:P], nat[:, i, :], ident[:, :]).then_inc(wT_done, 1)
                    pe.wait_ge(wT_ready, 5)
                    for f in range(FT):
                        i = pe.transpose(bA[:, f * P:(f + 1) * P], l1n[:, f, :], ident[:, :])
                    i.then_inc(wT_done, 1)
                    pe.wait_ge(wT_ready, 6)
                    for f in range(FT):
                        i = pe.transpose(bB[:, f * P:(f + 1) * P], l2n[:, f * P:(f + 1) * P], ident[:, :])
                    i.then_inc(wT_done, 1)
                    pe.wait_ge(bvb_ready, 1)
                    pe.wait_ge(wT_ready, 7)
                    pe.matmul(bC[:, 0:P], nat[:, 0, :], tr[:, 1, :], start=True, stop=True)
                    pe.matmul(bC[:, P:2 * P], bvb[:, 0, :], tr[:, 1, :], start=True, stop=True)
                    pe.matmul(bC[:, 2 * P:3 * P], bvb[:, 1, :], tr[:, 5, :], start=True, stop=True)
                    i = pe.matmul(bC[:, 3 * P:3 * P + 1], tr[:, 2, :], cols[:, 5:6], start=True, stop=True)
                    for f in range(FT):
                        i = pe.matmul(bC[:, 3 * P + 1 + f:3 * P + 2 + f], l1T[:, f, :], l2b[:, :],
                                      start=True, stop=True)
                    i.then_inc(fold_done, 1)

                    def four(dst, src, idn):
                        for b in range(GB):
                            i = pe.transpose(dst(b), src(b), idn)
                        return i

                    def at(bk, b, w=P):
                        return bk[:, b * w:(b + 1) * w]

                    def t0(g):
                        pe.wait_ge(n0_ready, g + 1)
                        if later(g, 2):
                            pe.wait_ge(y2_ready, g - 1)
                        elif later(g, 1):
                            pe.wait_ge(q_ready, g)
                        four(lambda b: at(bB, b), lambda b: xn[:, b, :], ident[:, :]).then_inc(t0_done, 1)

                    def y1_and_ctx(g, p, slot):
                        pe.wait_ge(t0_ready, g + 1)
                        if not later(g, 1):
                            pe.wait_ge(consts_ready, 1)
                        for b in range(GB):
                            i = pe.matmul(at(bB, b), xT[:, b * P:(b + 1) * P], m1t[:, :], start=True, stop=True)
                        i.then_inc(y1_done, 1)
                        pe.wait_ge(ctx_loaded[slot], 16 * (p + 1))
                        if later(g, 3):
                            pe.wait_ge(l1_ready, FT * (g - 2))
                        elif later(g, 1):
                            pe.wait_ge(v_ready, g)
                        four(lambda b: at(bC, b, M), lambda b: ctxs[:, slot, b, :], ident[0:M, 0:M])\
                            .then_inc(c_done, 1)

                    def kv(g):
                        pe.wait_ge(c_ready, g + 1)
                        pe.wait_ge(y1_ready, g + 1)
                        pe.matmul(bB[:, 0:GB * M], tr[:, 3, :], cT[:, :], start=True, stop=True).then_inc(k_done, 1)
                        for b in range(GB):
                            i = pe.matmul(bC[0:M, b * P:(b + 1) * P], cT[:, b * M:(b + 1) * M], tr[:, 4, :],
                                          start=True, stop=True)
                        i.then_inc(v_done, 1)

                    def t1(g):
                        pe.wait_ge(n1_ready, g + 1)
                        pe.wait_ge(k_ready, g + 1)
                        four(lambda b: at(bB, b), lambda b: n1[:, b, :], ident[:, :]).then_inc(t1_done, 1)

                    def q(g):
                        pe.wait_ge(t1_ready, g + 1)
                        pe.matmul(bB[:, :], qg[:, :], n1T[:, :], start=True, stop=True).then_inc(q_done, 1)

                    def scores(g, b, p, slot):
                        if b == 0:
                            pe.wait_ge(q_ready, g + 1)
                            pe.wait_ge(kbd_loaded[slot], 16 * H * (p + 1))
                        if b or later(g, 1):
                            pe.wait_ge(s_ready, GB * g + b)
                        for k in range(2):
                            i = pe.matmul(psS[:, k, 0:HB], qT[:, slot, b * P:(b + 1) * P],
                                          kbd[:, slot, b, k * HB:(k + 1) * HB], start=True, stop=True)
                        i.then_inc(s_done, 1)

                    def probsT(g, b):
                        pe.wait_ge(pn_ready, GB * g + b + 1)
                        for k in range(2):
                            if b or later(g, 1):
                                pe.wait_ge(tp_ready, 2 * (GB * g + b - 1) + k + 1)
                            for h in range(4 * k, 4 * k + 4):
                                i = pe.transpose(psP[0:M, k, (h % 4) * P:(h % 4 + 1) * P], pn[:, b % 2, h, :],
                                                 ident[:, :])
                            i.then_inc(tp_done, 1)

                    def pv(g, b, slot):
                        pe.wait_ge(tp_ready, 2 * (GB * g + b + 1))
                        if b == 0:
                            pe.wait_ge(v_ready, g + 1)
                            if later(g, 1):
                                pe.wait_ge(ca_ready, g)
                        for h in range(H):
                            i = pe.matmul(at(psO, b), vp[:, slot, b, h * P:(h + 1) * P], pT[:, b % 2, h, :],
                                          start=(h == 0), stop=(h == H - 1))
                        i.then_inc(pv_done, 1)

                    def out_proj(g, slot):
                        pe.wait_ge(ca_ready, g + 1)
                        if isinstance(g, int) and g == NG - 1:
                            pe.wait_ge(y2_ready, g)
                        else:
                            pe.wait_ge(q_ready, g + 2)
                        for b in range(GB):
                            i = pe.matmul(at(bB, b), ca[:, slot, b * P:(b + 1) * P], tr[:, 5, :],
                                          start=True, stop=True)
                        i.then_inc(out_done, 1)

                    def t2(g):
                        pe.wait_ge(n2_ready, g + 1)
                        if later(g, 1):
                            pe.wait_ge(y3_ready, g)
                        four(lambda b: at(bA, b), lambda b: n2[:, b, :], ident[:, :]).then_inc(t2_done, 1)

                    def lin1(g, f):
                        if f == 0:
                            pe.wait_ge(t2_ready, g + 1)
                        if f == 1:
                            pe.wait_ge(v_ready, NG if isinstance(g, int) and g > NG - 3 else g + 3)
                        if f >= 2:
                            pe.wait_ge(l1_ready, FT * g + f - 1)
                        pe.matmul((bA, bC)[f % 2][:, :], l1g[:, f, :], n2T[:, :], start=True, stop=True)                          .then_inc(l1_done, 1)

                    def lin2(g):
                        pe.wait_ge(l1_ready, FT * (g + 1))
                        for b in range(GB):
                            for f in range(FT):
                                i = pe.matmul(at(bA, b), hT[:, f, b * P:(b + 1) * P], l2T[:, f, :],
                                              start=(f == 0), stop=(f == FT - 1))
                        i.then_inc(l2_done, 1)

                    def prep(g):
                        t0(g)
                        y1_and_ctx(g, 0, 0)
                        kv(g)
                        t1(g)
                        q(g)

                    def group(g, slot, nxt, prv, pp, p):
                        other = 1 - slot
                        if prv is not None:
                            probsT(prv, GB - 1)
                        scores(g, 0, p, slot)
                        if prv is not None:
                            pv(prv, GB - 1, other)
                        if pp is not None:
                            lin2(pp)
                        if prv is not None:
                            out_proj(prv, other)
                        scores(g, 1, p, slot)
                        probsT(g, 0)
                        if nxt is not None:
                            t0(nxt)
                        pv(g, 0, slot)
                        if nxt is not None:
                            y1_and_ctx(nxt, p if slot == 0 else p + 1, other)
                        scores(g, 2, p, slot)
                        probsT(g, 1)
                        if prv is not None:
                            t2(prv)
                        if nxt is not None:
                            kv(nxt)
                        pv(g, 1, slot)
                        if prv is not None:
                            lin1(prv, 0)
                            lin1(prv, 1)
                        scores(g, 3, p, slot)
                        probsT(g, 2)
                        if nxt is not None:
                            t1(nxt)
                        if prv is not None:
                            lin1(prv, 2)
                            lin1(prv, 3)
                        pv(g, 2, slot)
                        if nxt is not None:
                            q(nxt)

                    def post():
                        probsT(NG - 1, GB - 1)
                        pv(NG - 1, GB - 1, 1)
                        lin2(NG - 2)
                        out_proj(NG - 1, 1)
                        t2(NG - 1)
                        for f in range(FT):
                            lin1(NG - 1, f)
                        lin2(NG - 1)

                    over_groups(pe, prep, group, post)

                @block.scalar
                def _(act):
                    for i in range(6):
                        act.wait_ge(wT_done, i + 1)
                        act.activation(tr[:, i, :], (bA, bB)[i % 2][:, 0:P], ACT.Copy).then_inc(wT_ready, 1)
                    act.wait_ge(wT_done, 7)
                    act.activation(l1T[:, :, :].rearrange("p f c -> p (f c)"), bA[:, :], ACT.Copy).then_inc(wT_ready, 1)
                    act.wait_ge(wT_done, 8)
                    act.activation(l2T[:, :, :].rearrange("p f c -> p (f c)"), bB[:, :], ACT.Copy).then_inc(wT_ready, 1)

                    def c_t0(g):
                        act.wait_ge(t0_done, g + 1)
                        if later(g, 1):
                            act.wait_ge(y1_done, g)
                        act.activation(xT[:, :], bB[:, :], ACT.Copy).then_inc(t0_ready, 1)

                    def c_ctx(g):
                        act.wait_ge(c_done, g + 1)
                        if later(g, 1):
                            act.wait_ge(v_done, g)
                        act.activation(cT[:, :], bC[:, 0:GB * M], ACT.Copy).then_inc(c_ready, 1)

                    def c_k(g, p, slot):
                        act.wait_ge(k_done, g + 1)
                        if later(g, 1):
                            act.wait_ge(kbd_loaded[1 - slot], 16 * H * (p + 1 if slot else p))
                        if later(g, 2):
                            act.wait_ge(s_done, GB * (g - 1))
                        act.activation(kT[:, :], bB[:, 0:GB * M], ACT.Identity, bias=cols[:, 2:3]).then_inc(k_ready, 1)

                    def c_v(g, slot):
                        act.wait_ge(v_done, g + 1)
                        if later(g, 2):
                            act.wait_ge(pv_done, GB * (g - 1))
                        else:
                            act.wait_ge(zeroed, 2)
                        dst = vp[:, slot, :, :].rearrange("p b (h w) -> p b h w", w=P + HD)[:, :, :, 0:HD]
                        act.activation(dst, bC[0:M, :].rearrange("p (b h i) -> p b h i", b=GB, h=H), ACT.Copy)\
                           .then_inc(v_ready, 1)

                    def c_t1(g):
                        act.wait_ge(t1_done, g + 1)
                        if later(g, 1):
                            act.wait_ge(q_done, g)
                        act.activation(n1T[:, :], bB[:, :], ACT.Copy).then_inc(t1_ready, 1)

                    def exps(g, b):
                        act.wait_ge(s_ready, GB * g + b + 1)
                        if b >= 2 or later(g, 1):
                            act.wait_ge(pn_ready, GB * g + b - 1)
                        act.activation(pr[:, b % 2, :, :], sc[:, b % 2, :, :], ACT.Exp).then_inc(exp_ready, 1)

                    def c_probsT(g, b):
                        for k in range(2):
                            act.wait_ge(tp_done, 2 * (GB * g + b) + k + 1)
                            if k == 0 and (b >= 2 or later(g, 1)):
                                act.wait_ge(pv_done, GB * g + b - 1)
                            act.activation(pT[:, b % 2, 4 * k:4 * k + 4, :].rearrange("p h t -> p (h t)"),
                                           psP[0:M, k, :], ACT.Copy).then_inc(tp_ready, 1)

                    def c_ca(g, slot):
                        act.wait_ge(pv_done, GB * (g + 1))
                        if later(g, 2):
                            act.wait_ge(out_done, g - 1)
                        act.activation(ca[:, slot, :], psO[:, :], ACT.Copy).then_inc(ca_ready, 1)

                    def c_t2(g):
                        act.wait_ge(t2_done, g + 1)
                        if later(g, 1):
                            act.wait_ge(l1_done, FT * g)
                        act.activation(n2T[:, :], bA[:, :], ACT.Copy).then_inc(t2_ready, 1)

                    def c_lin1(g, f):
                        act.wait_ge(l1_done, FT * g + f + 1)
                        if f == 0 and later(g, 1):
                            act.wait_ge(l2_done, g)
                        act.activation(hT[:, f, :], (bA, bC)[f % 2][:, :], ACT.Relu, bias=l1b2[:, f:f + 1])                           .then_inc(l1_ready, 1)

                    def c_q(g, slot):
                        act.wait_ge(q_done, g + 1)
                        if later(g, 2):
                            act.wait_ge(s_done, GB * (g - 1))
                        act.activation(qT[:, slot, :], bB[:, :], ACT.Identity, bias=bq3[:, :], scale=Q_SCALE)                           .then_inc(q_ready, 1)

                    def prep(g):
                        c_t0(g)
                        c_ctx(g)
                        c_k(g, 0, 0)
                        c_v(g, 0)
                        c_t1(g)
                        c_q(g, 0)

                    def group(g, slot, nxt, prv, pp, p):
                        other = 1 - slot
                        if prv is not None:
                            c_probsT(prv, GB - 1)
                        exps(g, 0)
                        if prv is not None:
                            c_ca(prv, other)
                        c_probsT(g, 0)
                        if nxt is not None:
                            c_t0(nxt)
                        exps(g, 1)
                        if nxt is not None:
                            c_ctx(nxt)
                        c_probsT(g, 1)
                        if prv is not None:
                            c_t2(prv)
                        if nxt is not None:
                            c_k(nxt, p if slot == 0 else p + 1, other)
                        exps(g, 2)
                        if nxt is not None:
                            c_v(nxt, other)
                        if prv is not None:
                            c_lin1(prv, 0)
                            c_lin1(prv, 1)
                        c_probsT(g, 2)
                        if nxt is not None:
                            c_t1(nxt)
                        if prv is not None:
                            c_lin1(prv, 2)
                        exps(g, 3)
                        if prv is not None:
                            c_lin1(prv, 3)
                        if nxt is not None:
                            c_q(nxt, other)

                    def post():
                        c_probsT(NG - 1, GB - 1)
                        c_ca(NG - 1, 1)
                        c_t2(NG - 1)
                        for f in range(FT):
                            c_lin1(NG - 1, f)

                    act.wait_ge(consts_ready, 1)
                    over_groups(act, prep, group, post)

                @block.gpsimd
                def _(pool):
                    for slot in range(2):
                        pool.memset(kbd[:, slot, :, :], 0.0)
                        pool.memset(vp[:, slot, :, :], 0.0).then_inc(zeroed, 1)
                    pool.wait_ge(consts_ready, 1)

                    def probs(g, b):
                        pool.wait_ge(exp_ready, GB * g + b + 1)
                        pool.wait_ge(inv_ready, GB * g + b + 1)
                        if b >= 2 or later(g, 1):
                            pool.wait_ge(tp_done, 2 * (GB * g + b - 1))
                        pool.tensor_tensor(pn[:, b % 2, :, :], pr[:, b % 2, :, :],
                                           iv[:, b % 2, :].unsqueeze(2).broadcast_to([P, H, M]), ALU.mult)\
                            .then_inc(pn_ready, 1)

                    def residual1(g, slot):
                        pool.wait_ge(n1_ready, g + 1)
                        if later(g, 2):
                            pool.wait_ge(y2_ready, g - 1)
                        pool.tensor_tensor(r1t[:, :, :], n1[:, :, :], bcast(rows_bc[:, G1, :]), ALU.mult)\
                            .then_inc(r1t_ready, 1)
                        pool.wait_ge(r1t_ready, g + 1)
                        pool.tensor_tensor(r1[:, slot, :, :], r1t[:, :, :], bcast(r1b), ALU.add).then_inc(r1_ready, 1)

                    def residual2(g):
                        pool.wait_ge(n2_ready, g + 1)
                        if later(g, 1):
                            pool.wait_ge(y3_ready, g)
                        pool.tensor_tensor(r2t[:, :, :], n2[:, :, :], bcast(rows_bc[:, G2, :]), ALU.mult)\
                            .then_inc(r2t_ready, 1)
                        pool.wait_ge(r2t_ready, g + 1)
                        pool.tensor_tensor(r2[:, :, :], r2t[:, :, :], bcast(r2b), ALU.add).then_inc(r2_ready, 1)

                    def last(g):
                        pool.wait_ge(n3_ready, g + 1)
                        if later(g, 1):
                            pool.wait_ge(x_ready, g)
                        pool.tensor_tensor(o3[:, :, :], n3[:, :, :], bcast(g3), ALU.mult).then_inc(o3_ready, 1)
                        pool.wait_ge(o3_ready, g + 1)
                        pool.tensor_tensor(o3b[:, :, :], o3[:, :, :], bcast(b3), ALU.add).then_inc(o3b_ready, 1)

                    def prep(g):
                        norm_pool(pool, g, 0, lns[0], sems[0])
                        norm_pool(pool, g, 0, lns[1], sems[1])
                        residual1(g, 0)

                    def group(g, slot, nxt, prv, pp, p):
                        other = 1 - slot
                        if nxt is not None:
                            norm_pool(pool, nxt, other, lns[0], sems[0])
                        probs(g, 0)
                        if prv is not None:
                            norm_pool(pool, prv, other, lns[2], sems[2])
                        probs(g, 1)
                        if prv is not None:
                            residual2(prv)
                        if nxt is not None:
                            norm_pool(pool, nxt, other, lns[1], sems[1])
                        if pp is not None:
                            norm_pool(pool, pp, slot, lns[3], sems[3])
                        probs(g, 2)
                        if pp is not None:
                            last(pp)
                        probs(g, 3)
                        if nxt is not None:
                            residual1(nxt, other)

                    def post():
                        norm_pool(pool, NG - 1, 1, lns[2], sems[2])
                        norm_pool(pool, NG - 2, 0, lns[3], sems[3])
                        residual2(NG - 1)
                        last(NG - 2)
                        norm_pool(pool, NG - 1, 1, lns[3], sems[3])
                        last(NG - 1)

                    over_groups(pool, prep, group, post)

                @block.vector
                def _(v):
                    v.wait_ge(w_loaded, ALL_LOADED)
                    for i, c in enumerate((0, 3)):
                        v.tensor_scalar(bvb[:, i, :], ident[:, :], 0.0, cols[:, c:c + 1], ALU.mult, ALU.add)\
                         .then_inc(rowsum_step, 1)
                    v.wait_ge(rowsum_step, 2)
                    v.sem_inc(bvb_ready, 1)
                    v.tensor_tensor(r1b0[:, :], rows_bc[:, B1, :], rows_bc[:, MHO, :], ALU.add).then_inc(rowsum_step, 1)
                    v.tensor_tensor(r2b[:, :], rows_bc[:, B2, :], rows_bc[:, L2B, :], ALU.add).then_inc(rowsum_step, 1)
                    v.tensor_scalar(g3[:, :], rows_bc[:, 8, :], gates[:, 1:2], None, ALU.mult)
                    v.tensor_scalar(b3[:, :], rows_bc[:, 2, :], gates[:, 1:2], None, ALU.mult)
                    v.wait_ge(wT_ready, 8)
                    v.tensor_scalar(qg[:, :], tr[:, 2, :], cols[:, 4:5], None, ALU.mult)
                    v.tensor_scalar(l1g[:, :, :], l1T[:, :, :], cols[:, 6:7], None, ALU.mult)
                    v.wait_ge(rowsum_step, 4)
                    v.wait_ge(fold_done, 1)
                    v.tensor_tensor(m1t[:, :], bC[:, 0:P], ident[:, :], ALU.add)
                    v.tensor_tensor(y1b[:, :], bC[:, P:2 * P], rows_bc[:, 0, :], ALU.add)
                    v.tensor_tensor(r1b[:, :], bC[:, 2 * P:3 * P], r1b0[:, :], ALU.add)
                    v.tensor_tensor(bq2[:, :], bC[:, 3 * P:3 * P + 1], cols[:, 1:2], ALU.add).then_inc(rowsum_step, 1)
                    v.tensor_tensor(l1b2[:, :], bC[:, 3 * P + 1:3 * P + 1 + FT], l1b[:, :], ALU.add)\
                     .then_inc(rowsum_step, 1)
                    v.wait_ge(rowsum_step, 5)
                    v.tensor_scalar(bq3[:, :], bq2[:, :], Q_SCALE, None, ALU.mult).then_inc(rowsum_step, 1)
                    v.wait_ge(rowsum_step, 7)
                    v.sem_inc(consts_ready, 1)

                    def x_of(g, b):
                        return X[:, bass.ds(g * GB + b, 1), :].rearrange("p a d -> p (a d)")

                    def moments(i, g, slot, src):
                        norm_moments(v, g, slot, src, lns[i], sems[i])

                    def apply(i, g, slot, src, dst):
                        norm_apply(v, g, slot, src, dst, lns[i], sems[i])

                    def moments0(g, slot):
                        moments(0, g, slot, lambda b: x_of(g, b))

                    def apply0(g, slot):
                        if later(g, 1):
                            v.wait_ge(t0_done, g)
                        apply(0, g, slot, lambda b: x_of(g, b), lambda b: xn[:, b, :])

                    def first_sum(g):
                        v.wait_ge(y1_done, g + 1)
                        v.tensor_tensor(y1[:, :, :], bB[:, :].rearrange("p (b d) -> p b d", b=GB), bcast(y1b), ALU.add)\
                         .then_inc(y1_ready, 1)

                    def moments1(g, slot):
                        v.wait_ge(y1_ready, g + 1)
                        moments(1, g, slot, lambda b: y1[:, b, :])

                    def apply1(g, slot):
                        if later(g, 1):
                            v.wait_ge(t1_done, g)
                            v.wait_ge(r1t_ready, g)
                        apply(1, g, slot, lambda b: y1[:, b, :], lambda b: n1[:, b, :])

                    def softmax_a(g, b):
                        s4 = psS[:, :, 0:HB].rearrange("p k (h m) -> p k h m", m=M)
                        v.wait_ge(s_done, GB * g + b + 1)
                        v.tensor_reduce(mx[:, b % 2, :].rearrange("p (k h) -> p k h", k=2), s4, AX.X, ALU.max)\
                         .then_inc(mx_ready, 1)
                        v.wait_ge(mx_ready, GB * g + b + 1)
                        if b >= 2 or later(g, 1):
                            v.wait_ge(exp_ready, GB * g + b - 1)
                        v.tensor_tensor(sc[:, b % 2, :, :].rearrange("p (k h) m -> p k h m", k=2), s4,
                                        mx[:, b % 2, :].rearrange("p (k h) -> p k h", k=2).unsqueeze(3)
                                        .broadcast_to([P, 2, H // 2, M]), ALU.subtract).then_inc(s_ready, 1)

                    def softmax_b(g, b):
                        v.wait_ge(exp_ready, GB * g + b + 1)
                        v.tensor_reduce(sm[:, b % 2, :], pr[:, b % 2, :, :], AX.X, ALU.add).then_inc(sum_ready, 1)
                        v.wait_ge(sum_ready, GB * g + b + 1)
                        if b >= 2 or later(g, 1):
                            v.wait_ge(pn_ready, GB * g + b - 1)
                        v.reciprocal(iv[:, b % 2, :], sm[:, b % 2, :]).then_inc(inv_ready, 1)

                    def second_sum(g, slot):
                        v.wait_ge(out_done, g + 1)
                        v.wait_ge(r1_ready, g + 1)
                        v.tensor_tensor(y2[:, :, :], bB[:, :].rearrange("p (b d) -> p b d", b=GB), r1[:, slot, :, :],
                                        ALU.add).then_inc(y2_ready, 1)

                    def moments2(g, slot):
                        v.wait_ge(y2_ready, g + 1)
                        moments(2, g, slot, lambda b: y2[:, b, :])

                    def apply2(g, slot):
                        if later(g, 1):
                            v.wait_ge(t2_done, g)
                            v.wait_ge(r2t_ready, g)
                        apply(2, g, slot, lambda b: y2[:, b, :], lambda b: n2[:, b, :])

                    def third_sum(g):
                        v.wait_ge(l2_done, g + 1)
                        v.wait_ge(r2_ready, g + 1)
                        v.tensor_tensor(y3[:, :, :], bA[:, :].rearrange("p (b d) -> p b d", b=GB), r2[:, :, :],
                                        ALU.add).then_inc(y3_ready, 1)

                    def moments3(g, slot):
                        v.wait_ge(y3_ready, g + 1)
                        moments(3, g, slot, lambda b: y3[:, b, :])

                    def apply3(g, slot):
                        if later(g, 1):
                            v.wait_ge(o3_ready, g)
                        apply(3, g, slot, lambda b: y3[:, b, :], lambda b: n3[:, b, :])

                    def add_x(g):
                        v.wait_ge(o3b_ready, g + 1)
                        xg = X[:, bass.ds(g * GB, GB), :].rearrange("p b d -> p (b d)")
                        v.tensor_tensor(xg, xg, o3b[:, :, :].rearrange("p b d -> p (b d)"), ALU.add).then_inc(x_ready, 1)

                    def prep(g):
                        moments0(g, 0)
                        apply0(g, 0)
                        first_sum(g)
                        moments1(g, 0)
                        apply1(g, 0)

                    def group(g, slot, nxt, prv, pp, p):
                        other = 1 - slot
                        if nxt is not None:
                            moments0(nxt, other)
                        softmax_a(g, 0)
                        if nxt is not None:
                            apply0(nxt, other)
                        softmax_b(g, 0)
                        if pp is not None:
                            third_sum(pp)
                        if prv is not None:
                            second_sum(prv, other)
                            moments2(prv, other)
                        softmax_a(g, 1)
                        if prv is not None:
                            apply2(prv, other)
                        softmax_b(g, 1)
                        if nxt is not None:
                            first_sum(nxt)
                            moments1(nxt, other)
                        softmax_a(g, 2)
                        if pp is not None:
                            moments3(pp, slot)
                        softmax_b(g, 2)
                        if nxt is not None:
                            apply1(nxt, other)
                        if pp is not None:
                            apply3(pp, slot)
                        softmax_a(g, 3)
                        softmax_b(g, 3)
                        if pp is not None:
                            add_x(pp)

                    def post():
                        third_sum(NG - 2)
                        second_sum(NG - 1, 1)
                        moments2(NG - 1, 1)
                        moments3(NG - 2, 0)
                        apply2(NG - 1, 1)
                        apply3(NG - 2, 0)
                        add_x(NG - 2)
                        third_sum(NG - 1)
                        moments3(NG - 1, 1)
                        apply3(NG - 1, 1)
                        add_x(NG - 1)

                    over_groups(v, prep, group, post)

        end_phase()

        with ExitStack() as st:
            HC = w1.shape[0] // P
            HW = HC * P
            TAPS = conv_w.shape[2]
            BIG = 1.5 * 2.0 ** 23
            QMAX = 127.0
            W_COUNT = float(HW * D)
            TQ_LAG = 3

            w1n = sb(st, "d_w1n", [P, HC, D])
            w2n = sb(st, "d_w2n", [P, HC, P])
            cwn = sb(st, "d_cwn", [P, HC, TAPS])
            cbn = sb(st, "d_cbn", [P, HW])
            asum = sb(st, "d_asum", [P, 2])
            ones = sb(st, "d_ones", [P, P])
            ones_bf = sb(st, "d_ones_bf", [P, P], BF16)
            mean = sb(st, "d_mean", [P, 2])
            rmean = sb(st, "d_rmean", [P, 2])
            ta = sb(st, "d_ta", [P, 2, HW])
            tb = sb(st, "d_tb", [P, 2, HW])
            tt = sb(st, "d_tt", [P, 2, HW])
            w1k = sb(st, "d_w1k", [P, TAPS, HC, D])
            wkh = sb(st, "d_wkh", [P, TAPS, HW], F32R)
            wkl = sb(st, "d_wkl", [P, TAPS, HW], F32R)
            w2T = sb(st, "d_w2T", [P, HC, P], BF16)
            cb1 = sb(st, "d_cb1", [P, HW], BF16)
            cr1 = sb(st, "d_cr1", [P, HW])
            cb2 = sb(st, "d_cb2", [P, HW], BF16)
            cr2 = sb(st, "d_cr2", [P, HW])
            cm1 = sb(st, "d_cm1", [P, HW])
            cm2 = sb(st, "d_cm2", [P, HW])
            cb = sb(st, "d_cb", [P, HW], BF16)
            sw2 = sb(st, "d_sw2", [P, 1])
            big = sb(st, "d_big", [P, HW])

            xn = sb(st, "d_xn", [P, GB, D])
            am = sb(st, "d_am", [P, GB])
            amc = sb(st, "d_amc", [P, GB])
            ar = sb(st, "d_ar", [P, GB])
            asc = sb(st, "d_asc", [P, GB])
            ais = sb(st, "d_ais", [P, GB])
            za = sb(st, "d_za", [P, GB, D])
            zb = sb(st, "d_zb", [P, GB, D])
            xq = sb(st, "d_xq", [P, GB, D])
            xh = sb(st, "d_xh", [P, 2, GB, P + 2], F32R)
            xl = sb(st, "d_xl", [P, 2, GB, P + 2], F32R)
            sl = sb(st, "d_sl", [P, GB, HW])
            hm = sb(st, "d_hm", [P, GB])
            hmc = sb(st, "d_hmc", [P, GB])
            hr = sb(st, "d_hr", [P, GB])
            hsc = sb(st, "d_hsc", [P, GB])
            hf = sb(st, "d_hf", [P, 2, GB])
            hz = sb(st, "d_hz", [P, GB, HW])
            hc = sb(st, "d_hc", [P, GB, HW])
            hq = sb(st, "d_hq", [P, GB, HW], BF16)
            hqT = sb(st, "d_hqT", [P, GB, HC, P], BF16)
            ln = norm_tiles(st, "lnD")

            psT = bank(st, "d_psT")
            psH = [bank(st, f"d_psH{b}") for b in range(GB)]
            psQ = [bank(st, f"d_psQ{b}", BF16, 1024) for b in range(2)]
            psO = bank(st, "d_psO")

            w_loaded = sem("d_w_loaded")
            prepv = sem("d_vector_prepared")
            step = sem("d_prepare_step")
            ones_ready = sem("d_ones_ready")
            sums_done = sem("d_sums_done")
            wk_done = sem("d_wk_done")
            wkh_ready = sem("d_wk_upper_ready")
            wkl_ready = sem("d_wk_lower_ready")
            w2T_ready = sem("d_w2T_ready")
            padded = sem("d_padded")
            lnD = norm_sems("d_ln")
            normed = lnD[-1]
            quant = sem("d_quant_step")
            xq_ready = sem("d_xq_ready")
            xT_done = sem("d_xT_done")
            xh_ready = sem("d_xh_ready")
            xl_ready = sem("d_xl_ready")
            h_done = sem("d_hidden_done")
            sl_ready = sem("d_silu_ready")
            hstep = sem("d_hidden_scale_step")
            hz_ready = sem("d_hidden_scaled")
            hc_ready = sem("d_hidden_clipped")
            hq_ready = sem("d_hidden_rounded")
            tq_done = sem("d_hiddenT_done")
            tq_ready = sem("d_hiddenT_ready")
            o_done = sem("d_out_done")
            x_ready = sem("d_x_ready")

            def over_groups(eng, prep, group, tail):
                def prepare(p):
                    prep(0)

                def work(p, ahead):
                    group(2 * p, 0, 2 * p + 1)
                    group(2 * p + 1, 1, None if ahead is None else 2 * ahead)

                over_pairs(eng, PAIRS, prepare, work)
                tail()

            with nc.Block() as block:
                @block.sync
                def _(sp):
                    sp.dma_start(w1n[:, :, :], w1.rearrange("(c p) d -> p c d", p=P)).then_inc(w_loaded, 16)
                    sp.dma_start(w2n[:, :, :].rearrange("p c k -> p (c k)"), w2).then_inc(w_loaded, 16)
                    sp.dma_start(cwn[:, :, :], conv_w.rearrange("(c p) a k -> p c (a k)", p=P)).then_inc(w_loaded, 16)
                    sp.dma_start(cbn[:, :], conv_b.partition_broadcast(P)).then_inc(w_loaded, 16)

                    def store(g):
                        sp.wait_ge(x_ready, g + 1)
                        sp.dma_start(out[bass.ds(g * GB, GB), :, :].rearrange("b s d -> s b d"),
                                     X[:, bass.ds(g * GB, GB), :]).then_inc(out_stored, 16)

                    with sp.Fori(0, NG) as g:
                        store(g)
                    sp.wait_ge(out_stored, 16 * NG)

                @block.tensor
                def _(pe):
                    pe.wait_ge(ones_ready, 1)
                    pe.wait_ge(prepv, 1)
                    pe.matmul(psO[:, 0:2], ones[:, :], asum[:, :], start=True, stop=True).then_inc(sums_done, 1)
                    pe.wait_ge(prepv, 2)
                    for k in range(TAPS):
                        for c in range(HC):
                            i = pe.transpose(psH[k][:, c * P:(c + 1) * P], w1k[:, k, c, :], ident[:, :])
                        i.then_inc(wk_done, 1)
                    for c in range(HC):
                        i = pe.transpose(psH[TAPS][:, c * P:(c + 1) * P], tt[:, 1, c * P:(c + 1) * P], ident[:, :])
                    i.then_inc(wk_done, 1)

                    def x_transposes(g):
                        pe.wait_ge(xq_ready, g + 1)
                        if later(g, 1):
                            pe.wait_ge(xl_ready, g)
                        for b in range(GB):
                            i = pe.transpose(psT[:, b * P:(b + 1) * P], xq[:, b, :], ident[:, :])
                        i.then_inc(xT_done, 1)

                    def hidden(g, b, slot):
                        if b == 0:
                            if not later(g, 1):
                                pe.wait_ge(wkl_ready, TAPS)
                                pe.wait_ge(w2T_ready, 1)
                                pe.wait_ge(prepv, 3)
                            pe.wait_ge(xh_ready, g + 1)
                            pe.wait_ge(xl_ready, g + 1)
                        if later(g, 1):
                            pe.wait_ge(sl_ready, GB * (g - 1) + b + 1)
                        pe.matmul(psH[b][:, :], ones_bf[:, :], cb[:, :], start=True, stop=False)
                        for k in range(TAPS):
                            h, lo = xh[:, slot, b, k:k + P], xl[:, slot, b, k:k + P]
                            pe.matmul(psH[b][:, :], lo, wkh[:, k, :], start=False, stop=False)
                            pe.matmul(psH[b][:, :], h, wkl[:, k, :], start=False, stop=False)
                            i = pe.matmul(psH[b][:, :], h, wkh[:, k, :], start=False, stop=(k == TAPS - 1))
                        i.then_inc(h_done, 1)

                    def hidden_transposes(g, b):
                        n = GB * g + b
                        pe.wait_ge(hq_ready, n + 1)
                        if b >= 2 or later(g, 1):
                            pe.wait_ge(tq_ready, n - 1)
                        for c in range(HC):
                            i = pe.transpose(psQ[b % 2][:, c * P:(c + 1) * P], hq[:, b, c * P:(c + 1) * P],
                                             ident_bf[:, :])
                        i.then_inc(tq_done, 1)

                    def second(g, b):
                        pe.wait_ge(tq_ready, GB * g + b + 1)
                        if b == 0 and later(g, 1):
                            pe.wait_ge(x_ready, g)
                        for c in range(HC):
                            i = pe.matmul(psO[:, b * P:(b + 1) * P], hqT[:, b, c, :], w2T[:, c, :],
                                          start=(c == 0), stop=(c == HC - 1))
                        i.then_inc(o_done, 1)

                    def group(g, slot, nxt):
                        for b in range(GB):
                            hidden(g, b, slot)
                            if b == TQ_LAG:
                                hidden_transposes(g, 0)
                            elif later(g, 1):
                                hidden_transposes(g - 1, b + 1)
                            if later(g, 1):
                                second(g - 1, b)
                            if b == 1 and nxt is not None:
                                x_transposes(nxt)

                    def tail():
                        for b in range(GB):
                            if b < GB - 1:
                                hidden_transposes(NG - 1, b + 1)
                            second(NG - 1, b)

                    over_groups(pe, x_transposes, group, tail)

                @block.scalar
                def _(act):
                    for k in range(TAPS):
                        act.wait_ge(wk_done, k + 1)
                        act.activation(wkh[:, k, :], psH[k][:, :], ACT.Copy).then_inc(wkh_ready, 1)
                    act.wait_ge(wk_done, TAPS + 1)
                    act.activation(w2T[:, :, :].rearrange("p c k -> p (c k)"), psH[TAPS][:, :], ACT.Copy)\
                       .then_inc(w2T_ready, 1)

                    def x_upper(g, slot):
                        act.wait_ge(xT_done, g + 1)
                        if later(g, 2):
                            act.wait_ge(h_done, GB * (g - 1))
                        else:
                            act.wait_ge(padded, 1)
                        act.activation(xh[:, slot, :, 1:P + 1], psT[:, :].rearrange("p (b t) -> p b t", b=GB),
                                       ACT.Copy).then_inc(xh_ready, 1)

                    def silu(g, b):
                        act.wait_ge(h_done, GB * g + b + 1)
                        if later(g, 1):
                            act.wait_ge(hz_ready, GB * (g - 1) + b + 1)
                        act.activation(sl[:, b, :], psH[b][:, :], ACT.Silu).then_inc(sl_ready, 1)

                    def scale(g, b):
                        act.wait_ge(hstep, 4 * (GB * g + b) + 4)
                        if later(g, 1):
                            act.wait_ge(hc_ready, GB * (g - 1) + b + 1)
                        act.activation(hz[:, b, :], sl[:, b, :], ACT.Identity, bias=big[:, 0:1],
                                       scale=hsc[:, b:b + 1]).then_inc(hz_ready, 1)

                    def copy_hidden(g, b):
                        act.wait_ge(tq_done, GB * g + b + 1)
                        if later(g, 1):
                            act.wait_ge(o_done, GB * (g - 1) + b + 1)
                        act.activation(hqT[:, b, :, :].rearrange("p c k -> p (c k)"), psQ[b % 2][:, 0:HW],
                                       ACT.Copy).then_inc(tq_ready, 1)

                    def group(g, slot, nxt):
                        for b in range(GB):
                            silu(g, b)
                            if b >= 1:
                                scale(g, b - 1)
                            elif later(g, 1):
                                scale(g - 1, GB - 1)
                            if later(g, 1):
                                copy_hidden(g - 1, b)
                            if b == 2 and nxt is not None:
                                x_upper(nxt, 1 - slot)

                    def tail():
                        scale(NG - 1, GB - 1)
                        for b in range(GB):
                            copy_hidden(NG - 1, b)

                    over_groups(act, lambda g: x_upper(g, 0), group, tail)

                @block.gpsimd
                def _(pool):
                    pool.memset(ones[:, :], 1.0)
                    pool.memset(ones_bf[:, :], 1.0)
                    pool.memset(big[:, :], BIG).then_inc(ones_ready, 1)
                    pool.memset(xh[:, :, :, :].bitcast(F32), 0.0)
                    pool.memset(xl[:, :, :, :].bitcast(F32), 0.0).then_inc(padded, 1)

                    def rounded(g, b):
                        pool.wait_ge(hc_ready, GB * g + b + 1)
                        if later(g, 1):
                            pool.wait_ge(tq_done, GB * (g - 1) + b + 1)
                        pool.tensor_tensor(hq[:, b, :], hc[:, b, :], big[:, :], ALU.subtract).then_inc(hq_ready, 1)

                    def group(g, slot, nxt):
                        for b in range(GB):
                            if b >= 1:
                                rounded(g, b - 1)
                            elif later(g, 1):
                                rounded(g - 1, GB - 1)
                            if b == 0 and nxt is not None:
                                norm_pool(pool, nxt, 1 - slot, ln, lnD)

                    over_groups(pool, lambda g: norm_pool(pool, g, 0, ln, lnD), group,
                                lambda: rounded(NG - 1, GB - 1))

                @block.vector
                def _(v):
                    v.wait_ge(w_loaded, 64)
                    for i, w in enumerate((w1n, w2n)):
                        ins = v.tensor_reduce(asum[:, i:i + 1], w[:, :, :].rearrange("p c d -> p (c d)"), AX.X,
                                              ALU.add, apply_absolute_value=True)
                    ins.then_inc(prepv, 1)
                    v.wait_ge(sums_done, 1)
                    v.tensor_scalar(mean[:, :], psO[:, 0:2], 1.0 / W_COUNT, 1e-5, ALU.mult, ALU.max).then_inc(step, 1)
                    v.wait_ge(step, 1)
                    v.reciprocal(rmean[:, :], mean[:, :])
                    v.tensor_scalar(sw2[:, :], mean[:, 1:2], gates[:, 3:4], None, ALU.mult).then_inc(step, 1)
                    v.wait_ge(step, 2)
                    for i, w in enumerate((w1n, w2n)):
                        ins = v.tensor_scalar(ta[:, i, :], w[:, :, :].rearrange("p c d -> p (c d)"),
                                              rmean[:, i:i + 1], BIG, ALU.mult, ALU.add)
                    ins.then_inc(step, 1)
                    v.wait_ge(step, 3)
                    v.tensor_scalar(tb[:, :, :], ta[:, :, :], BIG, 1.0, ALU.subtract, ALU.min).then_inc(step, 1)
                    v.wait_ge(step, 4)
                    v.tensor_scalar(tt[:, :, :], tb[:, :, :], -1.0, None, ALU.max).then_inc(step, 1)
                    v.wait_ge(step, 5)
                    for k in range(TAPS):
                        for c in range(HC):
                            ins = v.tensor_scalar(w1k[:, k, c, :], tt[:, 0, c * D:(c + 1) * D], cwn[:, c, k:k + 1],
                                                  mean[:, 0:1], ALU.mult, ALU.mult)
                    ins.then_inc(prepv, 1)
                    v.tensor_copy(cb1[:, :], cbn[:, :]).then_inc(step, 1)
                    v.wait_ge(step, 6)
                    v.tensor_tensor(cr1[:, :], cbn[:, :], cb1[:, :], ALU.subtract)
                    v.tensor_scalar(cm1[:, :], cb1[:, :], ident[:, 0:1], None, ALU.mult).then_inc(step, 1)
                    v.wait_ge(step, 7)
                    v.tensor_copy(cb2[:, :], cr1[:, :]).then_inc(step, 1)
                    v.wait_ge(step, 8)
                    v.tensor_tensor(cr2[:, :], cr1[:, :], cb2[:, :], ALU.subtract)
                    v.scalar_tensor_tensor(out=cm2[:, :], in0=cb2[:, :], scalar=ident[:, 1:2], in1=cm1[:, :],
                                           op0=ALU.mult, op1=ALU.add).then_inc(step, 1)
                    v.wait_ge(step, 9)
                    v.scalar_tensor_tensor(out=cb[:, :], in0=cr2[:, :], scalar=ident[:, 2:3], in1=cm2[:, :],
                                           op0=ALU.mult, op1=ALU.add).then_inc(prepv, 1)
                    for k in range(TAPS):
                        v.wait_ge(wkh_ready, k + 1)
                        v.tensor_tensor(wkl[:, k, :], psH[k][:, :], wkh[:, k, :].bitcast(F32), ALU.subtract)\
                         .then_inc(wkl_ready, 1)

                    def x_of(g, b):
                        return X[:, bass.ds(g * GB + b, 1), :].rearrange("p a d -> p (a d)")

                    def moments(g, slot):
                        norm_moments(v, g, slot, lambda b: x_of(g, b), ln, lnD)

                    STEPS = 6

                    def quantise(g, slot):
                        norm_apply(v, g, slot, lambda b: x_of(g, b), lambda b: xn[:, b, :], ln, lnD)
                        v.wait_ge(normed, g + 1)
                        v.tensor_reduce(am[:, :], xn[:, :, :], AX.X, ALU.max, apply_absolute_value=True)\
                         .then_inc(quant, 1)
                        v.wait_ge(quant, STEPS * g + 1)
                        v.tensor_scalar(amc[:, :], am[:, :], 1e-5, None, ALU.max).then_inc(quant, 1)
                        v.wait_ge(quant, STEPS * g + 2)
                        v.reciprocal(ar[:, :], amc[:, :])
                        v.tensor_scalar(ais[:, :], amc[:, :], 1.0 / QMAX, None, ALU.mult).then_inc(quant, 1)
                        v.wait_ge(quant, STEPS * g + 3)
                        v.tensor_scalar(asc[:, :], ar[:, :], QMAX, None, ALU.mult).then_inc(quant, 1)
                        v.wait_ge(quant, STEPS * g + 4)
                        for b in range(GB):
                            i = v.tensor_scalar(za[:, b, :], xn[:, b, :], asc[:, b:b + 1], BIG, ALU.mult, ALU.add)
                        i.then_inc(quant, 1)
                        v.wait_ge(quant, STEPS * g + 5)
                        v.tensor_scalar(zb[:, :, :], za[:, :, :], BIG - QMAX - 1, BIG + QMAX, ALU.max, ALU.min)\
                         .then_inc(quant, 1)
                        v.wait_ge(quant, STEPS * g + 6)
                        if later(g, 1):
                            v.wait_ge(xT_done, g)
                        for b in range(GB):
                            i = v.tensor_scalar(xq[:, b, :], zb[:, b, :], BIG, ais[:, b:b + 1],
                                                ALU.subtract, ALU.mult)
                        i.then_inc(xq_ready, 1)

                    def x_lower(g, slot):
                        v.wait_ge(xh_ready, g + 1)
                        v.tensor_tensor(xl[:, slot, :, 1:P + 1], psT[:, :].rearrange("p (b t) -> p b t", b=GB),
                                        xh[:, slot, :, 1:P + 1].bitcast(F32), ALU.subtract).then_inc(xl_ready, 1)

                    def hidden_scale(g, b, slot):
                        n = GB * g + b
                        v.wait_ge(sl_ready, n + 1)
                        v.tensor_reduce(hm[:, b:b + 1], sl[:, b, :], AX.X, ALU.max, apply_absolute_value=True)\
                         .then_inc(hstep, 1)
                        v.wait_ge(hstep, 4 * n + 1)
                        v.tensor_scalar(hmc[:, b:b + 1], hm[:, b:b + 1], 1e-5, None, ALU.max).then_inc(hstep, 1)
                        v.wait_ge(hstep, 4 * n + 2)
                        v.reciprocal(hr[:, b:b + 1], hmc[:, b:b + 1])
                        v.tensor_scalar(hf[:, slot, b:b + 1], hmc[:, b:b + 1], 1.0 / QMAX, sw2[:, :],
                                        ALU.mult, ALU.mult).then_inc(hstep, 1)
                        v.wait_ge(hstep, 4 * n + 3)
                        v.tensor_scalar(hsc[:, b:b + 1], hr[:, b:b + 1], QMAX, None, ALU.mult).then_inc(hstep, 1)

                    def hidden_clip(g, b):
                        n = GB * g + b
                        v.wait_ge(hz_ready, n + 1)
                        if later(g, 1):
                            v.wait_ge(hq_ready, GB * (g - 1) + b + 1)
                        v.tensor_scalar(hc[:, b, :], hz[:, b, :], BIG - QMAX - 1, BIG + QMAX, ALU.max, ALU.min)\
                         .then_inc(hc_ready, 1)

                    def final(g, slot):
                        v.wait_ge(o_done, GB * (g + 1))
                        for b in range(GB):
                            i = v.scalar_tensor_tensor(out=x_of(g, b), in0=psO[:, b * P:(b + 1) * P],
                                                       scalar=hf[:, slot, b:b + 1], in1=x_of(g, b),
                                                       op0=ALU.mult, op1=ALU.add)
                        i.then_inc(x_ready, 1)

                    def prep(g):
                        moments(g, 0)
                        quantise(g, 0)
                        x_lower(g, 0)

                    def group(g, slot, nxt):
                        for b in range(GB):
                            hidden_scale(g, b, slot)
                            if b >= 1:
                                hidden_clip(g, b - 1)
                            elif later(g, 1):
                                hidden_clip(g - 1, GB - 1)
                            if nxt is not None:
                                if b == 0:
                                    moments(nxt, 1 - slot)
                                    quantise(nxt, 1 - slot)
                                if b == 2:
                                    x_lower(nxt, 1 - slot)
                        if later(g, 1):
                            final(g - 1, 1 - slot)

                    def tail():
                        hidden_clip(NG - 1, GB - 1)
                        final(NG - 1, 1)

                    over_groups(v, prep, group, tail)


_INS = ['x', 'ctx_1024', 'mask_BxS2_if1', 'g_xattn', 'g_ffn', 'L0_xattn_W', 'L0_xattn_diagonal',
        'L0_ffn_gate_w', 'L0_ffn_wg', 'L0_ffn_wu', 'L0_ffn_wd', 'L0_ffn_swg', 'L0_ffn_swu', 'L0_ffn_swd',
        'L1_xattn_qkv_w', 'L1_xattn_qkv_b', 'L1_xattn_sa_out_w', 'L1_xattn_sa_out_b',
        'L1_xattn_in_proj_w', 'L1_xattn_in_proj_b', 'L1_xattn_mha_out_w', 'L1_xattn_mha_out_b',
        'L1_xattn_lin1_w', 'L1_xattn_lin1_b', 'L1_xattn_lin2_w', 'L1_xattn_lin2_b',
        'L1_xattn_ln1_g', 'L1_xattn_ln1_b', 'L1_xattn_ln2_g', 'L1_xattn_ln2_b', 'L1_xattn_ln3_g', 'L1_xattn_ln3_b',
        'L1_ffn_w1', 'L1_ffn_conv_w', 'L1_ffn_conv_b', 'L1_ffn_w2']


def kernel(**inputs):
    import numpy as np
    import concourse.bacc as bacc
    from concourse.bass_utils import run_bass_kernel_spmd

    nc = bacc.Bacc("TRN2", target_bir_lowering=False, num_devices=1)
    arrays, args = {}, []
    for name in _INS:
        a = np.ascontiguousarray(inputs[name])
        arrays[f"in_{name}"] = a
        args.append(nc.dram_tensor(f"in_{name}", a.shape, mybir.dt.from_np(a.dtype), kind="ExternalInput").ap())
    n_exp, _, inter = inputs['L0_ffn_wg'].shape
    consts = {
        "sel": np.tile(np.repeat(np.eye(n_exp, dtype=np.float32), inter, axis=1), (3, 1)),
        "ramp": np.arange(n_exp, 0, -1, dtype=np.float32),
    }
    for name, a in consts.items():
        arrays[f"const_{name}"] = a
        args.append(nc.dram_tensor(f"const_{name}", a.shape, F32, kind="ExternalInput").ap())
    out = nc.dram_tensor("out_x", inputs['x'].shape, F32, kind="ExternalOutput").ap()
    flamingo_gated(nc, *args, out)
    r = run_bass_kernel_spmd(nc, [arrays], core_ids=[0])
    return r.results[0]["out_x"]
```

```python
import math
from contextlib import ExitStack

import concourse.bass as bass
from concourse import mybir
from concourse.alu_op_type import AluOpType as ALU

ACT = mybir.ActivationFunctionType
AX = mybir.AxisListType
F32 = mybir.dt.float32
F32R = mybir.dt.float32r
BF16 = mybir.dt.bfloat16
I32 = mybir.dt.int32

P = 128
GB = 4
GT = GB * P
LN_EPS = 1e-5
NEG = -10000.0


def later(g, n):
    return not isinstance(g, int) or g >= n


def over_pairs(eng, pairs, prepare, work, peeled=1):
    prepare(0)
    for p in range(peeled):
        work(p, p + 1)
    with eng.Fori(peeled, pairs - 1) as p:
        work(p, p + 1)
    work(pairs - 1, None)


def flamingo_gated(nc, x, ctx_tokens, mask, g_xattn, g_ffn, W, diagonal, gate_w, wg, wu, wd, swg, swu, swd,
                   qkv_w, qkv_b, sa_out_w, sa_out_b, in_proj_w, in_proj_b, mha_out_w, mha_out_b,
                   lin1_w, lin1_b, lin2_w, lin2_b, ln1_g, ln1_b, ln2_g, ln2_b, ln3_g, ln3_b,
                   w1, conv_w, conv_b, w2, sel_const, ramp_const, out):
    B, S, D = x.shape
    M = ctx_tokens.shape[1]
    assert S == P and D == P and B % (2 * GB) == 0
    NG = B // GB
    PAIRS = NG // 2

    top = ExitStack()

    sems_of_phase = []

    def sem(name):
        s = nc.alloc_semaphore(name=name)
        sems_of_phase.append(s)
        return s

    def end_phase():
        nc.clear_and_free_semaphores(list(sems_of_phase))
        nc.all_engine_barrier()
        sems_of_phase.clear()

    def sb(stack, name, shape, dt=F32):
        return stack.enter_context(nc.sbuf_tensor(name, shape, dt))

    def bank(stack, name, dt=F32, width=512):
        return stack.enter_context(nc.psum_tensor(name, [P, width], dt))

    with top:
        X = sb(top, "X", [P, B, D])
        ident = sb(top, "ident", [P, P])
        ident_bf = sb(top, "ident_bf", [P, P], BF16)
        gates = sb(top, "gates", [P, 4])
        graw = sb(top, "graw", [P, 4])
        half_neg = sb(top, "half_neg", [P, GB])
        eps_tile = sb(top, "eps_tile", [P, GB])

        const_filled = sem("const_filled")
        const_ready = sem("const_ready")
        gates_loaded = sem("gates_loaded")
        gates_ready = sem("gates_ready")
        x_loaded = [sem("x_loaded_even"), sem("x_loaded_odd")]
        out_stored = sem("out_stored")

        weights_b = ExitStack()
        E, _, INTER = wg.shape
        SH = swg.shape[1]
        EH = E * INTER
        ET = EH // P
        ST = -(-SH // P)
        NT = ST + ET
        assert EH == ET * P and NT % 2 == 0
        PARTS = 3
        FT = lin1_w.shape[0] // P
        HC = w1.shape[0] // P
        HW = HC * P
        TAPS = conv_w.shape[2]
        nat = sb(top, "c_nat", [P, 6, D])
        l1n = sb(top, "c_l1n", [P, FT, D])
        l2n = sb(top, "c_l2n", [P, FT * P])
        cols = sb(top, "c_cols", [P, 7])
        l2b = sb(top, "c_ln2b", [P, 1])
        l1b = sb(top, "c_l1b", [P, FT])
        rows_bc = sb(top, "c_rows", [P, 9, D])
        w1n = sb(top, "d_w1n", [P, HC, D])
        w2n = sb(top, "d_w2n", [P, HC, P])
        cwn = sb(top, "d_cwn", [P, HC, TAPS])
        cbn = sb(top, "d_cbn", [P, HW])
        wn = sb(weights_b, "wn", [P, 2, NT * P])
        dn = sb(weights_b, "dn", [P, NT, D])
        gwn = sb(weights_b, "gwn", [E, D])
        seln = sb(weights_b, "seln", [PARTS * E, EH])
        ramp = sb(weights_b, "ramp", [P, E])

        up_loaded = sem("up_loaded")
        down_loaded = sem("down_loaded")
        router_loaded = sem("router_loaded")
        sel_loaded = sem("sel_loaded")
        layer_loaded = sem("layer_loaded")
        ffn_loaded = sem("ffn_loaded")
        sems_of_phase.clear()

        def load_experts_weights(sp):
            sp.dma_start(gwn[:, :], gate_w).then_inc(router_loaded, 16)
            sp.dma_start(ramp[:, :], ramp_const.partition_broadcast(P)).then_inc(router_loaded, 16)
            sp.dma_start(seln[:, :], sel_const).then_inc(sel_loaded, 16)
            for k, (we, ws) in enumerate(((wg, swg), (wu, swu))):
                sp.dma_start(wn[:, k, ST * P:NT * P].rearrange("h (e i) -> h e i", e=E),
                             we.rearrange("e h i -> h e i")).then_inc(up_loaded, 16)
                sp.dma_start(wn[:, k, 0:SH], ws).then_inc(up_loaded, 16)
            full = SH // P
            sp.dma_start(dn[:, 0:full, :], swd[0:full * P, :].rearrange("(j p) d -> p j d", p=P))\
              .then_inc(down_loaded, 16)
            sp.dma_start(dn[0:SH - full * P, full, :], swd[full * P:SH, :]).then_inc(down_loaded, 16)
            sp.dma_start(dn[:, ST:NT, :], wd.rearrange("e i d -> (e i) d").rearrange("(j p) d -> p j d", p=P))\
              .then_inc(down_loaded, 16)


        def load_layer1_weights(sp):
            def col(dst, src):
                sp.dma_start(dst, src.rearrange("(c a) -> c a", a=1)).then_inc(layer_loaded, 16)

            def row(i, src):
                sp.dma_start(rows_bc[:, i, :], src.partition_broadcast(P)).then_inc(layer_loaded, 16)

            sp.dma_start(nat[:, 0, :], qkv_w[2 * D:3 * D, :]).then_inc(layer_loaded, 16)
            sp.dma_start(nat[:, 1, :], sa_out_w).then_inc(layer_loaded, 16)
            for i in range(3):
                sp.dma_start(nat[:, 2 + i, :], in_proj_w[i * D:(i + 1) * D, :]).then_inc(layer_loaded, 16)
            sp.dma_start(nat[:, 5, :], mha_out_w).then_inc(layer_loaded, 16)
            sp.dma_start(l1n[:, :, :], lin1_w.rearrange("(f p) c -> p f c", p=P)).then_inc(layer_loaded, 16)
            sp.dma_start(l2n[:, :], lin2_w).then_inc(layer_loaded, 16)
            col(cols[:, 0:1], qkv_b[2 * D:3 * D])
            for i in range(3):
                col(cols[:, 1 + i:2 + i], in_proj_b[i * D:(i + 1) * D])
            col(cols[:, 4:5], ln1_g)
            col(cols[:, 5:6], ln1_b)
            col(cols[:, 6:7], ln2_g)
            col(l2b[:, :], ln2_b)
            for f in range(FT):
                col(l1b[:, f:f + 1], lin1_b[f * P:(f + 1) * P])
            for i, src in enumerate((sa_out_b, mha_out_b, ln3_b, ln1_g, ln1_b, ln2_g, ln2_b, lin2_b, ln3_g)):
                row(i, src)

            sp.dma_start(w1n[:, :, :], w1.rearrange("(c p) d -> p c d", p=P)).then_inc(ffn_loaded, 16)
            sp.dma_start(w2n[:, :, :].rearrange("p c k -> p (c k)"), w2).then_inc(ffn_loaded, 16)
            sp.dma_start(cwn[:, :, :], conv_w.rearrange("(c p) a k -> p c (a k)", p=P)).then_inc(ffn_loaded, 16)
            sp.dma_start(cbn[:, :], conv_b.partition_broadcast(P)).then_inc(ffn_loaded, 16)

        N_W = 2 + 4 + 2
        N_COL = 8 + FT
        N_ROW = 9
        ALL_LOADED = 16 * (N_W + N_COL + N_ROW)

        def norm_sems(tag):
            return [sem(f"{tag}_{what}") for what in ("stats", "step", "moments", "eps", "rstd", "normed")]

        def norm_tiles(stack, tag):
            return (sb(stack, f"{tag}_stats", [P, 2, GB, 6]), sb(stack, f"{tag}_sums", [P, 2, GB, 2]),
                    sb(stack, f"{tag}_diff", [P, 2, GB]), sb(stack, f"{tag}_diff2", [P, 2, GB]),
                    sb(stack, f"{tag}_mean", [P, 2, GB]), sb(stack, f"{tag}_var", [P, 2, GB]),
                    sb(stack, f"{tag}_vareps", [P, 2, GB]), sb(stack, f"{tag}_rstd", [P, 2, GB]))

        def norm_moments(v, g, slot, src, tiles, sems):
            stt, sums, diff, diff2, mean, var, _, _ = (t[:, slot] for t in tiles)
            stats, step, moments, _, _, _ = sems
            for b in range(GB):
                i = v.bn_stats(stt[:, b, :], src(b))
            i.then_inc(stats, 1)
            v.wait_ge(stats, g + 1)
            v.tensor_tensor(diff, stt[:, :, 1], stt[:, :, 4], ALU.subtract)
            v.tensor_tensor(sums, stt[:, :, 1:3], stt[:, :, 4:6], ALU.add).then_inc(step, 1)
            v.wait_ge(step, 2 * g + 1)
            v.tensor_scalar(mean, sums[:, :, 0], 0.5, None, ALU.mult)
            v.scalar_tensor_tensor(out=diff2, in0=diff, scalar=0.25, in1=diff, op0=ALU.mult, op1=ALU.mult)\
             .then_inc(step, 1)
            v.wait_ge(step, 2 * g + 2)
            v.scalar_tensor_tensor(out=var, in0=sums[:, :, 1], scalar=1.0 / D, in1=diff2,
                                   op0=ALU.mult, op1=ALU.add).then_inc(moments, 1)

        def norm_apply(v, g, slot, src, dst, tiles, sems):
            mean, rstd_t = tiles[4], tiles[7]
            v.wait_ge(sems[4], g + 1)
            for b in range(GB):
                i = v.tensor_scalar(dst(b), src(b), mean[:, slot, b:b + 1], rstd_t[:, slot, b:b + 1],
                                    ALU.subtract, ALU.mult)
            i.then_inc(sems[5], 1)

        def norm_pool(pool, g, slot, tiles, sems):
            var, vareps, rstd_t = tiles[5], tiles[6], tiles[7]
            _, _, moments, eps, rstd, normed = sems
            pool.wait_ge(moments, g + 1)
            if later(g, 2):
                pool.wait_ge(normed, g - 1)
            pool.tensor_tensor(vareps[:, slot, :], var[:, slot, :], eps_tile[:, :], ALU.add).then_inc(eps, 1)
            pool.wait_ge(eps, g + 1)
            pool.tensor_tensor(rstd_t[:, slot, :], vareps[:, slot, :], half_neg[:, :], ALU.pow).then_inc(rstd, 1)

        with ExitStack() as st:
            Wn = sb(st, "Wn", [P, P])
            WT = sb(st, "WT", [P, P])
            diag = sb(st, "diag", [P, 1])
            ctxs = sb(st, "ctxs", [M, 2, GB, D])
            ctxv = sb(st, "ctxv", [M, 2, GB, D])
            mski = sb(st, "mski", [P, 2, GB * M], I32)
            mskf = sb(st, "mskf", [P, 2, GB * M])
            xn = sb(st, "xn", [P, 2, GB, D])
            xT = sb(st, "xT", [P, 2, GT])
            cT = sb(st, "cT", [P, 2, GB * M])
            r1 = sb(st, "r1", [P, 2, GT])
            r2 = sb(st, "r2", [P, 2, GB * M])
            sc = sb(st, "sc", [P, 2, GB, M])
            mx = sb(st, "mx", [P, 2, GB])
            pr = sb(st, "pr", [P, 2, GB, M])
            sm = sb(st, "sm", [P, 2, GB])
            ri = sb(st, "ri", [P, 2, GB])
            rg = sb(st, "rg", [P, 2, GB])
            prT = sb(st, "prT", [M, 2, GT])
            ln = norm_tiles(st, "lnA")

            psX = [bank(st, f"a_psX{s}") for s in range(2)]
            psC = bank(st, "a_psC")
            psR1 = bank(st, "a_psR1")
            psR2 = bank(st, "a_psR2")
            psS = bank(st, "a_psS")
            psP = bank(st, "a_psP")
            psO = bank(st, "a_psO")

            w_loaded = sem("a_w_loaded")
            wT_done = sem("a_wT_done")
            wT_ready = sem("a_wT_ready")
            ctx_loaded = [sem("a_ctx_loaded_even"), sem("a_ctx_loaded_odd")]
            ctxv_loaded = [sem("a_ctxv_loaded_even"), sem("a_ctxv_loaded_odd")]
            mask_loaded = [sem("a_mask_loaded_even"), sem("a_mask_loaded_odd")]
            mask_ready = sem("a_mask_ready")
            lnA = norm_sems("a_ln")
            normed = lnA[-1]
            xT_done = sem("a_xT_done")
            xT_ready = sem("a_xT_ready")
            cT_done = sem("a_cT_done")
            cT_ready = sem("a_cT_ready")
            r1_done = sem("a_r1_done")
            r1_ready = sem("a_r1_ready")
            r2_done = sem("a_r2_done")
            r2_ready = sem("a_r2_ready")
            s_done = sem("a_scores_done")
            s_masked = sem("a_scores_masked")
            negmax_ready = sem("a_negmax_ready")
            p_ready = sem("a_probs_ready")
            inv_ready = sem("a_inv_ready")
            rg_ready = sem("a_gated_inv_ready")
            pT_done = sem("a_probsT_done")
            pT_ready = sem("a_probsT_ready")
            o_done = sem("a_out_done")
            x_ready = sem("a_x_ready")

            def over_groups(eng, first, second, group, last):
                def prepare(p):
                    first(0, 0, 0)
                    first(1, 0, 1)
                    second(0, 0)

                def work(p, ahead):
                    g, after = 2 * p, None if ahead is None else 2 * ahead
                    before = None if isinstance(p, int) and p == 0 else g - 1
                    group(g, 0, g + 1, after, before, p)
                    group(g + 1, 1, after, None if ahead is None else after + 1, g, p)

                over_pairs(eng, PAIRS, prepare, work, peeled=2)
                last(NG - 1, 1)

            with nc.Block() as block:
                @block.sync
                def _(sp):
                    sp.dma_start(Wn[:, :], W).then_inc(w_loaded, 16)
                    sp.dma_start(diag[:, :], diagonal.rearrange("(h a) -> h a", a=1)).then_inc(w_loaded, 16)
                    sp.dma_start(graw[:, 0:2], g_xattn.partition_broadcast(P)).then_inc(gates_loaded, 16)
                    sp.dma_start(graw[:, 2:4], g_ffn.partition_broadcast(P)).then_inc(gates_loaded, 16)

                    def load(g, p, slot):
                        if later(g, 2):
                            sp.wait_ge(x_loaded[slot], 16 * p)
                            sp.wait_ge(cT_done, g - 1)
                            sp.wait_ge(mask_ready, g - 1)
                        b0 = g * GB
                        sp.dma_start(X[:, bass.ds(b0, GB), :], x[bass.ds(b0, GB), :, :].rearrange("b s d -> s b d"))\
                          .then_inc(x_loaded[slot], 16)
                        sp.dma_start(ctxs[:, slot, :, :],
                                     ctx_tokens[bass.ds(b0, GB), :, :].rearrange("b m d -> m b d"))\
                          .then_inc(ctx_loaded[slot], 16)
                        sp.dma_start(mski[:, slot, :].rearrange("p (b m) -> p b m", b=GB),
                                     mask[bass.ds(b0, GB), :].partition_broadcast(P)).then_inc(mask_loaded[slot], 16)

                    def load_values(g, p, slot):
                        if later(g, 2):
                            sp.wait_ge(ctxv_loaded[slot], 16 * p)
                            sp.wait_ge(o_done, g - 1)
                        sp.dma_start(ctxv[:, slot, :, :],
                                     ctx_tokens[bass.ds(g * GB, GB), :, :].rearrange("b m d -> m b d"))\
                          .then_inc(ctxv_loaded[slot], 16)

                    def prepare(p):
                        for slot in range(2):
                            load(slot, 0, slot)

                    def work(p, ahead):
                        for slot in range(2):
                            if not (isinstance(p, int) and p == 0):
                                load_values(2 * p - 2 + slot, p - 1, slot)
                            if ahead is not None:
                                load(2 * ahead + slot, ahead, slot)
                        if ahead is None:
                            load_experts_weights(sp)

                    over_pairs(sp, PAIRS, prepare, work, peeled=2)
                    for slot in range(2):
                        load_values(NG - 2 + slot, PAIRS - 1, slot)

                @block.gpsimd
                def _(pool):
                    pool.memset(half_neg[:, :], -0.5).then_inc(const_filled, 1)
                    pool.memset(eps_tile[:, :], LN_EPS).then_inc(const_filled, 1)
                    pool.memset(ident[:, :], 0.0).then_inc(const_filled, 1)
                    pool.wait_ge(const_filled, 3)
                    pool.affine_select(out=ident[:, :], in_=ident[:, :], compare_op=ALU.not_equal, fill=1.0,
                                       base=0, pattern=[[-1, P]], channel_multiplier=1).then_inc(const_filled, 1)
                    pool.wait_ge(const_filled, 4)
                    pool.tensor_copy(ident_bf[:, :], ident[:, :]).then_inc(const_ready, 1)

                    def norm(g, p, slot):
                        norm_pool(pool, g, slot, ln, lnA)

                    def group(g, slot, nxt, nxt2, prv, p):
                        if nxt2 is not None:
                            norm(nxt2, p + 1, slot)

                    over_groups(pool, norm, lambda g, slot: None, group, lambda g, slot: None)

                @block.tensor
                def _(pe):
                    pe.wait_ge(const_ready, 1)
                    pe.wait_ge(w_loaded, 32)
                    pe.transpose(psR1[:, 0:P], Wn[:, :], ident[:, :]).then_inc(wT_done, 1)

                    def transposes(g, p, slot):
                        pe.wait_ge(normed, g + 1)
                        if later(g, 2):
                            pe.wait_ge(xT_ready, g - 1)
                        for b in range(GB):
                            i = pe.transpose(psX[slot][:, b * P:(b + 1) * P], xn[:, slot, b, :], ident[:, :])
                        i.then_inc(xT_done, 1)
                        pe.wait_ge(ctx_loaded[slot], 16 * (p + 1))
                        if later(g, 1):
                            pe.wait_ge(cT_ready, g)
                        for b in range(GB):
                            i = pe.transpose(psC[:, b * M:(b + 1) * M], ctxs[:, slot, b, :], ident[0:M, 0:M])
                        i.then_inc(cT_done, 1)

                    def projections(g, slot):
                        pe.wait_ge(xT_ready, g + 1)
                        if later(g, 1):
                            pe.wait_ge(r1_ready, g)
                        else:
                            pe.wait_ge(wT_ready, 1)
                        pe.matmul(psR1[:, :], WT[:, :], xT[:, slot, :], start=True, stop=True).then_inc(r1_done, 1)
                        pe.wait_ge(cT_ready, g + 1)
                        if later(g, 1):
                            pe.wait_ge(r2_ready, g)
                        pe.matmul(psR2[:, 0:GB * M], WT[:, :], cT[:, slot, :], start=True, stop=True)\
                          .then_inc(r2_done, 1)

                    def scores(g, slot):
                        pe.wait_ge(r1_ready, g + 1)
                        pe.wait_ge(r2_ready, g + 1)
                        if later(g, 1):
                            pe.wait_ge(s_masked, g)
                        for b in range(GB):
                            i = pe.matmul(psS[:, b * M:(b + 1) * M], r1[:, slot, b * P:(b + 1) * P],
                                          r2[:, slot, b * M:(b + 1) * M], start=True, stop=True)
                        i.then_inc(s_done, 1)

                    def probsT(g, slot):
                        pe.wait_ge(p_ready, GB * (g + 1))
                        if later(g, 1):
                            pe.wait_ge(pT_ready, g)
                        for b in range(GB):
                            i = pe.transpose(psP[0:M, b * P:(b + 1) * P], pr[:, slot, b, :], ident[:, :])
                        i.then_inc(pT_done, 1)

                    def attend(g, p, slot):
                        pe.wait_ge(pT_ready, g + 1)
                        pe.wait_ge(ctxv_loaded[slot], 16 * (p + 1))
                        if later(g, 1):
                            pe.wait_ge(x_ready, g)
                        for b in range(GB):
                            i = pe.matmul(psO[:, b * P:(b + 1) * P], prT[:, slot, b * P:(b + 1) * P],
                                          ctxv[:, slot, b, :], start=True, stop=True)
                        i.then_inc(o_done, 1)

                    def group(g, slot, nxt, nxt2, prv, p):
                        if prv is not None:
                            probsT(prv, 1 - slot)
                        scores(g, slot)
                        if prv is not None:
                            attend(prv, p - 1 if slot == 0 else p, 1 - slot)
                        if nxt is not None:
                            projections(nxt, 1 - slot)
                        if nxt2 is not None:
                            transposes(nxt2, p + 1, slot)

                    def last(g, slot):
                        probsT(g, slot)
                        attend(g, PAIRS - 1, slot)

                    over_groups(pe, transposes, projections, group, last)

                @block.scalar
                def _(act):
                    act.wait_ge(gates_loaded, 32)
                    act.activation(gates[:, :], graw[:, :], ACT.Tanh).then_inc(gates_ready, 1)
                    act.wait_ge(wT_done, 1)
                    act.activation(WT[:, :], psR1[:, 0:P], ACT.Copy).then_inc(wT_ready, 1)

                    def mask_copy(g, p, slot):
                        act.wait_ge(mask_loaded[slot], 16 * (p + 1))
                        if later(g, 2):
                            act.wait_ge(s_masked, g - 1)
                        act.activation(mskf[:, slot, :], mski[:, slot, :], ACT.Copy, scale=-1.0, bias=1.0)\
                           .then_inc(mask_ready, 1)

                    def copies(g, slot):
                        act.wait_ge(xT_done, g + 1)
                        if later(g, 2):
                            act.wait_ge(r1_done, g - 1)
                        act.activation(xT[:, slot, :], psX[slot][:, :], ACT.Copy).then_inc(xT_ready, 1)
                        act.wait_ge(cT_done, g + 1)
                        if later(g, 2):
                            act.wait_ge(r2_done, g - 1)
                        act.activation(cT[:, slot, :], psC[:, 0:GB * M], ACT.Copy).then_inc(cT_ready, 1)

                    def first(g, p, slot):
                        mask_copy(g, p, slot)
                        copies(g, slot)

                    def relu(g, slot):
                        act.wait_ge(r1_done, g + 1)
                        if later(g, 2):
                            act.wait_ge(s_done, g - 1)
                        act.activation(r1[:, slot, :], psR1[:, :], ACT.Relu).then_inc(r1_ready, 1)

                    def exps(g, slot):
                        act.wait_ge(negmax_ready, g + 1)
                        if later(g, 2):
                            act.wait_ge(pT_done, g - 1)
                            act.wait_ge(inv_ready, g - 1)
                        for b in range(GB):
                            act.activation(pr[:, slot, b, :], sc[:, slot, b, :], ACT.Exp,
                                           bias=mx[:, slot, b:b + 1], accum_out=sm[:, slot, b:b + 1])\
                               .then_inc(p_ready, 1)

                    def copy_probsT(g, slot):
                        act.wait_ge(pT_done, g + 1)
                        if later(g, 2):
                            act.wait_ge(o_done, g - 1)
                        act.activation(prT[:, slot, :], psP[0:M, :], ACT.Copy).then_inc(pT_ready, 1)

                    def group(g, slot, nxt, nxt2, prv, p):
                        if prv is not None:
                            copy_probsT(prv, 1 - slot)
                        exps(g, slot)
                        if nxt is not None:
                            relu(nxt, 1 - slot)
                        if nxt2 is not None:
                            mask_copy(nxt2, p + 1, slot)
                            copies(nxt2, slot)

                    over_groups(act, first, relu, group, copy_probsT)

                @block.vector
                def _(v):
                    def x_of(g, b):
                        return X[:, bass.ds(g * GB + b, 1), :].rearrange("p a d -> p (a d)")

                    def moments(g, p, slot):
                        v.wait_ge(x_loaded[slot], 16 * (p + 1))
                        norm_moments(v, g, slot, lambda b: x_of(g, b), ln, lnA)

                    def apply(g, slot):
                        if later(g, 2):
                            v.wait_ge(xT_done, g - 1)
                        norm_apply(v, g, slot, lambda b: x_of(g, b), lambda b: xn[:, slot, b, :], ln, lnA)

                    def first(g, p, slot):
                        moments(g, p, slot)
                        apply(g, slot)

                    def scaled_relu(g, slot):
                        v.wait_ge(r2_done, g + 1)
                        if later(g, 2):
                            v.wait_ge(s_done, g - 1)
                        v.tensor_scalar(r2[:, slot, :], psR2[:, 0:GB * M], 0.0, diag[:, 0:1], ALU.max, ALU.mult)\
                         .then_inc(r2_ready, 1)

                    def maxima(g, slot):
                        v.wait_ge(s_done, g + 1)
                        v.wait_ge(mask_ready, g + 1)
                        if later(g, 2):
                            v.wait_ge(p_ready, GB * (g - 1))
                        v.scalar_tensor_tensor(out=sc[:, slot, :, :].rearrange("p b m -> p (b m)"),
                                               in0=mskf[:, slot, :], scalar=NEG, in1=psS[:, 0:GB * M],
                                               op0=ALU.mult, op1=ALU.add).then_inc(s_masked, 1)
                        v.wait_ge(s_masked, g + 1)
                        v.tensor_reduce(mx[:, slot, :], sc[:, slot, :, :], AX.X, ALU.max, negate=True)\
                         .then_inc(negmax_ready, 1)

                    def inverse(g, slot):
                        v.wait_ge(p_ready, GB * (g + 1))
                        v.reciprocal(ri[:, slot, :], sm[:, slot, :]).then_inc(inv_ready, 1)
                        v.wait_ge(inv_ready, g + 1)
                        if not later(g, 1):
                            v.wait_ge(gates_ready, 1)
                        v.tensor_scalar(rg[:, slot, :], ri[:, slot, :], gates[:, 0:1], None, ALU.mult)\
                         .then_inc(rg_ready, 1)

                    def residual(g, slot):
                        v.wait_ge(o_done, g + 1)
                        v.wait_ge(rg_ready, g + 1)
                        for b in range(GB):
                            xb = x_of(g, b)
                            i = v.scalar_tensor_tensor(out=xb, in0=psO[:, b * P:(b + 1) * P],
                                                       scalar=rg[:, slot, b:b + 1], in1=xb,
                                                       op0=ALU.mult, op1=ALU.add)
                        i.then_inc(x_ready, 1)

                    def group(g, slot, nxt, nxt2, prv, p):
                        if nxt2 is not None:
                            moments(nxt2, p + 1, slot)
                        if prv is not None:
                            inverse(prv, 1 - slot)
                        maxima(g, slot)
                        if nxt2 is not None:
                            apply(nxt2, slot)
                        if prv is not None:
                            residual(prv, 1 - slot)
                        if nxt is not None:
                            scaled_relu(nxt, 1 - slot)

                    def last(g, slot):
                        inverse(g, slot)
                        residual(g, slot)

                    over_groups(v, first, scaled_relu, group, last)

        end_phase()

        with ExitStack() as st:
            rows = [min(P, SH - j * P) for j in range(ST)] + [P] * ET
            HS = NT // 2
            VECTOR_LOW = (8, 9, 10)
            POOL_LOW = [j for j in range(NT) if j not in VECTOR_LOW]
            LAG = 4
            DOWN_PARTS = [(slice(0, ST - 1), P), (slice(ST - 1, ST), rows[ST - 1]), (slice(ST, NT), P)]

            wh = sb(st, "wh", [P, 2, NT * P], F32R)
            wl = sb(st, "wl", [P, 2, NT * P], F32R)
            dh = sb(st, "dh", [P, NT, D], F32R)
            dl = sb(st, "dl", [P, NT, D], F32R)
            gwh = sb(st, "gwh", [P, P], F32R)
            gwl = sb(st, "gwl", [P, P], F32R)
            gwz = sb(st, "gwz", [P, P])
            sel = sb(st, "sel", [PARTS * E, EH], BF16)
            ebase = sb(st, "ebase", [P, E])

            xn = sb(st, "b_xn", [P, GB, D])
            xh = sb(st, "b_xh", [P, 2, GT], F32R)
            xl = sb(st, "b_xl", [P, 2, GT], F32R)
            lgT = sb(st, "b_lgT", [P, GT])
            lg = sb(st, "b_lg", [P, GB, E])
            m1 = sb(st, "b_m1", [P, GB])
            dif = sb(st, "b_dif", [P, GB, E])
            f1 = sb(st, "b_f1", [P, GB, E])
            q1 = sb(st, "b_q1", [P, GB])
            k1 = sb(st, "b_k1", [P, GB, E])
            d2 = sb(st, "b_d2", [P, GB, E])
            m2 = sb(st, "b_m2", [P, GB])
            e2 = sb(st, "b_e2", [P, GB, E])
            f2 = sb(st, "b_f2", [P, GB, E])
            q2 = sb(st, "b_q2", [P, GB])
            k2 = sb(st, "b_k2", [P, GB, E])
            kk = sb(st, "b_kk", [P, GB, E])
            ex = sb(st, "b_ex", [P, GB, E])
            em = sb(st, "b_em", [P, GB, E])
            se = sb(st, "b_se", [P, GB])
            sz = sb(st, "b_sz", [P, GB])
            den = sb(st, "b_den", [P, GB])
            rd = sb(st, "b_rd", [P, GB])
            wt = sb(st, "b_wt", [P, GB, E])
            wr = sb(st, "b_wr", [P, GB, E])
            w3 = sb(st, "b_w3", [P, GB, PARTS, E], BF16)
            w3T = sb(st, "b_w3T", [PARTS * E, 2, GT], BF16)
            sg = sb(st, "b_sg", [P, 2, GT])
            mu = sb(st, "b_mu", [P, HS, GT])
            hf = sb(st, "b_hf", [P, HS, GT])
            hh = sb(st, "b_hh", [P, HS, GT], F32R)
            hl = sb(st, "b_hl", [P, HS, GT], F32R)
            ysb = sb(st, "b_ysb", [P, GT])
            ln = norm_tiles(st, "lnB")

            psG = [bank(st, f"b_psG{s}") for s in range(2)]
            psU = [bank(st, f"b_psU{s}") for s in range(2)]
            psW = bank(st, "b_psW")
            psY = bank(st, "b_psY")
            psT = bank(st, "b_psT")
            psL = bank(st, "b_psL")
            psW3 = psL[:, 256:512].bitcast(BF16)

            uph_ready = sem("b_up_upper_ready")
            upl_ready = sem("b_up_lower_ready")
            dnh_ready = sem("b_down_upper_ready")
            dnl_ready = sem("b_down_lower_ready")
            gwT_done = sem("b_gwT_done")
            gwz_ready = sem("b_gwz_ready")
            gwh_ready = sem("b_gwh_ready")
            gwl_ready = sem("b_gwl_ready")
            sel_ready = sem("b_sel_ready")
            ebase_ready = sem("b_ebase_ready")
            lnB = norm_sems("b_ln")
            normed = lnB[-1]
            xT_done = sem("b_xT_done")
            xh_ready = sem("b_xh_ready")
            xl_ready = sem("b_xl_ready")
            lgT_done = sem("b_logitsT_done")
            lgT_ready = sem("b_logitsT_ready")
            lg_done = sem("b_logits_done")
            dif_ready = sem("b_dif_ready")
            ex_ready = sem("b_exp_ready")
            pick = sem("b_pick_step")
            split_step = sem("b_split_step")
            w3_ready = sem("b_w3_ready")
            w3T_done = sem("b_w3T_done")
            w3T_ready = sem("b_w3T_ready")
            g_done = sem("b_gate_done")
            u_done = sem("b_up_done")
            wb_done = sem("b_weight_done")
            sg_ready = sem("b_silu_ready")
            mu_ready = sem("b_mul_ready")
            hf_ready = sem("b_hidden_ready")
            hh_ready = sem("b_hidden_upper_ready")
            hlp_ready = sem("b_hidden_lower_pool_ready")
            hlv_ready = sem("b_hidden_lower_vector_ready")
            dn_done = sem("b_down_done")
            y_ready = sem("b_y_ready")
            yb_done = sem("b_y_back_done")
            x_ready = sem("b_x_ready")

            def wait_split(eng, g, j):
                if j in VECTOR_LOW:
                    eng.wait_ge(hlv_ready, len(VECTOR_LOW) * g + VECTOR_LOW.index(j) + 1)
                else:
                    eng.wait_ge(hlp_ready, len(POOL_LOW) * g + POOL_LOW.index(j) + 1)

            def wait_slot_split(eng, g, j):
                if j >= HS:
                    wait_split(eng, g, j - HS)
                elif later(g, 1):
                    wait_split(eng, g - 1, j + HS)

            def lower(eng, g, j, ready):
                n, m, q = NT * g + j, rows[j], j % HS
                eng.wait_ge(hh_ready, n + 1)
                if j >= HS or later(g, 1):
                    eng.wait_ge(dn_done, n - HS + 1)
                eng.tensor_tensor(hl[0:m, q, :], hf[0:m, q, :], hh[0:m, q, :].bitcast(F32),
                                  ALU.subtract).then_inc(ready, 1)

            def over_groups(eng, prep, group, tail):
                def prepare(p):
                    prep(0)

                def work(p, ahead):
                    group(2 * p, 0, 2 * p + 1, 1)
                    group(2 * p + 1, 1, None if ahead is None else 2 * ahead, 0)

                over_pairs(eng, PAIRS, prepare, work)
                tail()

            with nc.Block() as block:
                @block.sync
                def _(sp):
                    load_layer1_weights(sp)

                @block.tensor
                def _(pe):
                    pe.wait_ge(router_loaded, 32)
                    pe.transpose(psL[:, 0:E], gwn[:, :], ident[0:E, 0:E]).then_inc(gwT_done, 1)

                    def x_transposes(g):
                        pe.wait_ge(normed, g + 1)
                        if later(g, 1):
                            pe.wait_ge(xl_ready, g)
                        if later(g, 3):
                            pe.wait_ge(x_ready, g - 2)
                        for b in range(GB):
                            i = pe.transpose(psT[:, b * P:(b + 1) * P], xn[:, b, :], ident[:, :])
                        i.then_inc(xT_done, 1)

                    def logits(g, slot):
                        if not later(g, 1):
                            pe.wait_ge(gwh_ready, 1)
                            pe.wait_ge(gwl_ready, 1)
                        pe.wait_ge(xh_ready, g + 1)
                        pe.wait_ge(xl_ready, g + 1)
                        if later(g, 1):
                            pe.wait_ge(w3T_ready, g)
                        pe.matmul(psL[:, :], gwh[:, :], xl[:, slot, :], start=True, stop=False)
                        pe.matmul(psL[:, :], gwl[:, :], xh[:, slot, :], start=False, stop=False)
                        pe.matmul(psL[:, :], gwh[:, :], xh[:, slot, :], start=False, stop=True).then_inc(lgT_done, 1)

                    def logits_back(g):
                        pe.wait_ge(lgT_ready, g + 1)
                        for b in range(GB):
                            i = pe.transpose(psL[:, b * P:(b + 1) * P], lgT[:, b * P:(b + 1) * P], ident[:, :])
                        i.then_inc(lg_done, 1)

                    def weight_transposes(g):
                        pe.wait_ge(w3_ready, g + 1)
                        for b in range(GB):
                            i = pe.transpose(psW3[0:PARTS * E, b * P:(b + 1) * P],
                                             w3[:, b, :, :].rearrange("p a e -> p (a e)"), ident_bf[:, :])
                        i.then_inc(w3T_done, 1)

                    def prep(g):
                        x_transposes(g)
                        logits(g, 0)
                        logits_back(g)

                    def spread(g, j, slot):
                        e = j - ST
                        if e == 0:
                            pe.wait_ge(w3T_ready, g + 1)
                            if not later(g, 1):
                                pe.wait_ge(sel_ready, 1)
                        if e > 0 or later(g, 1):
                            pe.wait_ge(hf_ready, ET * g + e)
                        pe.matmul(psW[:, :], sel[:, e * P:(e + 1) * P], w3T[:, slot, :],
                                  start=True, stop=True).then_inc(wb_done, 1)

                    def down(g, j):
                        n, m, q = NT * g + j, rows[j], j % HS
                        pe.wait_ge(hh_ready, n + 1)
                        wait_split(pe, g, j)
                        if j == 0:
                            if later(g, 1):
                                pe.wait_ge(y_ready, g)
                            else:
                                pe.wait_ge(dnl_ready, 1)
                        pe.matmul(psY[:, :], dh[0:m, j, :], hl[0:m, q, :], start=(j == 0), stop=False)
                        pe.matmul(psY[:, :], dl[0:m, j, :], hh[0:m, q, :], start=False, stop=False)
                        pe.matmul(psY[:, :], dh[0:m, j, :], hh[0:m, q, :], start=False, stop=(j == NT - 1))\
                          .then_inc(dn_done, 1)

                    def y_back(g, bank_free, count):
                        pe.wait_ge(y_ready, g + 1)
                        pe.wait_ge(bank_free, count)
                        for b in range(GB):
                            i = pe.transpose(psT[:, b * P:(b + 1) * P], ysb[:, b * P:(b + 1) * P], ident[:, :])
                        i.then_inc(yb_done, 1)

                    def group(g, slot, nxt, nslot):
                        for j in range(NT):
                            n, m = NT * g + j, rows[j]
                            cols = slice(j * P, j * P + m)
                            if j == 0:
                                pe.wait_ge(xh_ready, g + 1)
                                pe.wait_ge(xl_ready, g + 1)
                            if not later(g, 1):
                                pe.wait_ge(uph_ready, j + 1)
                                pe.wait_ge(upl_ready, j + 1)
                            if j >= 2 or later(g, 1):
                                pe.wait_ge(sg_ready, n - 1)
                            for k, ps in enumerate((psG[j % 2], psU[j % 2])):
                                if k == 1 and (j >= 2 or later(g, 1)):
                                    pe.wait_ge(mu_ready, n - 1)
                                pe.matmul(ps[0:m, :], wh[:, k, cols], xl[:, slot, :], start=True, stop=False)
                                pe.matmul(ps[0:m, :], wl[:, k, cols], xh[:, slot, :], start=False, stop=False)
                                pe.matmul(ps[0:m, :], wh[:, k, cols], xh[:, slot, :], start=False, stop=True)\
                                  .then_inc((g_done, u_done)[k], 1)
                            if j > ST:
                                spread(g, j - 1, slot)
                            elif j == 0 and later(g, 1):
                                spread(g - 1, NT - 1, 1 - slot)
                            if j >= LAG:
                                down(g, j - LAG)
                            elif later(g, 1):
                                down(g - 1, NT - LAG + j)
                            if j == 3:
                                weight_transposes(g)
                            if j == 5 and nxt is not None:
                                x_transposes(nxt)
                            if j == 7 and later(g, 1):
                                if nxt is None:
                                    y_back(g - 1, x_ready, g - 1)
                                else:
                                    y_back(g - 1, xl_ready, g + 2)
                            if nxt is not None:
                                if j == 7:
                                    logits(nxt, nslot)
                                if j == 8:
                                    logits_back(nxt)

                    def tail():
                        spread(NG - 1, NT - 1, 1)
                        for j in range(NT - LAG, NT):
                            down(NG - 1, j)
                        y_back(NG - 1, x_ready, NG - 1)

                    over_groups(pe, prep, group, tail)

                @block.scalar
                def _(act):
                    act.wait_ge(gwz_ready, 2)
                    act.activation(gwh[:, :], gwz[:, :], ACT.Copy).then_inc(gwh_ready, 1)
                    act.wait_ge(up_loaded, 64)
                    for j in range(NT):
                        cols = slice(j * P, j * P + rows[j])
                        act.activation(wh[:, :, cols], wn[:, :, cols], ACT.Copy).then_inc(uph_ready, 1)
                    act.wait_ge(down_loaded, 48)
                    for tiles, m in DOWN_PARTS:
                        i = act.activation(dh[0:m, tiles, :], dn[0:m, tiles, :], ACT.Copy)
                    i.then_inc(dnh_ready, 1)

                    def x_upper(g, slot):
                        act.wait_ge(xT_done, g + 1)
                        if later(g, 2):
                            act.wait_ge(u_done, NT * (g - 1))
                        act.activation(xh[:, slot, :], psT[:, :], ACT.Copy).then_inc(xh_ready, 1)

                    def logits_copy(g):
                        act.wait_ge(lgT_done, g + 1)
                        act.activation(lgT[:, :], psL[:, :], ACT.Copy).then_inc(lgT_ready, 1)

                    def weights_copy(g, slot):
                        act.wait_ge(w3T_done, g + 1)
                        if later(g, 2):
                            act.wait_ge(wb_done, ET * (g - 1))
                        act.activation(w3T[:, slot, :], psW3[0:PARTS * E, :], ACT.Copy).then_inc(w3T_ready, 1)

                    def prep(g):
                        x_upper(g, 0)
                        logits_copy(g)
                        act.wait_ge(sel_loaded, 16)
                        act.activation(sel[:, :], seln[:, :], ACT.Copy).then_inc(sel_ready, 1)

                    def upper(g, j):
                        n, m, q = NT * g + j, rows[j], j % HS
                        if j < ST:
                            act.wait_ge(mu_ready, n + 1)
                        else:
                            act.wait_ge(hf_ready, ET * g + j - ST + 1)
                        if j >= HS or later(g, 1):
                            act.wait_ge(dn_done, n - HS + 1)
                        act.activation(hh[0:m, q, :], hf[0:m, q, :], ACT.Copy).then_inc(hh_ready, 1)

                    def y_copy(g):
                        act.wait_ge(dn_done, NT * (g + 1))
                        if later(g, 1):
                            act.wait_ge(yb_done, g)
                        act.activation(ysb[:, :], psY[:, :], ACT.Copy, scale=gates[:, 2:3]).then_inc(y_ready, 1)

                    def group(g, slot, nxt, nslot):
                        for j in range(NT):
                            n, m = NT * g + j, rows[j]
                            act.wait_ge(g_done, n + 1)
                            if j >= 2 or later(g, 1):
                                act.wait_ge(mu_ready, n - 1)
                            act.activation(sg[0:m, j % 2, :], psG[j % 2][0:m, :], ACT.Silu).then_inc(sg_ready, 1)
                            if j >= 2:
                                upper(g, j - 2)
                            elif later(g, 1):
                                upper(g - 1, NT - 2 + j)
                            if j == 3:
                                weights_copy(g, slot)
                            if j == 3 and later(g, 1):
                                y_copy(g - 1)
                            if nxt is not None:
                                if j == 5:
                                    x_upper(nxt, nslot)
                                if j == 7:
                                    logits_copy(nxt)

                    def tail():
                        upper(NG - 1, NT - 2)
                        upper(NG - 1, NT - 1)
                        y_copy(NG - 1)

                    over_groups(act, prep, group, tail)

                @block.gpsimd
                def _(pool):
                    pool.memset(ebase[:, :], math.e).then_inc(ebase_ready, 1)

                    EXP_STEPS = (7, 8, 9, 10)

                    def exps(g, b):
                        if b == 0:
                            pool.wait_ge(dif_ready, g + 1)
                            if later(g, 1):
                                pool.wait_ge(w3_ready, g)
                        pool.tensor_tensor(ex[:, b, :], ebase[:, :], dif[:, b, :], ALU.pow).then_inc(ex_ready, 1)

                    def prep(g):
                        pool.wait_ge(ebase_ready, 1)
                        norm_pool(pool, g, 0, ln, lnB)
                        for b in range(GB):
                            exps(g, b)

                    def group(g, slot, nxt, nslot):
                        for j in range(NT):
                            if j in POOL_LOW:
                                lower(pool, g, j, hlp_ready)
                            if nxt is not None:
                                if j == 0:
                                    norm_pool(pool, nxt, nslot, ln, lnB)
                                for b in range(GB):
                                    if j == EXP_STEPS[b]:
                                        exps(nxt, b)

                    over_groups(pool, prep, group, lambda: None)

                @block.vector
                def _(v):
                    v.memset(gwz[:, :], 0.0).then_inc(gwz_ready, 1)
                    v.wait_ge(gwz_ready, 1)
                    v.wait_ge(gwT_done, 1)
                    v.tensor_copy(gwz[:, 0:E], psL[:, 0:E]).then_inc(gwz_ready, 1)
                    v.wait_ge(gwh_ready, 1)
                    v.tensor_tensor(gwl[:, :], gwz[:, :], gwh[:, :].bitcast(F32), ALU.subtract).then_inc(gwl_ready, 1)

                    def x_of(g, b):
                        return X[:, bass.ds(g * GB + b, 1), :].rearrange("p a d -> p (a d)")

                    def moments(g, slot):
                        norm_moments(v, g, slot, lambda b: x_of(g, b), ln, lnB)

                    def apply(g, slot):
                        if later(g, 1):
                            v.wait_ge(xT_done, g)
                        norm_apply(v, g, slot, lambda b: x_of(g, b), lambda b: xn[:, b, :], ln, lnB)

                    def x_lower(g, slot):
                        v.wait_ge(xh_ready, g + 1)
                        if later(g, 2):
                            v.wait_ge(u_done, NT * (g - 1))
                        v.tensor_tensor(xl[:, slot, :], psT[:, :], xh[:, slot, :].bitcast(F32), ALU.subtract)\
                         .then_inc(xl_ready, 1)

                    def wide(t):
                        return t[:, :].unsqueeze(2).broadcast_to([P, GB, E])

                    ramp4 = ramp[:, :].unsqueeze(1).broadcast_to([P, GB, E])
                    STEPS = 18

                    def differences(g):
                        v.wait_ge(lg_done, g + 1)
                        v.tensor_copy(lg[:, :, :], psL[:, :].rearrange("p (b e) -> p b e", b=GB)[:, :, 0:E])\
                         .then_inc(pick, 1)
                        v.wait_ge(pick, STEPS * g + 1)
                        v.tensor_reduce(m1[:, :], lg[:, :, :], AX.X, ALU.max).then_inc(pick, 1)
                        v.wait_ge(pick, STEPS * g + 2)
                        if later(g, 1):
                            v.wait_ge(ex_ready, GB * g)
                        v.tensor_tensor(dif[:, :, :], lg[:, :, :], wide(m1), ALU.subtract).then_inc(dif_ready, 1)

                    def pick_first(g):
                        v.wait_ge(dif_ready, g + 1)
                        v.scalar_tensor_tensor(out=f1[:, :, :], in0=dif[:, :, :], scalar=0.0, in1=ramp4,
                                               op0=ALU.is_equal, op1=ALU.mult).then_inc(pick, 1)
                        v.wait_ge(pick, STEPS * g + 3)
                        v.tensor_reduce(q1[:, :], f1[:, :, :], AX.X, ALU.max).then_inc(pick, 1)
                        v.wait_ge(pick, STEPS * g + 4)
                        v.tensor_tensor(k1[:, :, :], f1[:, :, :], wide(q1), ALU.is_equal).then_inc(pick, 1)
                        v.wait_ge(pick, STEPS * g + 5)
                        v.scalar_tensor_tensor(out=d2[:, :, :], in0=k1[:, :, :], scalar=-3e38, in1=dif[:, :, :],
                                               op0=ALU.mult, op1=ALU.add).then_inc(pick, 1)

                    def pick_second(g):
                        v.wait_ge(pick, STEPS * g + 6)
                        v.tensor_reduce(m2[:, :], d2[:, :, :], AX.X, ALU.max).then_inc(pick, 1)
                        v.wait_ge(pick, STEPS * g + 7)
                        v.tensor_tensor(e2[:, :, :], d2[:, :, :], wide(m2), ALU.is_equal).then_inc(pick, 1)
                        v.wait_ge(pick, STEPS * g + 8)
                        v.tensor_tensor(f2[:, :, :], e2[:, :, :], ramp4, ALU.mult).then_inc(pick, 1)
                        v.wait_ge(pick, STEPS * g + 9)
                        v.tensor_reduce(q2[:, :], f2[:, :, :], AX.X, ALU.max).then_inc(pick, 1)
                        v.wait_ge(pick, STEPS * g + 10)
                        v.tensor_tensor(k2[:, :, :], f2[:, :, :], wide(q2), ALU.is_equal).then_inc(pick, 1)
                        v.wait_ge(pick, STEPS * g + 11)
                        v.tensor_tensor(kk[:, :, :], k1[:, :, :], k2[:, :, :], ALU.add).then_inc(pick, 1)

                    def routing(g):
                        v.wait_ge(ex_ready, GB * (g + 1))
                        v.wait_ge(pick, STEPS * g + 12)
                        v.tensor_tensor(em[:, :, :], ex[:, :, :], kk[:, :, :], ALU.mult)
                        v.tensor_reduce(sz[:, :], ex[:, :, :], AX.X, ALU.add).then_inc(pick, 1)
                        v.wait_ge(pick, STEPS * g + 13)
                        v.tensor_reduce(se[:, :], em[:, :, :], AX.X, ALU.add).then_inc(pick, 1)
                        v.wait_ge(pick, STEPS * g + 14)
                        v.scalar_tensor_tensor(out=den[:, :], in0=sz[:, :], scalar=1e-20, in1=se[:, :],
                                               op0=ALU.mult, op1=ALU.add).then_inc(pick, 1)
                        v.wait_ge(pick, STEPS * g + 15)
                        v.reciprocal(rd[:, :], den[:, :]).then_inc(pick, 1)
                        v.wait_ge(pick, STEPS * g + 16)
                        v.tensor_tensor(wt[:, :, :], em[:, :, :], wide(rd), ALU.mult).then_inc(pick, 1)
                        v.wait_ge(pick, STEPS * g + 17)
                        if later(g, 1):
                            v.wait_ge(w3T_done, g)
                        v.tensor_copy(w3[:, :, 0, :], wt[:, :, :]).then_inc(pick, 1)
                        v.wait_ge(pick, STEPS * g + 18)

                    def routing_parts(g):
                        v.tensor_tensor(wr[:, :, :], wt[:, :, :], w3[:, :, 0, :], ALU.subtract).then_inc(split_step, 1)
                        v.wait_ge(split_step, 2 * g + 1)
                        v.tensor_copy(w3[:, :, 1, :], wr[:, :, :]).then_inc(split_step, 1)
                        v.wait_ge(split_step, 2 * g + 2)
                        v.tensor_tensor(w3[:, :, 2, :], wr[:, :, :], w3[:, :, 1, :], ALU.subtract).then_inc(w3_ready, 1)

                    def up_lower(tiles):
                        for j in tiles:
                            cols = slice(j * P, j * P + rows[j])
                            v.wait_ge(uph_ready, j + 1)
                            v.tensor_tensor(wl[:, :, cols], wn[:, :, cols], wh[:, :, cols].bitcast(F32),
                                            ALU.subtract).then_inc(upl_ready, 1)

                    def prep(g):
                        moments(g, 0)
                        up_lower(range(0, 8))
                        apply(g, 0)
                        x_lower(g, 0)
                        up_lower(range(8, NT))
                        differences(g)
                        pick_first(g)
                        pick_second(g)
                        v.wait_ge(dnh_ready, 1)
                        for tiles, m in DOWN_PARTS:
                            i = v.tensor_tensor(dl[0:m, tiles, :], dn[0:m, tiles, :], dh[0:m, tiles, :].bitcast(F32),
                                                ALU.subtract)
                        i.then_inc(dnl_ready, 1)

                    def add_y(g):
                        v.wait_ge(yb_done, g + 1)
                        xg = X[:, bass.ds(g * GB, GB), :].rearrange("p b d -> p (b d)")
                        v.tensor_tensor(xg, psT[:, :], xg, ALU.add).then_inc(x_ready, 1)

                    def weighted(g, j):
                        n, e, q = NT * g + j, ET * g + j - ST, j % HS
                        v.wait_ge(mu_ready, n + 1)
                        v.wait_ge(wb_done, e + 1)
                        wait_slot_split(v, g, j)
                        v.tensor_tensor(hf[:, q, :], psW[:, :], mu[:, q, :], ALU.mult).then_inc(hf_ready, 1)

                    def group(g, slot, nxt, nslot):
                        for j in range(NT):
                            n, m, q = NT * g + j, rows[j], j % HS
                            v.wait_ge(u_done, n + 1)
                            v.wait_ge(sg_ready, n + 1)
                            if j < ST:
                                wait_slot_split(v, g, j)
                            elif j >= ST + HS:
                                v.wait_ge(hf_ready, ET * g + j - ST - HS + 1)
                            elif j >= ST and later(g, 1):
                                v.wait_ge(hf_ready, ET * g + j - HS + 1)
                            v.tensor_tensor((hf if j < ST else mu)[0:m, q, :],
                                            psU[j % 2][0:m, :], sg[0:m, j % 2, :], ALU.mult).then_inc(mu_ready, 1)
                            if j > ST:
                                weighted(g, j - 1)
                            elif j == 0 and later(g, 1):
                                weighted(g - 1, NT - 1)
                            if j == 0 and later(g, 1):
                                pick_second(g)
                            if j == 1:
                                routing(g)
                                routing_parts(g)
                            if j == 8 and later(g, 1):
                                add_y(g - 1)
                            if nxt is not None:
                                if j == 2:
                                    moments(nxt, nslot)
                                if j == 4:
                                    apply(nxt, nslot)
                                if j == 5:
                                    x_lower(nxt, nslot)
                                if j == 9:
                                    differences(nxt)
                                if j == 10:
                                    pick_first(nxt)
                            if j - 3 in VECTOR_LOW:
                                lower(v, g, j - 3, hlv_ready)

                    def tail():
                        weighted(NG - 1, NT - 1)
                        add_y(NG - 1)

                    over_groups(v, prep, group, tail)

        end_phase()

        weights_b.close()

        BIG = 1.5 * 2.0 ** 23
        QMAX = 127.0
        W_COUNT = float(HW * D)
        asum = sb(top, "d_asum", [P, 2])
        ones = sb(top, "d_ones", [P, P])
        ones_bf = sb(top, "d_ones_bf", [P, P], BF16)
        mean = sb(top, "d_mean", [P, 2])
        rmean = sb(top, "d_rmean", [P, 2])
        ta = sb(top, "d_ta", [P, 2, HW])
        w1k = sb(top, "d_w1k", [P, TAPS, HC, D])
        wkh = sb(top, "d_wkh", [P, TAPS, HW], F32R)
        wkl = sb(top, "d_wkl", [P, TAPS, HW], F32R)
        w2T = sb(top, "d_w2T", [P, HC, P], BF16)
        cb1 = sb(top, "d_cb1", [P, HW], BF16)
        cr1, cm1 = (t[:, :, :].rearrange("p c d -> p (c d)") for t in (w1n, w2n))
        cb2 = sb(top, "d_cb2", [P, HW], BF16)
        cb = sb(top, "d_cb", [P, HW], BF16)
        sw2 = sb(top, "d_sw2", [P, 1])
        big = sb(top, "d_big", [P, HW])
        prepv = sem("d_vector_prepared")
        step = sem("d_prepare_step")
        ones_ready = sem("d_ones_ready")
        sums_done = sem("d_sums_done")
        wk_done = sem("d_wk_done")
        wkh_ready = sem("d_wk_upper_ready")
        wkl_ready = sem("d_wk_lower_ready")
        w2T_ready = sem("d_w2T_ready")
        sems_of_phase.clear()

        with ExitStack() as st:
            H = 8
            HD = D // H
            HM = H * M
            HB = HM // 2

            NC = -(-HM // P)
            assert NC == 5
            chunk = [min(P, HM - c * P) for c in range(NC)]
            PIECES = []
            for h in range(H):
                m = 0
                while m < M:
                    c, row = divmod(h * M + m, P)
                    PIECES.append((h, m, min(M - m, P - row), c, row))
                    m += PIECES[-1][2]
            Q_SCALE = HD ** -0.5

            tr = sb(st, "c_tr", [P, 6, D])
            l1T = sb(st, "c_l1T", [P, FT, P])
            l1g = sb(st, "c_l1g", [P, FT, P])
            l2T = sb(st, "c_l2T", [P, FT, P])
            qg = sb(st, "c_qg", [P, D])
            m1t = sb(st, "c_m1t", [P, D])
            bvb = sb(st, "c_bvb", [P, 2, P])
            y1b = sb(st, "c_y1b", [P, D])
            r1b = sb(st, "c_r1b", [P, D])
            r1b0 = sb(st, "c_r1b0", [P, D])
            r2b = sb(st, "c_r2b", [P, D])
            g3 = sb(st, "c_g3", [P, D])
            b3 = sb(st, "c_b3", [P, D])
            bq2 = sb(st, "c_bq2", [P, 1])
            bq3 = sb(st, "c_bq3", [P, 1])
            l1b2 = sb(st, "c_l1b2", [P, FT])
            SAO, MHO, L1B, G1, B1, G2, B2, L2B = range(8)

            ctxs = sb(st, "c_ctxs", [M, 2, GB, D])
            xn = sb(st, "c_xn", [P, GB, D])
            xT = sb(st, "c_xT", [P, GT])
            y1 = sb(st, "c_y1", [P, GB, D])
            n1 = sb(st, "c_n1", [P, GB, D])
            n1T = sb(st, "c_n1T", [P, GT])
            r1 = sb(st, "c_r1", [P, 2, GB, D])
            cT = sb(st, "c_cT", [P, GB * M])
            qT = sb(st, "c_qT", [P, 2, GT])
            kT = sb(st, "c_kT", [P, GB * M])
            kbd = sb(st, "c_kbd", [P, 2, GB, HM])
            vs = sb(st, "c_vs", [M, GB, D])
            vp = sb(st, "c_vp", [P, 2, GB, NC, D])
            sc = sb(st, "c_sc", [P, 2, H, M])
            mx = sb(st, "c_mx", [P, 2, H])
            pr = sb(st, "c_pr", [P, 2, H, M])
            sm = sb(st, "c_sm", [P, 2, H])
            iv = sb(st, "c_iv", [P, 2, H])
            pn = sb(st, "c_pn", [P, 2, H, M])
            pT = sb(st, "c_pT", [P, 2, NC, P])
            ca = sb(st, "c_ca", [P, 2, GT])
            y2 = sb(st, "c_y2", [P, GB, D])
            n2 = sb(st, "c_n2", [P, GB, D])
            n2T = sb(st, "c_n2T", [P, GT])
            r2 = sb(st, "c_r2", [P, GB, D])
            hT = sb(st, "c_hT", [P, FT, GT])
            y3 = sb(st, "c_y3", [P, GB, D])
            n3 = sb(st, "c_n3", [P, GB, D])
            o3 = sb(st, "c_o3", [P, GB, D])
            lns = [norm_tiles(st, f"c_ln{i}") for i in range(4)]

            psS = st.enter_context(nc.psum_tensor("c_psS", [P, 2, 512], F32))
            psP = st.enter_context(nc.psum_tensor("c_psP", [P, 2, 512], F32))
            psO = bank(st, "c_psO")
            psPrep = [psS[:, 0, :], psS[:, 1, :], psP[:, 0, :], psP[:, 1, :]]
            bA = bank(st, "c_bA")
            bB = bank(st, "c_bB")
            bC = bank(st, "c_bC")

            zeroed = sem("c_zeroed")
            kbd0_zeroed = sem("c_kbd0_zeroed")
            wT_done = sem("c_wT_done")
            wT_ready = sem("c_wT_ready")
            fold_done = sem("c_fold_done")
            bvb_ready = sem("c_bvb_ready")
            rowsum_step = sem("c_rowsum_step")
            consts_ready = sem("c_consts_ready")
            ctx_loaded = [sem("c_ctx_loaded_even"), sem("c_ctx_loaded_odd")]
            kbd_loaded = [sem("c_kbd_loaded_even"), sem("c_kbd_loaded_odd")]
            vp_loaded = [sem("c_vp_loaded_even"), sem("c_vp_loaded_odd")]
            sems = [norm_sems(f"c_ln{i}") for i in range(4)]
            n0_ready, n1_ready, n2_ready, n3_ready = (s[-1] for s in sems)
            t0_done, t0_ready = sem("c_t0_done"), sem("c_t0_ready")
            y1_done, y1_ready = sem("c_y1_done"), sem("c_y1_ready")
            c_done, c_ready = sem("c_ctxT_done"), sem("c_ctxT_ready")
            k_done, k_ready = sem("c_k_done"), sem("c_k_ready")
            v_done, v_ready = sem("c_v_done"), sem("c_v_ready")
            t1_done, t1_ready = sem("c_t1_done"), sem("c_t1_ready")
            q_done, q_ready = sem("c_q_done"), sem("c_q_ready")
            s_done, s_ready = sem("c_scores_done"), sem("c_scores_ready")
            mx_ready = sem("c_max_ready")
            exp_ready = sem("c_exp_ready")
            sum_ready = sem("c_sum_ready")
            inv_ready = sem("c_inv_ready")
            pn_ready = sem("c_probs_ready")
            tp_done, tp_ready = sem("c_probsT_done"), sem("c_probsT_ready")
            pv_done, ca_ready = sem("c_pv_done"), sem("c_ca_ready")
            out_done, y2_ready = sem("c_out_done"), sem("c_y2_ready")
            t2_done, t2_ready = sem("c_t2_done"), sem("c_t2_ready")
            l1_done = sem("c_lin1_done")
            l1_ready = sem("c_lin1_ready")
            l2_done, y3_ready = sem("c_lin2_done"), sem("c_y3_ready")
            r1t_ready, r1_ready = sem("c_r1_product"), sem("c_r1_ready")
            r2t_ready, r2_ready = sem("c_r2_product"), sem("c_r2_ready")
            o3_ready, o3b_ready = sem("c_o3_product"), sem("c_o3_ready")
            x_ready = sem("c_x_ready")

            def over_groups(eng, prep, group, post):
                def prepare(p):
                    prep(0)

                def work(p, ahead):
                    g = 2 * p
                    started = not isinstance(p, int) or p > 0
                    group(g, 0, g + 1, g - 1 if started else None, g - 2 if started else None, p)
                    group(g + 1, 1, None if ahead is None else 2 * ahead, g, g - 1 if started else None, p)

                over_pairs(eng, PAIRS, prepare, work, peeled=2)
                post()

            def bcast(t):
                return t[:, :].unsqueeze(1).broadcast_to([P, GB, D])

            with nc.Block() as block:
                @block.sync
                def _(sp):
                    def load(g, p, slot):
                        if later(g, 2):
                            sp.wait_ge(c_done, g - 1)
                        sp.dma_start(ctxs[:, slot, :, :],
                                     ctx_tokens[bass.ds(g * GB, GB), :, :].rearrange("b m d -> m b d"))\
                          .then_inc(ctx_loaded[slot], 16)

                    def spread(g, p, slot):
                        sp.wait_ge(k_ready, g + 1)
                        if not later(g, 1):
                            sp.wait_ge(kbd0_zeroed, 1)
                        elif not later(g, 2):
                            sp.wait_ge(zeroed, 3)
                        for h in range(H):
                            sp.dma_start(kbd[h * HD:(h + 1) * HD, slot, :, h * M:(h + 1) * M],
                                         kT[h * HD:(h + 1) * HD, :].rearrange("p (b m) -> p b m", b=GB))\
                              .then_inc(kbd_loaded[slot], 16)

                    def spread_values(g, slot):
                        sp.wait_ge(v_ready, g + 1)
                        if not later(g, 2):
                            sp.wait_ge(zeroed, 3 if later(g, 1) else 1)
                        for h, m, n, c, row in PIECES:
                            sp.dma_start(vp[row:row + n, slot, :, c, h * HD:(h + 1) * HD],
                                         vs[m:m + n, :, h * HD:(h + 1) * HD]).then_inc(vp_loaded[slot], 16)

                    def prepare(p):
                        load(0, 0, 0)
                        load(1, 0, 1)
                        spread(0, 0, 0)
                        spread_values(0, 0)

                    def work(p, ahead):
                        spread(2 * p + 1, p, 1)
                        spread_values(2 * p + 1, 1)
                        if ahead is not None:
                            load(2 * ahead, ahead, 0)
                            load(2 * ahead + 1, ahead, 1)
                            spread(2 * ahead, ahead, 0)
                            spread_values(2 * ahead, 0)

                    over_pairs(sp, PAIRS, prepare, work)

                @block.tensor
                def _(pe):
                    pe.wait_ge(layer_loaded, ALL_LOADED)
                    for i in range(6):
                        bk = (bA, bB)[i % 2]
                        if i >= 2:
                            pe.wait_ge(wT_ready, i - 1)
                        pe.transpose(bk[:, 0:P], nat[:, i, :], ident[:, :]).then_inc(wT_done, 1)
                    pe.wait_ge(wT_ready, 5)
                    for f in range(FT):
                        i = pe.transpose(bA[:, f * P:(f + 1) * P], l1n[:, f, :], ident[:, :])
                    i.then_inc(wT_done, 1)
                    pe.wait_ge(wT_ready, 6)
                    for f in range(FT):
                        i = pe.transpose(bB[:, f * P:(f + 1) * P], l2n[:, f * P:(f + 1) * P], ident[:, :])
                    i.then_inc(wT_done, 1)
                    pe.wait_ge(bvb_ready, 1)
                    pe.wait_ge(wT_ready, 7)
                    pe.matmul(bC[:, 0:P], nat[:, 0, :], tr[:, 1, :], start=True, stop=True)
                    pe.matmul(bC[:, P:2 * P], bvb[:, 0, :], tr[:, 1, :], start=True, stop=True)
                    pe.matmul(bC[:, 2 * P:3 * P], bvb[:, 1, :], tr[:, 5, :], start=True, stop=True)
                    i = pe.matmul(bC[:, 3 * P:3 * P + 1], tr[:, 2, :], cols[:, 5:6], start=True, stop=True)
                    for f in range(FT):
                        i = pe.matmul(bC[:, 3 * P + 1 + f:3 * P + 2 + f], l1T[:, f, :], l2b[:, :],
                                      start=True, stop=True)
                    i.then_inc(fold_done, 1)

                    def four(dst, src, idn):
                        for b in range(GB):
                            i = pe.transpose(dst(b), src(b), idn)
                        return i

                    def at(bk, b, w=P):
                        return bk[:, b * w:(b + 1) * w]

                    def t0(g):
                        pe.wait_ge(n0_ready, g + 1)
                        if later(g, 2):
                            pe.wait_ge(y2_ready, g - 1)
                        elif later(g, 1):
                            pe.wait_ge(q_ready, g)
                        else:
                            pe.wait_ge(wT_ready, 8)
                        four(lambda b: at(bB, b), lambda b: xn[:, b, :], ident[:, :]).then_inc(t0_done, 1)

                    def ctxT(g, p, slot):
                        pe.wait_ge(ctx_loaded[slot], 16 * (p + 1))
                        if later(g, 3):
                            pe.wait_ge(l1_ready, FT * (g - 2))
                        elif later(g, 1):
                            pe.wait_ge(v_ready, g)
                        else:
                            pe.wait_ge(consts_ready, 1)
                        four(lambda b: at(bC, b, M), lambda b: ctxs[:, slot, b, :], ident[0:M, 0:M])\
                            .then_inc(c_done, 1)

                    def self_attention(g):
                        pe.wait_ge(t0_ready, g + 1)
                        for b in range(GB):
                            i = pe.matmul(at(bB, b), xT[:, b * P:(b + 1) * P], m1t[:, :], start=True, stop=True)
                        i.then_inc(y1_done, 1)

                    def values(g):
                        pe.wait_ge(c_ready, g + 1)
                        for b in range(GB):
                            i = pe.matmul(bC[0:M, b * P:(b + 1) * P], cT[:, b * M:(b + 1) * M], tr[:, 4, :],
                                          start=True, stop=True)
                        i.then_inc(v_done, 1)

                    def keys(g):
                        pe.wait_ge(y1_ready, g + 1)
                        pe.matmul(bB[:, 0:GB * M], tr[:, 3, :], cT[:, :], start=True, stop=True).then_inc(k_done, 1)

                    def t1(g):
                        pe.wait_ge(n1_ready, g + 1)
                        pe.wait_ge(k_ready, g + 1)
                        four(lambda b: at(bB, b), lambda b: n1[:, b, :], ident[:, :]).then_inc(t1_done, 1)

                    def q(g):
                        pe.wait_ge(t1_ready, g + 1)
                        pe.matmul(bB[:, :], qg[:, :], n1T[:, :], start=True, stop=True).then_inc(q_done, 1)

                    def scores(g, b, p, slot):
                        if b == 0:
                            pe.wait_ge(q_ready, g + 1)
                            pe.wait_ge(kbd_loaded[slot], 16 * H * (p + 1))
                        if b or later(g, 1):
                            pe.wait_ge(s_ready, GB * g + b)
                        for k in range(2):
                            i = pe.matmul(psS[:, k, 0:HB], qT[:, slot, b * P:(b + 1) * P],
                                          kbd[:, slot, b, k * HB:(k + 1) * HB], start=True, stop=True)
                        i.then_inc(s_done, 1)

                    def probsT(g, b):
                        pe.wait_ge(pn_ready, GB * g + b + 1)
                        pf = pn[:, b % 2, :, :].rearrange("p h m -> p (h m)")
                        for k, cs in enumerate((range(0, 4), range(4, NC))):
                            if b or later(g, 1):
                                pe.wait_ge(tp_ready, 2 * (GB * g + b - 1) + k + 1)
                            for c in cs:
                                i = pe.transpose(psP[0:chunk[c], k, (c % 4) * P:(c % 4 + 1) * P],
                                                 pf[:, c * P:c * P + chunk[c]], ident[:, :])
                            i.then_inc(tp_done, 1)

                    def pv(g, b, slot, p=None):
                        pe.wait_ge(tp_ready, 2 * (GB * g + b + 1))
                        if b == 0:
                            pe.wait_ge(vp_loaded[slot], 16 * len(PIECES) * (p + 1))
                            if later(g, 1):
                                pe.wait_ge(ca_ready, g)
                        for c in range(NC):
                            i = pe.matmul(at(psO, b), vp[0:chunk[c], slot, b, c, :], pT[0:chunk[c], b % 2, c, :],
                                          start=(c == 0), stop=(c == NC - 1))
                        i.then_inc(pv_done, 1)

                    def out_proj(g, slot):
                        pe.wait_ge(ca_ready, g + 1)
                        if isinstance(g, int) and g == NG - 1:
                            pe.wait_ge(y2_ready, g)
                        else:
                            pe.wait_ge(q_ready, g + 2)
                        for b in range(GB):
                            i = pe.matmul(at(bB, b), ca[:, slot, b * P:(b + 1) * P], tr[:, 5, :],
                                          start=True, stop=True)
                        i.then_inc(out_done, 1)

                    def t2(g):
                        pe.wait_ge(n2_ready, g + 1)
                        if later(g, 1):
                            pe.wait_ge(y3_ready, g)
                        four(lambda b: at(bA, b), lambda b: n2[:, b, :], ident[:, :]).then_inc(t2_done, 1)

                    def lin1(g, f):
                        if f == 0:
                            pe.wait_ge(t2_ready, g + 1)
                        if f == 1:
                            pe.wait_ge(v_ready, NG if isinstance(g, int) and g > NG - 3 else g + 3)
                        if f >= 2:
                            pe.wait_ge(l1_ready, FT * g + f - 1)
                        pe.matmul((bA, bC)[f % 2][:, :], l1g[:, f, :], n2T[:, :], start=True, stop=True)\
                            .then_inc(l1_done, 1)

                    def lin2(g, half):
                        pe.wait_ge(l1_ready, FT * (g + 1))
                        for b in (2 * half, 2 * half + 1):
                            for f in range(FT):
                                i = pe.matmul(at(bA, b), hT[:, f, b * P:(b + 1) * P], l2T[:, f, :],
                                              start=(f == 0), stop=(f == FT - 1))
                        if half == 1:
                            i.then_inc(l2_done, 1)

                    def prep(g):
                        t0(g)
                        ctxT(g, 0, 0)
                        self_attention(g)
                        values(g)
                        keys(g)
                        t1(g)
                        q(g)

                    def group(g, slot, nxt, prv, pp, p):
                        other = 1 - slot
                        scores(g, 0, p, slot)
                        if prv is not None:
                            probsT(prv, GB - 1)
                        if pp is not None:
                            lin2(pp, 0)
                        if prv is not None:
                            pv(prv, GB - 1, other)
                        if pp is not None:
                            lin2(pp, 1)
                        if prv is not None:
                            out_proj(prv, other)
                        scores(g, 1, p, slot)
                        probsT(g, 0)
                        if nxt is not None:
                            t0(nxt)
                            ctxT(nxt, p if slot == 0 else p + 1, other)
                        pv(g, 0, slot, p)
                        if nxt is not None:
                            self_attention(nxt)
                            values(nxt)
                        scores(g, 2, p, slot)
                        probsT(g, 1)
                        if nxt is not None:
                            keys(nxt)
                        if prv is not None:
                            t2(prv)
                        pv(g, 1, slot)
                        if prv is not None:
                            lin1(prv, 0)
                            lin1(prv, 1)
                        scores(g, 3, p, slot)
                        probsT(g, 2)
                        if nxt is not None:
                            t1(nxt)
                        if prv is not None:
                            lin1(prv, 2)
                            lin1(prv, 3)
                        if nxt is not None:
                            q(nxt)
                        pv(g, 2, slot)

                    def weight_sums():
                        pe.wait_ge(ones_ready, 1)
                        pe.wait_ge(prepv, 1)
                        pe.wait_ge(s_ready, GB * NG)
                        pe.matmul(psS[:, 0, 0:2], ones[:, :], asum[:, :], start=True, stop=True)\
                          .then_inc(sums_done, 1)

                    def weight_transposes():
                        pe.wait_ge(prepv, 2)
                        pe.wait_ge(tp_ready, 2 * GB * NG)
                        for k in range(TAPS):
                            for c in range(HC):
                                i = pe.transpose(psPrep[k][:, c * P:(c + 1) * P], w1k[:, k, c, :], ident[:, :])
                            i.then_inc(wk_done, 1)
                        for c in range(HC):
                            i = pe.transpose(psPrep[TAPS][:, c * P:(c + 1) * P], ta[:, 1, c * P:(c + 1) * P],
                                             ident[:, :])
                        i.then_inc(wk_done, 1)

                    def post():
                        probsT(NG - 1, GB - 1)
                        lin2(NG - 2, 0)
                        weight_sums()
                        pv(NG - 1, GB - 1, 1)
                        lin2(NG - 2, 1)
                        out_proj(NG - 1, 1)
                        t2(NG - 1)
                        for f in range(FT):
                            lin1(NG - 1, f)
                        lin2(NG - 1, 0)
                        lin2(NG - 1, 1)
                        weight_transposes()

                    over_groups(pe, prep, group, post)

                @block.scalar
                def _(act):
                    for i in range(6):
                        act.wait_ge(wT_done, i + 1)
                        act.activation(tr[:, i, :], (bA, bB)[i % 2][:, 0:P], ACT.Copy).then_inc(wT_ready, 1)
                    act.wait_ge(wT_done, 7)
                    act.activation(l1T[:, :, :].rearrange("p f c -> p (f c)"), bA[:, :], ACT.Copy).then_inc(wT_ready, 1)
                    act.wait_ge(wT_done, 8)
                    act.activation(l2T[:, :, :].rearrange("p f c -> p (f c)"), bB[:, :], ACT.Copy).then_inc(wT_ready, 1)

                    def c_t0(g):
                        act.wait_ge(t0_done, g + 1)
                        if later(g, 1):
                            act.wait_ge(y1_done, g)
                        act.activation(xT[:, :], bB[:, :], ACT.Copy).then_inc(t0_ready, 1)

                    def c_ctx(g):
                        act.wait_ge(c_done, g + 1)
                        if later(g, 1):
                            act.wait_ge(v_done, g)
                        act.activation(cT[:, :], bC[:, 0:GB * M], ACT.Copy).then_inc(c_ready, 1)

                    def c_k(g, p, slot):
                        act.wait_ge(k_done, g + 1)
                        if later(g, 1):
                            act.wait_ge(kbd_loaded[1 - slot], 16 * H * (p + 1 if slot else p))
                        if later(g, 2):
                            act.wait_ge(s_done, GB * (g - 1))
                        act.activation(kT[:, :], bB[:, 0:GB * M], ACT.Identity, bias=cols[:, 2:3]).then_inc(k_ready, 1)

                    def c_v(g, p, slot):
                        act.wait_ge(v_done, g + 1)
                        if later(g, 1):
                            act.wait_ge(vp_loaded[1 - slot], 16 * len(PIECES) * (p + 1 if slot else p))
                        if later(g, 2):
                            act.wait_ge(pv_done, GB * (g - 1))
                        act.activation(vs[:, :, :].rearrange("m b d -> m (b d)"), bC[0:M, :], ACT.Copy)\
                           .then_inc(v_ready, 1)

                    def c_t1(g):
                        act.wait_ge(t1_done, g + 1)
                        if later(g, 1):
                            act.wait_ge(q_done, g)
                        act.activation(n1T[:, :], bB[:, :], ACT.Copy).then_inc(t1_ready, 1)

                    def exps(g, b):
                        act.wait_ge(s_ready, GB * g + b + 1)
                        if b >= 2 or later(g, 1):
                            act.wait_ge(pn_ready, GB * g + b - 1)
                        act.activation(pr[:, b % 2, :, :], sc[:, b % 2, :, :], ACT.Exp).then_inc(exp_ready, 1)

                    def c_probsT(g, b):
                        for k in range(2):
                            act.wait_ge(tp_done, 2 * (GB * g + b) + k + 1)
                            if k == 0 and (b >= 2 or later(g, 1)):
                                act.wait_ge(pv_done, GB * g + b - 1)
                            if k == 0:
                                act.activation(pT[:, b % 2, 0:4, :].rearrange("p c t -> p (c t)"), psP[:, 0, :],
                                               ACT.Copy).then_inc(tp_ready, 1)
                            else:
                                act.activation(pT[0:chunk[-1], b % 2, 4, :], psP[0:chunk[-1], 1, 0:P],
                                               ACT.Copy).then_inc(tp_ready, 1)

                    def c_ca(g, slot):
                        act.wait_ge(pv_done, GB * (g + 1))
                        if later(g, 2):
                            act.wait_ge(out_done, g - 1)
                        act.activation(ca[:, slot, :], psO[:, :], ACT.Copy).then_inc(ca_ready, 1)

                    def c_t2(g):
                        act.wait_ge(t2_done, g + 1)
                        if later(g, 1):
                            act.wait_ge(l1_done, FT * g)
                        act.activation(n2T[:, :], bA[:, :], ACT.Copy).then_inc(t2_ready, 1)

                    def c_lin1(g, f):
                        act.wait_ge(l1_done, FT * g + f + 1)
                        if f == 0 and later(g, 1):
                            act.wait_ge(l2_done, g)
                        act.activation(hT[:, f, :], (bA, bC)[f % 2][:, :], ACT.Relu, bias=l1b2[:, f:f + 1])\
                            .then_inc(l1_ready, 1)

                    def c_q(g, slot):
                        act.wait_ge(q_done, g + 1)
                        if later(g, 2):
                            act.wait_ge(s_done, GB * (g - 1))
                        act.activation(qT[:, slot, :], bB[:, :], ACT.Identity, bias=bq3[:, :], scale=Q_SCALE)\
                            .then_inc(q_ready, 1)

                    def prep(g):
                        c_t0(g)
                        c_ctx(g)
                        c_v(g, 0, 0)
                        c_k(g, 0, 0)
                        c_t1(g)
                        c_q(g, 0)

                    def group(g, slot, nxt, prv, pp, p):
                        other = 1 - slot
                        nxt_p = p if slot == 0 else p + 1
                        if prv is not None:
                            c_probsT(prv, GB - 1)
                        exps(g, 0)
                        if prv is not None:
                            c_ca(prv, other)
                        c_probsT(g, 0)
                        if nxt is not None:
                            c_t0(nxt)
                            c_ctx(nxt)
                        exps(g, 1)
                        if nxt is not None:
                            c_v(nxt, nxt_p, other)
                            c_k(nxt, nxt_p, other)
                        c_probsT(g, 1)
                        if prv is not None:
                            c_t2(prv)
                        exps(g, 2)
                        if prv is not None:
                            c_lin1(prv, 0)
                            c_lin1(prv, 1)
                        c_probsT(g, 2)
                        if nxt is not None:
                            c_t1(nxt)
                        if prv is not None:
                            c_lin1(prv, 2)
                        exps(g, 3)
                        if prv is not None:
                            c_lin1(prv, 3)
                        if nxt is not None:
                            c_q(nxt, other)

                    def post():
                        c_probsT(NG - 1, GB - 1)
                        c_ca(NG - 1, 1)
                        c_t2(NG - 1)
                        for f in range(FT):
                            c_lin1(NG - 1, f)
                        for k in range(TAPS):
                            act.wait_ge(wk_done, k + 1)
                            act.activation(wkh[:, k, :], psPrep[k], ACT.Copy).then_inc(wkh_ready, 1)
                        act.wait_ge(wk_done, TAPS + 1)
                        act.activation(w2T[:, :, :].rearrange("p c k -> p (c k)"), psPrep[TAPS], ACT.Copy)\
                           .then_inc(w2T_ready, 1)

                    act.wait_ge(consts_ready, 1)
                    over_groups(act, prep, group, post)

                @block.gpsimd
                def _(pool):

                    def probs(g, b):
                        pool.wait_ge(exp_ready, GB * g + b + 1)
                        pool.wait_ge(inv_ready, GB * g + b + 1)
                        if b >= 2 or later(g, 1):
                            pool.wait_ge(tp_done, 2 * (GB * g + b - 1))
                        pool.tensor_tensor(pn[:, b % 2, :, :], pr[:, b % 2, :, :],
                                           iv[:, b % 2, :].unsqueeze(2).broadcast_to([P, H, M]), ALU.mult)\
                            .then_inc(pn_ready, 1)

                    def residual1(g, slot):
                        pool.wait_ge(n1_ready, g + 1)
                        if later(g, 2):
                            pool.wait_ge(y2_ready, g - 1)
                        pool.tensor_tensor(r1[:, slot, :, :], n1[:, :, :], bcast(rows_bc[:, G1, :]), ALU.mult)\
                            .then_inc(r1t_ready, 1)
                        pool.wait_ge(r1t_ready, g + 1)
                        pool.tensor_tensor(r1[:, slot, :, :], r1[:, slot, :, :], bcast(r1b), ALU.add)\
                          .then_inc(r1_ready, 1)

                    def residual2(g):
                        pool.wait_ge(n2_ready, g + 1)
                        if later(g, 1):
                            pool.wait_ge(y3_ready, g)
                        pool.tensor_tensor(r2[:, :, :], n2[:, :, :], bcast(rows_bc[:, G2, :]), ALU.mult)\
                            .then_inc(r2t_ready, 1)
                        pool.wait_ge(r2t_ready, g + 1)
                        pool.tensor_tensor(r2[:, :, :], r2[:, :, :], bcast(r2b), ALU.add).then_inc(r2_ready, 1)

                    def last(g):
                        pool.wait_ge(n3_ready, g + 1)
                        if later(g, 1):
                            pool.wait_ge(x_ready, g)
                        pool.tensor_tensor(o3[:, :, :], n3[:, :, :], bcast(g3), ALU.mult).then_inc(o3_ready, 1)
                        pool.wait_ge(o3_ready, g + 1)
                        pool.tensor_tensor(o3[:, :, :], o3[:, :, :], bcast(b3), ALU.add).then_inc(o3b_ready, 1)

                    def prep(g):
                        norm_pool(pool, g, 0, lns[0], sems[0])
                        pool.memset(vp[:, 0, :, :, :], 0.0).then_inc(zeroed, 1)
                        norm_pool(pool, g, 0, lns[1], sems[1])
                        pool.memset(kbd[:, 1, :, :], 0.0).then_inc(zeroed, 1)
                        pool.memset(vp[:, 1, :, :, :], 0.0).then_inc(zeroed, 1)
                        pool.wait_ge(consts_ready, 1)
                        residual1(g, 0)
                        pool.memset(ones[:, :], 1.0)
                        pool.memset(ones_bf[:, :], 1.0)
                        pool.memset(big[:, :], BIG).then_inc(ones_ready, 1)

                    def group(g, slot, nxt, prv, pp, p):
                        other = 1 - slot
                        if nxt is not None:
                            norm_pool(pool, nxt, other, lns[0], sems[0])
                        probs(g, 0)
                        if prv is not None:
                            norm_pool(pool, prv, other, lns[2], sems[2])
                        probs(g, 1)
                        if prv is not None:
                            residual2(prv)
                        if nxt is not None:
                            norm_pool(pool, nxt, other, lns[1], sems[1])
                        probs(g, 2)
                        if pp is not None:
                            norm_pool(pool, pp, slot, lns[3], sems[3])
                        if nxt is not None:
                            residual1(nxt, other)
                        probs(g, 3)
                        if pp is not None:
                            last(pp)

                    def post():
                        norm_pool(pool, NG - 1, 1, lns[2], sems[2])
                        norm_pool(pool, NG - 2, 0, lns[3], sems[3])
                        residual2(NG - 1)
                        last(NG - 2)
                        norm_pool(pool, NG - 1, 1, lns[3], sems[3])
                        last(NG - 1)

                    over_groups(pool, prep, group, post)

                @block.vector
                def _(v):
                    def x_of(g, b):
                        return X[:, bass.ds(g * GB + b, 1), :].rearrange("p a d -> p (a d)")

                    def moments(i, g, slot, src):
                        norm_moments(v, g, slot, src, lns[i], sems[i])

                    def apply(i, g, slot, src, dst):
                        norm_apply(v, g, slot, src, dst, lns[i], sems[i])

                    def moments0(g, slot):
                        moments(0, g, slot, lambda b: x_of(g, b))

                    def apply0(g, slot):
                        if later(g, 1):
                            v.wait_ge(t0_done, g)
                        apply(0, g, slot, lambda b: x_of(g, b), lambda b: xn[:, b, :])

                    moments0(0, 0)
                    v.memset(kbd[:, 0, :, :], 0.0).then_inc(kbd0_zeroed, 1)
                    v.wait_ge(layer_loaded, ALL_LOADED)
                    for i, c in enumerate((0, 3)):
                        v.tensor_scalar(bvb[:, i, :], ident[:, :], 0.0, cols[:, c:c + 1], ALU.mult, ALU.add)\
                         .then_inc(rowsum_step, 1)
                    v.wait_ge(rowsum_step, 2)
                    v.sem_inc(bvb_ready, 1)
                    v.tensor_tensor(r1b0[:, :], rows_bc[:, B1, :], rows_bc[:, MHO, :], ALU.add).then_inc(rowsum_step, 1)
                    v.tensor_tensor(r2b[:, :], rows_bc[:, B2, :], rows_bc[:, L2B, :], ALU.add).then_inc(rowsum_step, 1)
                    v.tensor_scalar(g3[:, :], rows_bc[:, 8, :], gates[:, 1:2], None, ALU.mult)
                    v.tensor_scalar(b3[:, :], rows_bc[:, 2, :], gates[:, 1:2], None, ALU.mult)
                    apply0(0, 0)
                    v.wait_ge(wT_ready, 8)
                    v.tensor_scalar(qg[:, :], tr[:, 2, :], cols[:, 4:5], None, ALU.mult)
                    v.tensor_scalar(l1g[:, :, :], l1T[:, :, :], cols[:, 6:7], None, ALU.mult)
                    v.wait_ge(rowsum_step, 4)
                    v.wait_ge(fold_done, 1)
                    v.tensor_tensor(m1t[:, :], bC[:, 0:P], ident[:, :], ALU.add)
                    v.tensor_tensor(y1b[:, :], bC[:, P:2 * P], rows_bc[:, 0, :], ALU.add)
                    v.tensor_tensor(r1b[:, :], bC[:, 2 * P:3 * P], r1b0[:, :], ALU.add)
                    v.tensor_tensor(bq2[:, :], bC[:, 3 * P:3 * P + 1], cols[:, 1:2], ALU.add).then_inc(rowsum_step, 1)
                    v.tensor_tensor(l1b2[:, :], bC[:, 3 * P + 1:3 * P + 1 + FT], l1b[:, :], ALU.add)\
                     .then_inc(rowsum_step, 1)
                    v.wait_ge(rowsum_step, 5)
                    v.tensor_scalar(bq3[:, :], bq2[:, :], Q_SCALE, None, ALU.mult).then_inc(rowsum_step, 1)
                    v.wait_ge(rowsum_step, 7)
                    v.sem_inc(consts_ready, 1)

                    def first_sum(g):
                        v.wait_ge(y1_done, g + 1)
                        v.tensor_tensor(y1[:, :, :], bB[:, :].rearrange("p (b d) -> p b d", b=GB), bcast(y1b), ALU.add)\
                         .then_inc(y1_ready, 1)

                    def moments1(g, slot):
                        v.wait_ge(y1_ready, g + 1)
                        moments(1, g, slot, lambda b: y1[:, b, :])

                    def apply1(g, slot):
                        if later(g, 1):
                            v.wait_ge(t1_done, g)
                            v.wait_ge(r1t_ready, g)
                        apply(1, g, slot, lambda b: y1[:, b, :], lambda b: n1[:, b, :])

                    def softmax_a(g, b):
                        s4 = psS[:, :, 0:HB].rearrange("p k (h m) -> p k h m", m=M)
                        v.wait_ge(s_done, GB * g + b + 1)
                        v.tensor_reduce(mx[:, b % 2, :].rearrange("p (k h) -> p k h", k=2), s4, AX.X, ALU.max)\
                         .then_inc(mx_ready, 1)
                        v.wait_ge(mx_ready, GB * g + b + 1)
                        if b >= 2 or later(g, 1):
                            v.wait_ge(exp_ready, GB * g + b - 1)
                        v.tensor_tensor(sc[:, b % 2, :, :].rearrange("p (k h) m -> p k h m", k=2), s4,
                                        mx[:, b % 2, :].rearrange("p (k h) -> p k h", k=2).unsqueeze(3)
                                        .broadcast_to([P, 2, H // 2, M]), ALU.subtract).then_inc(s_ready, 1)

                    def softmax_b(g, b):
                        v.wait_ge(exp_ready, GB * g + b + 1)
                        v.tensor_reduce(sm[:, b % 2, :], pr[:, b % 2, :, :], AX.X, ALU.add).then_inc(sum_ready, 1)
                        v.wait_ge(sum_ready, GB * g + b + 1)
                        if b >= 2 or later(g, 1):
                            v.wait_ge(pn_ready, GB * g + b - 1)
                        v.reciprocal(iv[:, b % 2, :], sm[:, b % 2, :]).then_inc(inv_ready, 1)

                    def second_sum(g, slot):
                        v.wait_ge(out_done, g + 1)
                        v.wait_ge(r1_ready, g + 1)
                        v.tensor_tensor(y2[:, :, :], bB[:, :].rearrange("p (b d) -> p b d", b=GB), r1[:, slot, :, :],
                                        ALU.add).then_inc(y2_ready, 1)

                    def moments2(g, slot):
                        v.wait_ge(y2_ready, g + 1)
                        moments(2, g, slot, lambda b: y2[:, b, :])

                    def apply2(g, slot):
                        if later(g, 1):
                            v.wait_ge(t2_done, g)
                            v.wait_ge(r2t_ready, g)
                        apply(2, g, slot, lambda b: y2[:, b, :], lambda b: n2[:, b, :])

                    def third_sum(g):
                        v.wait_ge(l2_done, g + 1)
                        v.wait_ge(r2_ready, g + 1)
                        v.tensor_tensor(y3[:, :, :], bA[:, :].rearrange("p (b d) -> p b d", b=GB), r2[:, :, :],
                                        ALU.add).then_inc(y3_ready, 1)

                    def moments3(g, slot):
                        v.wait_ge(y3_ready, g + 1)
                        moments(3, g, slot, lambda b: y3[:, b, :])

                    def apply3(g, slot):
                        if later(g, 1):
                            v.wait_ge(o3_ready, g)
                        apply(3, g, slot, lambda b: y3[:, b, :], lambda b: n3[:, b, :])

                    def add_x(g):
                        v.wait_ge(o3b_ready, g + 1)
                        xg = X[:, bass.ds(g * GB, GB), :].rearrange("p b d -> p (b d)")
                        v.tensor_tensor(xg, xg, o3[:, :, :].rearrange("p b d -> p (b d)"), ALU.add).then_inc(x_ready, 1)

                    def prep(g):
                        first_sum(g)
                        moments1(g, 0)
                        apply1(g, 0)

                    def group(g, slot, nxt, prv, pp, p):
                        other = 1 - slot
                        if nxt is not None:
                            moments0(nxt, other)
                        softmax_a(g, 0)
                        softmax_b(g, 0)
                        if pp is not None and later(pp, 1):
                            add_x(pp - 1)
                        if nxt is not None:
                            apply0(nxt, other)
                        if pp is not None:
                            third_sum(pp)
                        if prv is not None:
                            second_sum(prv, other)
                        softmax_a(g, 1)
                        if prv is not None:
                            moments2(prv, other)
                        softmax_b(g, 1)
                        if nxt is not None:
                            first_sum(nxt)
                        if prv is not None:
                            apply2(prv, other)
                        softmax_a(g, 2)
                        if nxt is not None:
                            moments1(nxt, other)
                        softmax_b(g, 2)
                        if nxt is not None:
                            apply1(nxt, other)
                        if pp is not None:
                            moments3(pp, slot)
                        softmax_a(g, 3)
                        if pp is not None:
                            apply3(pp, slot)
                        softmax_b(g, 3)

                    def weight_sums():
                        v.wait_ge(ffn_loaded, 64)
                        for i, w in enumerate((w1n, w2n)):
                            ins = v.tensor_reduce(asum[:, i:i + 1], w[:, :, :].rearrange("p c d -> p (c d)"), AX.X,
                                                  ALU.add, apply_absolute_value=True)
                        ins.then_inc(prepv, 1)

                    def ternary_weights():
                        v.wait_ge(sums_done, 1)
                        v.tensor_scalar(mean[:, :], psS[:, 0, 0:2], 1.0 / W_COUNT, 1e-5, ALU.mult, ALU.max)\
                          .then_inc(step, 1)
                        v.wait_ge(step, 1)
                        v.reciprocal(rmean[:, :], mean[:, :])
                        v.tensor_scalar(sw2[:, :], mean[:, 1:2], gates[:, 3:4], None, ALU.mult).then_inc(step, 1)
                        v.wait_ge(step, 2)
                        for i, w in enumerate((w1n, w2n)):
                            ins = v.tensor_scalar(ta[:, i, :], w[:, :, :].rearrange("p c d -> p (c d)"),
                                                  rmean[:, i:i + 1], BIG, ALU.mult, ALU.add)
                        ins.then_inc(step, 1)
                        v.wait_ge(step, 3)
                        v.tensor_scalar(ta[:, :, :], ta[:, :, :], BIG, 1.0, ALU.subtract, ALU.min).then_inc(step, 1)
                        v.wait_ge(step, 4)
                        v.tensor_scalar(ta[:, :, :], ta[:, :, :], -1.0, None, ALU.max).then_inc(step, 1)
                        v.wait_ge(step, 5)

                    def tap_weights():
                        for k in range(TAPS):
                            for c in range(HC):
                                ins = v.tensor_scalar(w1k[:, k, c, :], ta[:, 0, c * D:(c + 1) * D], cwn[:, c, k:k + 1],
                                                      mean[:, 0:1], ALU.mult, ALU.mult)
                        ins.then_inc(prepv, 1)

                    def bias_parts():
                        v.tensor_copy(cb1[:, :], cbn[:, :]).then_inc(step, 1)
                        v.wait_ge(step, 6)
                        v.tensor_tensor(cr1, cbn[:, :], cb1[:, :], ALU.subtract)
                        v.tensor_scalar(cm1, cb1[:, :], ident[:, 0:1], None, ALU.mult).then_inc(step, 1)
                        v.wait_ge(step, 7)
                        v.tensor_copy(cb2[:, :], cr1).then_inc(step, 1)
                        v.wait_ge(step, 8)
                        v.tensor_tensor(cr1, cr1, cb2[:, :], ALU.subtract)
                        v.scalar_tensor_tensor(out=cm1, in0=cb2[:, :], scalar=ident[:, 1:2], in1=cm1,
                                               op0=ALU.mult, op1=ALU.add).then_inc(step, 1)
                        v.wait_ge(step, 9)
                        v.scalar_tensor_tensor(out=cb[:, :], in0=cr1, scalar=ident[:, 2:3], in1=cm1,
                                               op0=ALU.mult, op1=ALU.add).then_inc(prepv, 1)

                    def lower_weights():
                        for k in range(TAPS):
                            v.wait_ge(wkh_ready, k + 1)
                            v.tensor_tensor(wkl[:, k, :], psPrep[k], wkh[:, k, :].bitcast(F32), ALU.subtract)\
                             .then_inc(wkl_ready, 1)

                    def post():
                        add_x(NG - 3)
                        weight_sums()
                        third_sum(NG - 2)
                        second_sum(NG - 1, 1)
                        moments2(NG - 1, 1)
                        moments3(NG - 2, 0)
                        apply2(NG - 1, 1)
                        apply3(NG - 2, 0)
                        ternary_weights()
                        tap_weights()
                        add_x(NG - 2)
                        bias_parts()
                        third_sum(NG - 1)
                        moments3(NG - 1, 1)
                        lower_weights()
                        apply3(NG - 1, 1)
                        add_x(NG - 1)

                    over_groups(v, prep, group, post)

        end_phase()

        with ExitStack() as st:
            TQ_LAG = 2
            O_LAG = 3

            xn = sb(st, "d_xn", [P, GB, D])
            am = sb(st, "d_am", [P, GB])
            asc = sb(st, "d_asc", [P, GB])
            ais = sb(st, "d_ais", [P, GB])
            za = sb(st, "d_za", [P, GB, D])
            zb = sb(st, "d_zb", [P, GB, D])
            xq = sb(st, "d_xq", [P, GB, D])
            xh = sb(st, "d_xh", [P, 2, GB, P + 2], F32R)
            xl = sb(st, "d_xl", [P, 2, GB, P + 2], F32R)
            sl = sb(st, "d_sl", [P, GB, HW])
            hm = sb(st, "d_hm", [P, GB])
            hs = sb(st, "d_hs", [P, GB])
            hsc = sb(st, "d_hsc", [P, GB])
            hf = sb(st, "d_hf", [P, 2, GB])
            hz = sb(st, "d_hz", [P, GB, HW])
            hc = sb(st, "d_hc", [P, GB, HW])
            hq = sb(st, "d_hq", [P, GB, HW], BF16)
            hqT = sb(st, "d_hqT", [P, GB, HC, P], BF16)
            ln = norm_tiles(st, "lnD")

            psT = bank(st, "d_psT")
            psH = [bank(st, f"d_psH{b}") for b in range(2)]
            psQ = [bank(st, f"d_psQ{b}", BF16, 1024) for b in range(2)]
            psO = [bank(st, f"d_psO{s}") for s in range(2)]

            padded = sem("d_padded")
            lnD = norm_sems("d_ln")
            normed = lnD[-1]
            quant = sem("d_quant_step")
            za_ready = sem("d_x_scaled")
            STEPS = 4
            xq_ready = sem("d_xq_ready")
            xT_done = sem("d_xT_done")
            xh_ready = sem("d_xh_ready")
            xl_ready = sem("d_xl_ready")
            h_done = sem("d_hidden_done")
            sl_ready = sem("d_silu_ready")
            hstep = sem("d_hidden_scale_step")
            hz_ready = sem("d_hidden_scaled")
            hc_ready = sem("d_hidden_clipped")
            hq_ready = sem("d_hidden_rounded")
            tq_done = sem("d_hiddenT_done")
            tq_ready = sem("d_hiddenT_ready")
            o_done = sem("d_out_done")
            x_ready = sem("d_x_ready")

            def over_groups(eng, prep, group, tail):
                def prepare(p):
                    prep(0)

                def work(p, ahead):
                    after = None if ahead is None else 2 * ahead
                    group(2 * p, 0, 2 * p + 1, after)
                    group(2 * p + 1, 1, after, None if ahead is None else after + 1)

                over_pairs(eng, PAIRS, prepare, work, peeled=2)
                tail()

            def before(step, g, slot, b, lag):
                if b >= lag:
                    step(g, slot, b - lag)
                elif later(g, 1):
                    step(g - 1, 1 - slot, b - lag + GB)

            with nc.Block() as block:
                @block.sync
                def _(sp):
                    def store(g):
                        sp.wait_ge(x_ready, g + 1)
                        sp.dma_start(out[bass.ds(g * GB, GB), :, :].rearrange("b s d -> s b d"),
                                     X[:, bass.ds(g * GB, GB), :]).then_inc(out_stored, 16)

                    with sp.Fori(0, NG) as g:
                        store(g)
                    sp.wait_ge(out_stored, 16 * NG)

                @block.tensor
                def _(pe):
                    def x_transposes(g):
                        pe.wait_ge(xq_ready, g + 1)
                        if later(g, 1):
                            pe.wait_ge(xl_ready, g)
                        for b in range(GB):
                            i = pe.transpose(psT[:, b * P:(b + 1) * P], xq[:, b, :], ident[:, :])
                        i.then_inc(xT_done, 1)

                    def hidden(g, b, slot):
                        if b == 0:
                            pe.wait_ge(xh_ready, g + 1)
                            pe.wait_ge(xl_ready, g + 1)
                        if b >= 2 or later(g, 1):
                            pe.wait_ge(sl_ready, GB * g + b - 1)
                        pe.matmul(psH[b % 2][:, :], ones_bf[:, :], cb[:, :], start=True, stop=False)
                        for k in range(TAPS):
                            h, lo = xh[:, slot, b, k:k + P], xl[:, slot, b, k:k + P]
                            pe.matmul(psH[b % 2][:, :], lo, wkh[:, k, :], start=False, stop=False)
                            pe.matmul(psH[b % 2][:, :], h, wkl[:, k, :], start=False, stop=False)
                            i = pe.matmul(psH[b % 2][:, :], h, wkh[:, k, :], start=False, stop=(k == TAPS - 1))
                        i.then_inc(h_done, 1)

                    def hidden_transposes(g, slot, b):
                        n = GB * g + b
                        pe.wait_ge(hq_ready, n + 1)
                        if b >= 2 or later(g, 1):
                            pe.wait_ge(tq_ready, n - 1)
                        for c in range(HC):
                            i = pe.transpose(psQ[b % 2][:, c * P:(c + 1) * P], hq[:, b, c * P:(c + 1) * P],
                                             ident_bf[:, :])
                        i.then_inc(tq_done, 1)

                    def second(g, slot, b):
                        pe.wait_ge(tq_ready, GB * g + b + 1)
                        if b == 0 and later(g, 2):
                            pe.wait_ge(x_ready, g - 1)
                        for c in range(HC):
                            i = pe.matmul(psO[slot][:, b * P:(b + 1) * P], hqT[:, b, c, :], w2T[:, c, :],
                                          start=(c == 0), stop=(c == HC - 1))
                        i.then_inc(o_done, 1)

                    def group(g, slot, nxt, nxt2):
                        for b in range(GB):
                            hidden(g, b, slot)
                            before(hidden_transposes, g, slot, b, TQ_LAG)
                            before(second, g, slot, b, O_LAG)
                            if b == 2 and nxt is not None:
                                x_transposes(nxt)

                    def tail():
                        for b in range(GB, GB + O_LAG):
                            if b < GB + TQ_LAG:
                                hidden_transposes(NG - 1, 1, b - TQ_LAG)
                            second(NG - 1, 1, b - O_LAG)

                    over_groups(pe, x_transposes, group, tail)

                @block.scalar
                def _(act):
                    def x_upper(g, slot):
                        act.wait_ge(xT_done, g + 1)
                        if later(g, 2):
                            act.wait_ge(h_done, GB * (g - 1))
                        else:
                            act.wait_ge(padded, 1)
                        act.activation(xh[:, slot, :, 1:P + 1], psT[:, :].rearrange("p (b t) -> p b t", b=GB),
                                       ACT.Copy).then_inc(xh_ready, 1)

                    def silu(g, b):
                        act.wait_ge(h_done, GB * g + b + 1)
                        if later(g, 1):
                            act.wait_ge(hz_ready, GB * (g - 1) + b + 1)
                        act.activation(sl[:, b, :], psH[b % 2][:, :], ACT.Silu).then_inc(sl_ready, 1)

                    def scale(g, b):
                        act.wait_ge(hstep, 3 * (GB * g + b) + 3)
                        if later(g, 1):
                            act.wait_ge(hc_ready, GB * (g - 1) + b + 1)
                        act.activation(hz[:, b, :], sl[:, b, :], ACT.Identity, bias=big[:, 0:1],
                                       scale=hsc[:, b:b + 1]).then_inc(hz_ready, 1)

                    def copy_hidden(g, slot, b):
                        act.wait_ge(tq_done, GB * g + b + 1)
                        if later(g, 1):
                            act.wait_ge(o_done, GB * (g - 1) + b + 1)
                        act.activation(hqT[:, b, :, :].rearrange("p c k -> p (c k)"), psQ[b % 2][:, 0:HW],
                                       ACT.Copy).then_inc(tq_ready, 1)

                    def scale_x(g):
                        act.wait_ge(quant, STEPS * g + 3)
                        if later(g, 1):
                            act.wait_ge(quant, STEPS * g)
                        for b in range(GB):
                            i = act.activation(za[:, b, :], xn[:, b, :], ACT.Identity, bias=big[:, 0:1],
                                               scale=asc[:, b:b + 1])
                        i.then_inc(za_ready, 1)

                    def prep(g):
                        scale_x(g)
                        x_upper(g, 0)

                    def group(g, slot, nxt, nxt2):
                        for b in range(GB):
                            before(copy_hidden, g, slot, b, O_LAG)
                            if b >= 1:
                                scale(g, b - 1)
                            elif later(g, 1):
                                scale(g - 1, GB - 1)
                            if b == 3 and nxt is not None:
                                x_upper(nxt, 1 - slot)
                            silu(g, b)
                            if b == 0 and nxt is not None:
                                scale_x(nxt)

                    def tail():
                        scale(NG - 1, GB - 1)
                        for b in range(GB - O_LAG, GB):
                            copy_hidden(NG - 1, 1, b)

                    over_groups(act, prep, group, tail)

                @block.gpsimd
                def _(pool):
                    def rounded(g, b):
                        pool.wait_ge(hc_ready, GB * g + b + 1)
                        if later(g, 1):
                            pool.wait_ge(tq_done, GB * (g - 1) + b + 1)
                        pool.tensor_tensor(hq[:, b, :], hc[:, b, :], big[:, :], ALU.subtract).then_inc(hq_ready, 1)

                    def group(g, slot, nxt, nxt2):
                        for b in range(GB):
                            if b >= 1:
                                rounded(g, b - 1)
                            elif later(g, 1):
                                rounded(g - 1, GB - 1)
                            if b == 1 and nxt2 is not None:
                                norm_pool(pool, nxt2, slot, ln, lnD)

                    def prep(g):
                        norm_pool(pool, g, 0, ln, lnD)
                        pool.memset(xh[:, :, :, :].bitcast(F32), 0.0)
                        pool.memset(xl[:, :, :, :].bitcast(F32), 0.0).then_inc(padded, 1)
                        norm_pool(pool, g + 1, 1, ln, lnD)

                    over_groups(pool, prep, group,
                                lambda: rounded(NG - 1, GB - 1))

                @block.vector
                def _(v):
                    def x_of(g, b):
                        return X[:, bass.ds(g * GB + b, 1), :].rearrange("p a d -> p (a d)")

                    def moments(g, slot):
                        norm_moments(v, g, slot, lambda b: x_of(g, b), ln, lnD)

                    def normed_max(g, slot):
                        if later(g, 1):
                            v.wait_ge(za_ready, g)
                        norm_apply(v, g, slot, lambda b: x_of(g, b), lambda b: xn[:, b, :], ln, lnD)
                        v.wait_ge(normed, g + 1)
                        v.tensor_reduce(am[:, :], xn[:, :, :], AX.X, ALU.max, apply_absolute_value=True)\
                         .then_inc(quant, 1)

                    moments(0, 0)
                    normed_max(0, 0)

                    def token_scale(g):
                        v.wait_ge(quant, STEPS * g + 1)
                        v.tensor_scalar(ais[:, :], am[:, :], 1e-5, 1.0 / QMAX, ALU.max, ALU.mult).then_inc(quant, 1)
                        v.wait_ge(quant, STEPS * g + 2)
                        v.reciprocal(asc[:, :], ais[:, :]).then_inc(quant, 1)

                    def quantise(g):
                        v.wait_ge(za_ready, g + 1)
                        v.tensor_scalar(zb[:, :, :], za[:, :, :], BIG - QMAX - 1, BIG + QMAX, ALU.max, ALU.min)\
                         .then_inc(quant, 1)
                        v.wait_ge(quant, STEPS * g + 4)
                        if later(g, 1):
                            v.wait_ge(xT_done, g)
                        for b in range(GB):
                            i = v.tensor_scalar(xq[:, b, :], zb[:, b, :], BIG, ais[:, b:b + 1],
                                                ALU.subtract, ALU.mult)
                        i.then_inc(xq_ready, 1)

                    def x_lower(g, slot):
                        v.wait_ge(xh_ready, g + 1)
                        v.tensor_tensor(xl[:, slot, :, 1:P + 1], psT[:, :].rearrange("p (b t) -> p b t", b=GB),
                                        xh[:, slot, :, 1:P + 1].bitcast(F32), ALU.subtract).then_inc(xl_ready, 1)

                    def hidden_scale(g, b, slot):
                        n = GB * g + b
                        v.wait_ge(sl_ready, n + 1)
                        v.tensor_reduce(hm[:, b:b + 1], sl[:, b, :], AX.X, ALU.max, apply_absolute_value=True)\
                         .then_inc(hstep, 1)
                        v.wait_ge(hstep, 3 * n + 1)
                        v.tensor_scalar(hs[:, b:b + 1], hm[:, b:b + 1], 1e-5, 1.0 / QMAX, ALU.max, ALU.mult)\
                         .then_inc(hstep, 1)
                        v.wait_ge(hstep, 3 * n + 2)
                        v.reciprocal(hsc[:, b:b + 1], hs[:, b:b + 1])
                        v.tensor_scalar(hf[:, slot, b:b + 1], hs[:, b:b + 1], sw2[:, :], None, ALU.mult)\
                         .then_inc(hstep, 1)

                    def hidden_clip(g, b):
                        n = GB * g + b
                        v.wait_ge(hz_ready, n + 1)
                        if later(g, 1):
                            v.wait_ge(hq_ready, GB * (g - 1) + b + 1)
                        v.tensor_scalar(hc[:, b, :], hz[:, b, :], BIG - QMAX - 1, BIG + QMAX, ALU.max, ALU.min)\
                         .then_inc(hc_ready, 1)

                    def final(g, slot):
                        v.wait_ge(o_done, GB * (g + 1))
                        for b in range(GB):
                            i = v.scalar_tensor_tensor(out=x_of(g, b), in0=psO[slot][:, b * P:(b + 1) * P],
                                                       scalar=hf[:, slot, b:b + 1], in1=x_of(g, b),
                                                       op0=ALU.mult, op1=ALU.add)
                        i.then_inc(x_ready, 1)

                    def prep(g):
                        token_scale(g)
                        quantise(g)
                        x_lower(g, 0)
                        moments(g + 1, 1)
                        normed_max(g + 1, 1)

                    def group(g, slot, nxt, nxt2):
                        for b in range(GB):
                            if b >= 1:
                                hidden_clip(g, b - 1)
                            elif later(g, 1):
                                hidden_clip(g - 1, GB - 1)
                            if b == 3 and nxt is not None:
                                x_lower(nxt, 1 - slot)
                            if b == 0 and nxt is not None:
                                token_scale(nxt)
                            hidden_scale(g, b, slot)
                            if b == 0 and nxt2 is not None:
                                moments(nxt2, slot)
                            if b == 1 and nxt is not None:
                                quantise(nxt)
                            if b == 2 and later(g, 1):
                                final(g - 1, 1 - slot)
                            if b == 3 and nxt2 is not None:
                                normed_max(nxt2, slot)

                    def tail():
                        hidden_clip(NG - 1, GB - 1)
                        final(NG - 1, 1)

                    over_groups(v, prep, group, tail)

_INS = ['x', 'ctx_1024', 'mask_BxS2_if1', 'g_xattn', 'g_ffn', 'L0_xattn_W', 'L0_xattn_diagonal',
        'L0_ffn_gate_w', 'L0_ffn_wg', 'L0_ffn_wu', 'L0_ffn_wd', 'L0_ffn_swg', 'L0_ffn_swu', 'L0_ffn_swd',
        'L1_xattn_qkv_w', 'L1_xattn_qkv_b', 'L1_xattn_sa_out_w', 'L1_xattn_sa_out_b',
        'L1_xattn_in_proj_w', 'L1_xattn_in_proj_b', 'L1_xattn_mha_out_w', 'L1_xattn_mha_out_b',
        'L1_xattn_lin1_w', 'L1_xattn_lin1_b', 'L1_xattn_lin2_w', 'L1_xattn_lin2_b',
        'L1_xattn_ln1_g', 'L1_xattn_ln1_b', 'L1_xattn_ln2_g', 'L1_xattn_ln2_b', 'L1_xattn_ln3_g', 'L1_xattn_ln3_b',
        'L1_ffn_w1', 'L1_ffn_conv_w', 'L1_ffn_conv_b', 'L1_ffn_w2']

def kernel(**inputs):
    import numpy as np
    import concourse.bacc as bacc
    from concourse.bass_utils import run_bass_kernel_spmd

    nc = bacc.Bacc("TRN2", target_bir_lowering=False, num_devices=1)
    arrays, args = {}, []
    for name in _INS:
        a = np.ascontiguousarray(inputs[name])
        arrays[f"in_{name}"] = a
        args.append(nc.dram_tensor(f"in_{name}", a.shape, mybir.dt.from_np(a.dtype), kind="ExternalInput").ap())
    n_exp, _, inter = inputs['L0_ffn_wg'].shape
    consts = {
        "sel": np.tile(np.repeat(np.eye(n_exp, dtype=np.float32), inter, axis=1), (3, 1)),
        "ramp": np.arange(n_exp, 0, -1, dtype=np.float32),
    }
    for name, a in consts.items():
        arrays[f"const_{name}"] = a
        args.append(nc.dram_tensor(f"const_{name}", a.shape, F32, kind="ExternalInput").ap())
    out = nc.dram_tensor("out_x", inputs['x'].shape, F32, kind="ExternalOutput").ap()
    flamingo_gated(nc, *args, out)
    r = run_bass_kernel_spmd(nc, [arrays], core_ids=[0])
    return r.results[0]["out_x"]
```
